# Optimizing a Trainium2 kernel written in Bass

```python
import numpy as np
import jax
import jax.numpy as jnp

def _softmax(x, axis=-1):
    return jax.nn.softmax(x, axis=axis)

def _gelu(x):
    return jax.nn.gelu(x, approximate=True)

def _silu(x):
    return jax.nn.silu(x)

def _sigmoid(x):
    return jax.nn.sigmoid(x)

def _layernorm(x, axis=-1, eps=1e-05):
    m = jnp.mean(x, axis=axis, keepdims=True)
    v = jnp.var(x, axis=axis, keepdims=True)
    return (x - m) / jnp.sqrt(v + eps)

def _scatter_add(tgt, idx, src, axis=0):
    return tgt.at[idx].add(src)

def _segment_sum(src, seg, n):
    return jax.ops.segment_sum(src, seg, n)
kernel_name = 'mk_flamingo_gated_d2_seqx_r4_6a84ba'

def setup_inputs(seed: int=0):
    np.random.seed(seed)
    _w = jnp.asarray

    def _rec_inputs():
        import jax
        import jax.numpy as jnp
        _rk = jax.random.key(seed)
        x = -0.0002928 + 1 * jax.random.normal(jax.random.fold_in(_rk, 1), (16, 128, 256), jnp.float32)
        _lenS = 128 - jax.random.randint(jax.random.fold_in(_rk, 7), (16,), 0, max(1, 128 // 4) + 1, jnp.int32)
        _lenS2 = 128 - jax.random.randint(jax.random.fold_in(_rk, 8), (16,), 0, max(1, 128 // 4) + 1, jnp.int32)
        _ctx_1024P = jax.random.normal(jax.random.fold_in(_rk, 11), (16, 16, 256), jnp.float32)
        _ctx_1024c = jax.random.dirichlet(jax.random.fold_in(_rk, 511), 0.3 * jnp.ones((16,), jnp.float32), (16, 128))
        _ctx_1024t = jnp.einsum('bsk,bkd->bsd', _ctx_1024c, _ctx_1024P)
        _ctx_1024t = _ctx_1024t * jax.lax.rsqrt(jnp.mean(jnp.square(_ctx_1024t)) + 1e-12) * 0.953939
        ctx_1024 = -1.39393e-06 + 0.999914 * (_ctx_1024t + 0.3 * jax.random.normal(jax.random.fold_in(_rk, 611), (16, 128, 256), jnp.float32))
        _validS = jnp.arange(128)[None, :] < _lenS[:, None]
        _validS2 = jnp.arange(128)[None, :] < _lenS2[:, None]
        _causal = jnp.tril(jnp.ones((128, 128), dtype=bool))
        mask_BxSxS2_ff1 = jnp.where(jnp.ones((16, 128, 128), dtype=bool), 1.0, 0.0).astype(jnp.float32)
        _g = jax.random.normal(jax.random.fold_in(_rk, 9001), (2, 2), jnp.float32)
        _g = jnp.sign(_g) * jnp.maximum(jnp.abs(_g), 1.0) + (_g == 0) * 1.0
        g_xattn = _g[0]
        g_ffn = _g[1]
        return (x, ctx_1024, mask_BxSxS2_ff1, g_xattn, g_ffn)
    x, ctx_1024, mask_BxSxS2_ff1, g_xattn, g_ffn = _rec_inputs()

    def _L0_xattn_setup():
        import jax, jax.numpy as jnp
        import numpy as np
        B, S, D, NH = (2, 512, 256, 8)
        DH = D // NH
        EPS = 1e-06
        LN_EPS = 1e-05

        def _mlstm_cell(q, k, v, igate_w, igate_b, fgate_w, fgate_b, ln_scale):
            Slen = q.shape[0]
            ifg = jnp.concatenate([q, k, v], axis=-1)
            ig = (ifg @ igate_w.T + igate_b).T
            fg = (ifg @ fgate_w.T + fgate_b).T
            qh = q.reshape(Slen, NH, DH).transpose(1, 0, 2)
            kh = k.reshape(Slen, NH, DH).transpose(1, 0, 2)
            vh = v.reshape(Slen, NH, DH).transpose(1, 0, 2)
            log_f = jax.nn.log_sigmoid(fg)
            cs = jnp.cumsum(log_f, axis=1)
            fg_mat = cs[:, :, None] - cs[:, None, :]
            mask = jnp.tril(jnp.ones((Slen, Slen), dtype=bool))
            log_fg_mat = jnp.where(mask, fg_mat, -jnp.inf)
            log_D = log_fg_mat + ig[:, None, :]
            max_log_D = jnp.max(log_D, axis=-1, keepdims=True)
            D_mat = jnp.exp(log_D - max_log_D)
            qk = jnp.einsum('hsd,htd->hst', qh, kh) / np.sqrt(DH)
            C = qk * D_mat
            normalizer = jnp.maximum(jnp.abs(C.sum(axis=-1, keepdims=True)), jnp.exp(-max_log_D))
            h = jnp.einsum('hst,htd->hsd', C / (normalizer + EPS), vh)
            h = h.transpose(1, 0, 2).reshape(Slen, D)
            mu = h.mean(axis=-1, keepdims=True)
            var = h.var(axis=-1, keepdims=True)
            return (h - mu) / jnp.sqrt(var + LN_EPS) * ln_scale
        key = jax.random.key(seed)
        ks = jax.random.split(key, 8)
        rnd = lambda k, sh, s=1.0: jax.random.normal(k, sh, dtype=jnp.float32) * s
        return {'q': rnd(ks[0], (B, S, D)), 'k': rnd(ks[1], (B, S, D)), 'v': rnd(ks[2], (B, S, D)), 'igate_w': rnd(ks[3], (NH, 3 * D), 0.02), 'igate_b': jnp.linspace(3.0, 6.0, NH, dtype=jnp.float32), 'fgate_w': rnd(ks[4], (NH, 3 * D), 0.02), 'fgate_b': rnd(ks[5], (NH,), 0.3162278), 'ln_scale': jnp.ones((D,), dtype=jnp.float32)}
    _L0_xattn_all = _L0_xattn_setup()
    _L0_xattn_in = {k: v for k, v in _L0_xattn_all.items() if k in ('igate_w', 'igate_b', 'fgate_w', 'fgate_b', 'ln_scale')}
    del _L0_xattn_all

    def _L0_ffn_setup():
        import jax, jax.numpy as jnp
        import numpy as np
        B, S, DIM = (2, 512, 256)
        HID = 512
        E, NSH, TOPK = (8, 2, 2)

        def _ffn(x, w1, w2, w3):
            return jax.nn.silu(x @ w1.T) * (x @ w3.T) @ w2.T
        key = jax.random.key(seed)
        ks = jax.random.split(key, 8)
        sc = 0.02
        return {'x': jax.random.normal(ks[0], (B, S, DIM), jnp.float32), 'router_w': jax.random.normal(ks[1], (E, DIM), jnp.float32) * sc, 'expert_bias': jnp.zeros((E,), jnp.float32), 'w1': jax.random.normal(ks[2], (E, HID, DIM), jnp.float32) * sc, 'w3': jax.random.normal(ks[3], (E, HID, DIM), jnp.float32) * sc, 'w2': jax.random.normal(ks[4], (E, DIM, HID), jnp.float32) * sc, 'sw1': jax.random.normal(ks[5], (NSH, HID, DIM), jnp.float32) * sc, 'sw3': jax.random.normal(ks[6], (NSH, HID, DIM), jnp.float32) * sc, 'sw2': jax.random.normal(ks[7], (NSH, DIM, HID), jnp.float32) * sc}
    _L0_ffn_all = _L0_ffn_setup()
    _L0_ffn_in = {k: v for k, v in _L0_ffn_all.items() if k in ('router_w', 'expert_bias', 'w1', 'w3', 'w2', 'sw1', 'sw3', 'sw2')}
    del _L0_ffn_all

    def _L1_xattn_setup():
        import jax, jax.numpy as jnp
        import numpy as np
        HIDDEN = 256
        NUM_HEADS = 16
        HEAD_DIM = HIDDEN // NUM_HEADS
        B, LQ, LK = (2, 512, 512)

        def _split_heads(x):
            b, l, _ = x.shape
            return x.reshape(b, l, NUM_HEADS, HEAD_DIM).transpose(0, 2, 1, 3)
        key = jax.random.key(seed)
        ks = jax.random.split(key, 9)
        s = 1.0 / np.sqrt(HIDDEN)
        return {'hidden_states_query': jax.random.normal(ks[0], (B, LQ, HIDDEN), jnp.float32), 'hidden_states_key': jax.random.normal(ks[1], (B, LK, HIDDEN), jnp.float32), 'attention_mask': jnp.ones((B, LQ, LK), jnp.float32), 'Wq': jax.random.normal(ks[2], (HIDDEN, HIDDEN), jnp.float32) * s, 'bq': jax.random.normal(ks[3], (HIDDEN,), jnp.float32) * s, 'Wk': jax.random.normal(ks[4], (HIDDEN, HIDDEN), jnp.float32) * s, 'bk': jax.random.normal(ks[5], (HIDDEN,), jnp.float32) * s, 'Wv': jax.random.normal(ks[6], (HIDDEN, HIDDEN), jnp.float32) * s, 'bv': jax.random.normal(ks[7], (HIDDEN,), jnp.float32) * s}
    _L1_xattn_all = _L1_xattn_setup()
    _L1_xattn_in = {k: v for k, v in _L1_xattn_all.items() if k in ('Wq', 'bq', 'Wk', 'bk', 'Wv', 'bv')}
    del _L1_xattn_all

    def _L1_ffn_setup():
        import jax, jax.numpy as jnp
        import numpy as np
        E = 16
        G = 4
        EPG = E // G
        K = 4
        TOPK_GROUP = 2
        PER_GROUP_K = K // TOPK_GROUP

        def _route(xf, router_w, correction_bias):
            S = xf.shape[0]
            logits = xf @ router_w.T
            scores = jax.nn.sigmoid(logits)
            sb = scores + correction_bias
            grp_top = jax.lax.top_k(sb.reshape(S, G, EPG), PER_GROUP_K)[0]
            group_scores = grp_top.sum(axis=-1)
            _, group_idx = jax.lax.top_k(group_scores, TOPK_GROUP)
            group_mask = jnp.zeros((S, G), sb.dtype).at[jnp.arange(S)[:, None], group_idx].set(1.0)
            score_mask = jnp.broadcast_to(group_mask[:, :, None], (S, G, EPG)).reshape(S, E)
            masked = jnp.where(score_mask > 0, sb, -jnp.inf)
            _, topk_idx = jax.lax.top_k(masked, K)
            w = jnp.take_along_axis(scores, topk_idx, axis=1)
            w = w / (w.sum(axis=-1, keepdims=True) + 1e-20)
            return (topk_idx, w, scores)
        key = jax.random.key(seed)
        ks = jax.random.split(key, 9)
        B, T, C, H, HS = (2, 256, 256, 64, 512)
        std = 0.02
        return {'x': jax.random.normal(ks[0], (B, T, C), jnp.float32), 'router_w': jax.random.normal(ks[1], (E, C), jnp.float32) * std, 'correction_bias': jnp.zeros((E,), jnp.float32), 'gate_w': jax.random.normal(ks[2], (E, C, H), jnp.float32) * std, 'up_w': jax.random.normal(ks[3], (E, C, H), jnp.float32) * std, 'down_w': jax.random.normal(ks[4], (E, H, C), jnp.float32) * std, 'shared_gate_w': jax.random.normal(ks[5], (HS, C), jnp.float32) * std, 'shared_up_w': jax.random.normal(ks[6], (HS, C), jnp.float32) * std, 'shared_down_w': jax.random.normal(ks[7], (C, HS), jnp.float32) * std}
    _L1_ffn_all = _L1_ffn_setup()
    _L1_ffn_in = {k: v for k, v in _L1_ffn_all.items() if k in ('router_w', 'correction_bias', 'gate_w', 'up_w', 'down_w', 'shared_gate_w', 'shared_up_w', 'shared_down_w')}
    del _L1_ffn_all
    return {'x': x, 'ctx_1024': ctx_1024, 'mask_BxSxS2_ff1': mask_BxSxS2_ff1, 'g_xattn': g_xattn, 'g_ffn': g_ffn, 'L0_xattn_igate_w': _L0_xattn_in['igate_w'], 'L0_xattn_igate_b': _L0_xattn_in['igate_b'], 'L0_xattn_fgate_w': _L0_xattn_in['fgate_w'], 'L0_xattn_fgate_b': _L0_xattn_in['fgate_b'], 'L0_xattn_ln_scale': _L0_xattn_in['ln_scale'], 'L0_ffn_router_w': _L0_ffn_in['router_w'], 'L0_ffn_expert_bias': _L0_ffn_in['expert_bias'], 'L0_ffn_w1': _L0_ffn_in['w1'], 'L0_ffn_w3': _L0_ffn_in['w3'], 'L0_ffn_w2': _L0_ffn_in['w2'], 'L0_ffn_sw1': _L0_ffn_in['sw1'], 'L0_ffn_sw3': _L0_ffn_in['sw3'], 'L0_ffn_sw2': _L0_ffn_in['sw2'], 'L1_xattn_Wq': _L1_xattn_in['Wq'], 'L1_xattn_bq': _L1_xattn_in['bq'], 'L1_xattn_Wk': _L1_xattn_in['Wk'], 'L1_xattn_bk': _L1_xattn_in['bk'], 'L1_xattn_Wv': _L1_xattn_in['Wv'], 'L1_xattn_bv': _L1_xattn_in['bv'], 'L1_ffn_router_w': _L1_ffn_in['router_w'], 'L1_ffn_correction_bias': _L1_ffn_in['correction_bias'], 'L1_ffn_gate_w': _L1_ffn_in['gate_w'], 'L1_ffn_up_w': _L1_ffn_in['up_w'], 'L1_ffn_down_w': _L1_ffn_in['down_w'], 'L1_ffn_shared_gate_w': _L1_ffn_in['shared_gate_w'], 'L1_ffn_shared_up_w': _L1_ffn_in['shared_up_w'], 'L1_ffn_shared_down_w': _L1_ffn_in['shared_down_w']}

def reference(x, ctx_1024, mask_BxSxS2_ff1, g_xattn, g_ffn, L0_xattn_igate_w, L0_xattn_igate_b, L0_xattn_fgate_w, L0_xattn_fgate_b, L0_xattn_ln_scale, L0_ffn_router_w, L0_ffn_expert_bias, L0_ffn_w1, L0_ffn_w3, L0_ffn_w2, L0_ffn_sw1, L0_ffn_sw3, L0_ffn_sw2, L1_xattn_Wq, L1_xattn_bq, L1_xattn_Wk, L1_xattn_bk, L1_xattn_Wv, L1_xattn_bv, L1_ffn_router_w, L1_ffn_correction_bias, L1_ffn_gate_w, L1_ffn_up_w, L1_ffn_down_w, L1_ffn_shared_gate_w, L1_ffn_shared_up_w, L1_ffn_shared_down_w):
    import jax
    import jax.numpy as jnp

    def _L0_xattn_ref(q, k, v, igate_w, igate_b, fgate_w, fgate_b, ln_scale):
        import jax, jax.numpy as jnp
        import numpy as np
        B, S, D, NH = (2, 512, 256, 8)
        DH = D // NH
        EPS = 1e-06
        LN_EPS = 1e-05

        def _mlstm_cell(q, k, v, igate_w, igate_b, fgate_w, fgate_b, ln_scale):
            Slen = q.shape[0]
            ifg = jnp.concatenate([q, k, v], axis=-1)
            ig = (ifg @ igate_w.T + igate_b).T
            fg = (ifg @ fgate_w.T + fgate_b).T
            qh = q.reshape(Slen, NH, DH).transpose(1, 0, 2)
            kh = k.reshape(Slen, NH, DH).transpose(1, 0, 2)
            vh = v.reshape(Slen, NH, DH).transpose(1, 0, 2)
            log_f = jax.nn.log_sigmoid(fg)
            cs = jnp.cumsum(log_f, axis=1)
            fg_mat = cs[:, :, None] - cs[:, None, :]
            mask = jnp.tril(jnp.ones((Slen, Slen), dtype=bool))
            log_fg_mat = jnp.where(mask, fg_mat, -jnp.inf)
            log_D = log_fg_mat + ig[:, None, :]
            max_log_D = jnp.max(log_D, axis=-1, keepdims=True)
            D_mat = jnp.exp(log_D - max_log_D)
            qk = jnp.einsum('hsd,htd->hst', qh, kh) / np.sqrt(DH)
            C = qk * D_mat
            normalizer = jnp.maximum(jnp.abs(C.sum(axis=-1, keepdims=True)), jnp.exp(-max_log_D))
            h = jnp.einsum('hst,htd->hsd', C / (normalizer + EPS), vh)
            h = h.transpose(1, 0, 2).reshape(Slen, D)
            mu = h.mean(axis=-1, keepdims=True)
            var = h.var(axis=-1, keepdims=True)
            return (h - mu) / jnp.sqrt(var + LN_EPS) * ln_scale
        return jax.vmap(lambda qq, kk, vv: _mlstm_cell(qq, kk, vv, igate_w, igate_b, fgate_w, fgate_b, ln_scale))(q, k, v)

    def _L0_ffn_ref(x, router_w, expert_bias, w1, w3, w2, sw1, sw3, sw2):
        import jax, jax.numpy as jnp
        import numpy as np
        B, S, DIM = (2, 512, 256)
        HID = 512
        E, NSH, TOPK = (8, 2, 2)

        def _ffn(x, w1, w2, w3):
            return jax.nn.silu(x @ w1.T) * (x @ w3.T) @ w2.T
        bs, sl, d = x.shape
        xf = x.reshape(-1, d)
        shared = jnp.zeros_like(xf)
        for i in range(sw1.shape[0]):
            shared = shared + _ffn(xf, sw1[i], sw2[i], sw3[i])
        logits = xf @ router_w.T + expert_bias
        rw, sel = jax.lax.top_k(logits, TOPK)
        rw = jax.nn.softmax(rw.astype(jnp.float32), axis=-1).astype(x.dtype)
        onehot = jax.nn.one_hot(sel, E, dtype=x.dtype)
        combine = jnp.einsum('tk,tke->te', rw, onehot)

        def body(acc, ew):
            e1, e3, e2, cw = ew
            acc = acc + cw[:, None] * _ffn(xf, e1, e2, e3)
            return (acc, None)
        out, _ = jax.lax.scan(body, jnp.zeros_like(xf), (w1, w3, w2, combine.T))
        out = out + shared
        return out.reshape(bs, sl, -1)

    def _L1_xattn_ref(hidden_states_query, hidden_states_key, attention_mask, Wq, bq, Wk, bk, Wv, bv):
        import jax, jax.numpy as jnp
        import numpy as np
        HIDDEN = 256
        NUM_HEADS = 16
        HEAD_DIM = HIDDEN // NUM_HEADS
        B, LQ, LK = (2, 512, 512)

        def _split_heads(x):
            b, l, _ = x.shape
            return x.reshape(b, l, NUM_HEADS, HEAD_DIM).transpose(0, 2, 1, 3)
        q = _split_heads(hidden_states_query @ Wq.T + bq)
        k = _split_heads(hidden_states_key @ Wk.T + bk)
        v = _split_heads(hidden_states_key @ Wv.T + bv)
        scale = 1.0 / np.sqrt(HEAD_DIM)
        scores = jnp.einsum('bhqd,bhkd->bhqk', q * scale, k)
        scores = scores + ((1.0 - attention_mask) * -10000.0)[:, None, :, :]
        probs = jax.nn.softmax(scores, axis=-1)
        ctx = jnp.einsum('bhqk,bhkd->bhqd', probs, v)
        b, h, lq, d = ctx.shape
        return ctx.transpose(0, 2, 1, 3).reshape(b, lq, h * d)

    def _L1_ffn_ref(x, router_w, correction_bias, gate_w, up_w, down_w, shared_gate_w, shared_up_w, shared_down_w):
        import jax, jax.numpy as jnp
        import numpy as np
        E = 16
        G = 4
        EPG = E // G
        K = 4
        TOPK_GROUP = 2
        PER_GROUP_K = K // TOPK_GROUP

        def _route(xf, router_w, correction_bias):
            S = xf.shape[0]
            logits = xf @ router_w.T
            scores = jax.nn.sigmoid(logits)
            sb = scores + correction_bias
            grp_top = jax.lax.top_k(sb.reshape(S, G, EPG), PER_GROUP_K)[0]
            group_scores = grp_top.sum(axis=-1)
            _, group_idx = jax.lax.top_k(group_scores, TOPK_GROUP)
            group_mask = jnp.zeros((S, G), sb.dtype).at[jnp.arange(S)[:, None], group_idx].set(1.0)
            score_mask = jnp.broadcast_to(group_mask[:, :, None], (S, G, EPG)).reshape(S, E)
            masked = jnp.where(score_mask > 0, sb, -jnp.inf)
            _, topk_idx = jax.lax.top_k(masked, K)
            w = jnp.take_along_axis(scores, topk_idx, axis=1)
            w = w / (w.sum(axis=-1, keepdims=True) + 1e-20)
            return (topk_idx, w, scores)
        B, T, C = x.shape
        S = B * T
        xf = x.reshape(S, C)
        sg = xf @ shared_gate_w.T
        su = xf @ shared_up_w.T
        shared_out = jax.nn.silu(sg) * su @ shared_down_w.T
        topk_idx, w, _scores = _route(xf, router_w, correction_bias)
        combine = jnp.zeros((S, E), xf.dtype).at[jnp.arange(S)[:, None], topk_idx].add(w)
        g = jnp.einsum('sc,ech->esh', xf, gate_w)
        u = jnp.einsum('sc,ech->esh', xf, up_w)
        h = jax.nn.silu(g) * u
        hw = h * combine.T[:, :, None]
        routed = jnp.einsum('esh,ehc->sc', hw, down_w)
        return (shared_out + routed).reshape(B, T, C)
    x = x + jnp.tanh(g_xattn[0]) * _L0_xattn_ref(_layernorm(x, axis=-1), ctx_1024, ctx_1024, L0_xattn_igate_w, L0_xattn_igate_b, L0_xattn_fgate_w, L0_xattn_fgate_b, L0_xattn_ln_scale)
    x = x + jnp.tanh(g_ffn[0]) * _L0_ffn_ref(_layernorm(x, axis=-1), L0_ffn_router_w, L0_ffn_expert_bias, L0_ffn_w1, L0_ffn_w3, L0_ffn_w2, L0_ffn_sw1, L0_ffn_sw3, L0_ffn_sw2)
    x = x + jnp.tanh(g_xattn[1]) * _L1_xattn_ref(_layernorm(x, axis=-1), ctx_1024, mask_BxSxS2_ff1, L1_xattn_Wq, L1_xattn_bq, L1_xattn_Wk, L1_xattn_bk, L1_xattn_Wv, L1_xattn_bv)
    x = x + jnp.tanh(g_ffn[1]) * _L1_ffn_ref(_layernorm(x, axis=-1), L1_ffn_router_w, L1_ffn_correction_bias, L1_ffn_gate_w, L1_ffn_up_w, L1_ffn_down_w, L1_ffn_shared_gate_w, L1_ffn_shared_up_w, L1_ffn_shared_down_w)
    return x

_drawn_inputs = setup_inputs


def setup_inputs(seed=0):
    import zlib

    import numpy as np

    out = dict(_drawn_inputs(seed))
    spreads = {'g_ffn': (-1.0, 0.6),
     'L0_xattn_ln_scale': (1.0, 0.2),
     'L0_ffn_expert_bias': (0.0, 0.8),
     'L1_ffn_correction_bias': (0.0, 0.8)}
    factors = {'L0_ffn_router_w': 8.0,
     'L0_ffn_w1': 7.472,
     'L0_ffn_w3': 7.387,
     'L0_ffn_w2': 7.393,
     'L0_ffn_sw1': 3.781,
     'L0_ffn_sw3': 3.739,
     'L0_ffn_sw2': 3.742,
     'L1_xattn_Wq': 8.0,
     'L1_xattn_bq': 135.616,
     'L1_xattn_Wk': 8.0,
     'L1_xattn_bk': 200.0,
     'L1_ffn_router_w': 8.0,
     'L1_ffn_gate_w': 8.0,
     'L1_ffn_up_w': 8.0,
     'L1_ffn_down_w': 8.0,
     'L1_ffn_shared_gate_w': 4.855,
     'L1_ffn_shared_up_w': 4.787,
     'L1_ffn_shared_down_w': 4.809}
    for name, (base, spread) in spreads.items():
        noise = np.random.default_rng([zlib.crc32(name.encode()), seed]).standard_normal(out[name].shape)
        drawn = base * np.exp(spread * noise) if base else spread * noise
        out[name] = jnp.asarray(drawn.astype(out[name].dtype))
    for name, factor in factors.items():
        out[name] = (out[name] * factor).astype(out[name].dtype)
    return out
```

```python
from contextlib import ExitStack
import math
import numpy as np
import concourse.bass as bass
from concourse import mybir

F32 = mybir.dt.float32
F32R = mybir.dt.float32r
ALU = mybir.AluOpType
ACT = mybir.ActivationFunctionType
AX = mybir.AxisListType
ds = bass.ds

B, S, D = 16, 128, 256
KT = D // 128
T = B * S
CH = 4
NCH = B // CH
NH0, DH0 = 8, 32
NH1, DH1 = 16, 16
HID = 512
HT = HID // 128
E0, NSH0 = 8, 2
NB0 = E0 + NSH0
E1, H1 = 16, 64
EPB = HID // H1
NB1 = 1 + E1 // EPB
G1 = 4
EPG = E1 // G1
LN_EPS = 1e-5
CELL_EPS = 1e-6
ROOT0 = math.sqrt(DH0)
BIG = 1e30

C_ID, C_PEN, C_BD0, C_BD1, C_REV, C_EPS, C_LNR, C_ONE, C_END = 0, 128, 256, 260, 268, 284, 285, 286, 287


def norm_transpose(nc, tag, X, XNT, cst):
    with ExitStack() as ctx:
        sb = lambda n, s, d=F32: ctx.enter_context(nc.sbuf_tensor(tag + n, s, d))
        sem = lambda n: ctx.enter_context(nc.semaphore(tag + n))
        stats = sb("stats", [128, B, 6])
        mean_var = sb("mean_var", [128, B, 2])
        std = sb("std", [128, B])
        rstd = sb("rstd", [128, B])
        xn = [sb(f"xn{p}", [128, CH, D]) for p in range(2)]
        turned = [[ctx.enter_context(nc.psum_tensor(f"{tag}tp{p}{k}", [128, 512], F32)) for k in range(KT)]
                  for p in range(2)]
        var_ready, std_ready = sem("var_ready"), sem("std_ready")
        xn_ready = [sem(f"xn_ready{p}") for p in range(2)]
        turned_ready = [sem(f"turned_ready{p}") for p in range(2)]
        turned_free = [sem(f"turned_free{p}") for p in range(2)]
        block = ctx.enter_context(nc.Block())

        @block.vector
        def _(dve):
            with dve.Fori(0, B) as s:
                dve.bn_stats(stats[:, ds(s, 1), :], X[:, ds(s, 1), :])
            dve.drain()
            for s in range(B):
                dve.bn_aggr(mean_var[:, s, :], stats[:, s, :])
            dve.drain().then_inc(var_ready, 1)
            dve.wait_ge(std_ready, 1)
            dve.reciprocal(rstd[:], std[:])
            dve.drain()
            with dve.Fori(0, NCH // 2) as i:
                for p in range(2):
                    dve.wait_ge(turned_ready[p], i + 1)
                    for j in range(CH):
                        s = i * 2 * CH + p * CH + j
                        last = dve.tensor_scalar(xn[p][:, j, :], X[:, ds(s, 1), :], mean_var[:, ds(s, 1), 0:1],
                                                 rstd[:, ds(s, 1)], ALU.subtract, ALU.mult)
                    last.then_inc(xn_ready[p], 1)

        @block.tensor
        def _(pe):
            for p in range(2):
                pe.sem_inc(turned_ready[p], 1)
            with pe.Fori(0, NCH // 2) as i:
                for p in range(2):
                    pe.wait_ge(xn_ready[p], i + 1)
                    pe.wait_ge(turned_free[p], i + 1)
                    for k in range(KT):
                        for j in range(CH):
                            last = pe.transpose(turned[p][k][:, j * 128:(j + 1) * 128],
                                                xn[p][:, j, k * 128:(k + 1) * 128], cst[:, C_ID:C_ID + 128])
                    last.then_inc(turned_ready[p], 1)

        @block.scalar
        def _(act):
            for p in range(2):
                act.sem_inc(turned_free[p], 1)
            act.wait_ge(var_ready, 1)
            act.activation(std[:], mean_var[:, :, 1], ACT.Sqrt, bias=cst[:, C_EPS:C_EPS + 1]).then_inc(std_ready, 1)
            with act.Fori(0, NCH // 2) as i:
                for p in range(2):
                    act.wait_ge(turned_ready[p], i + 1 + 1)
                    for k in range(KT):
                        last = act.copy(XNT[:, k, ds(i * 1024 + p * 512, 512)], turned[p][k][:])
                    last.then_inc(turned_free[p], 1)


def gates(nc, XNT, ctxT, cst, wg, bg, AT, ET, m_dram, run_loads):
    with ExitStack() as ctx:
        sb = lambda n, s, d=F32: ctx.enter_context(nc.sbuf_tensor("g_" + n, s, d))
        sem = lambda n: ctx.enter_context(nc.semaphore("g_" + n))
        gate_tok = sb("gate_tok", [128, 2, B, NH0])
        gate_row = sb("gate_row", [128, 2, 128])
        absf, ef, lf, logf, ones = (sb(n, [128, 128]) for n in ("absf", "ef", "lf", "logf", "ones"))
        cs, a_row, m_row, ml, e_row = (sb(n, [128, 128]) for n in ("cs", "a_row", "m_row", "ml", "e_row"))
        gate_ps = ctx.enter_context(nc.psum_tensor("g_gate", [128, 512], F32))
        row_ps = ctx.enter_context(nc.psum_tensor("g_row", [128, 512], F32))
        tok_ps = ctx.enter_context(nc.psum_tensor("g_tok", [128, 512], F32))
        loaded, gate_ready, tok_ready, row_ready = sem("loaded"), sem("gate_ready"), sem("tok_ready"), sem("row_ready")
        abs_ready, ln_ready, max_ready, exp_ready = sem("abs_ready"), sem("ln_ready"), sem("max_ready"), sem("exp_ready")
        back_ready, m_stored, act_chain = sem("back_ready"), sem("m_stored"), sem("act_chain")
        block = ctx.enter_context(nc.Block())

        @block.sync
        def _(sp):
            n = run_loads(sp, loaded)
            sp.wait_ge(loaded, 16 * n)
            sp.wait_ge(max_ready, 1)
            sp.dma_start(m_dram, m_row[:]).then_inc(m_stored, 16)
            sp.wait_ge(m_stored, 16)

        @block.tensor
        def _(pe):
            pe.wait_ge(loaded, 16 * 4)
            for s in range(B):
                for k in range(3 * KT):
                    src = XNT if k < KT else ctxT
                    last = pe.matmul(gate_ps[:, s * 16:(s + 1) * 16], src[:, k % KT, s * 128:(s + 1) * 128],
                                     wg[:, k, :], start=(k == 0), stop=(k == 3 * KT - 1))
            last.then_inc(gate_ready, 1)
            pe.wait_ge(tok_ready, 1)
            for g in range(2):
                last = pe.transpose(row_ps[:, g * 128:(g + 1) * 128],
                                    gate_tok[:, g, :, :].rearrange("p s h -> p (s h)"), cst[:, C_ID:C_ID + 128])
            last.then_inc(row_ready, 1)
            pe.wait_ge(exp_ready, 1)
            pe.transpose(tok_ps[:, 0:128], a_row[:], cst[:, C_ID:C_ID + 128])
            pe.transpose(tok_ps[:, 128:256], e_row[:], cst[:, C_ID:C_ID + 128]).then_inc(back_ready, 1)

        @block.vector
        def _(dve):
            dve.memset(ones[:], 1.0)
            dve.wait_ge(loaded, 16 * 4)
            dve.wait_ge(gate_ready, 1)
            dve.tensor_tensor(gate_tok[:].rearrange("p g s h -> p s g h"),
                              gate_ps[:, 0:256].rearrange("p (s g h) -> p s g h", s=B, g=2),
                              bg[:].rearrange("p (o g h) -> p o g h", o=1, g=2).broadcast_to([128, B, 2, NH0]),
                              ALU.add).then_inc(tok_ready, 1)
            dve.wait_ge(row_ready, 1)
            dve.tensor_copy(gate_row[:].rearrange("p g t -> p (g t)"), row_ps[:, 0:256])
            dve.drain()
            ig, fg = gate_row[:, 0, :], gate_row[:, 1, :]
            dve.scalar_tensor_tensor(absf[:], fg, -1.0, fg, ALU.mult, ALU.max)
            dve.drain().then_inc(abs_ready, 1)
            dve.wait_ge(ln_ready, 1)
            dve.scalar_tensor_tensor(logf[:], fg, 0.0, lf[:], ALU.min, ALU.subtract)
            dve.drain()
            dve.tensor_tensor_scan(cs[:], ones[:], logf[:], 0.0, ALU.mult, ALU.add)
            dve.drain()
            dve.tensor_tensor(a_row[:], ig, cs[:], ALU.subtract)
            dve.drain()
            dve.tensor_tensor_scan(m_row[:], a_row[:], a_row[:], -3e38, ALU.max, ALU.max)
            dve.drain()
            dve.tensor_tensor(ml[:], cs[:], m_row[:], ALU.add)
            dve.drain().then_inc(max_ready, 1)
            dve.wait_ge(back_ready, 1)
            dve.tensor_copy(AT, tok_ps[:, 0:128])
            dve.tensor_copy(ET, tok_ps[:, 128:256])

        @block.scalar
        def _(act):
            act.wait_ge(abs_ready, 1)
            act.activation(ef[:], absf[:], ACT.Exp, scale=-1.0).then_inc(act_chain, 1)
            act.wait_ge(act_chain, 1)
            act.activation(lf[:], ef[:], ACT.Ln, bias=1.0).then_inc(ln_ready, 1)
            act.wait_ge(max_ready, 1)
            act.activation(e_row[:], ml[:], ACT.Exp, bias=cst[:, C_LNR:C_LNR + 1], scale=-1.0).then_inc(exp_ready, 1)


def cell(nc, X, XNT, ctxT_dram, ctx_dram, m_dram, cst, AT, ET, ln_tanh):
    with ExitStack() as ctx:
        sb = lambda n, s, d=F32: ctx.enter_context(nc.sbuf_tensor("c_" + n, s, d))
        sem = lambda n: ctx.enter_context(nc.semaphore("c_" + n))
        two = lambda f, n, *a: [f(f"{n}{p}", *a) for p in range(2)]
        keyT = two(sb, "keyT", [128, KT, 128])
        val = two(sb, "val", [128, NH0, DH0])
        val1 = two(sb, "val1", [128, NH0, DH0 + 1])
        mrow = two(sb, "mrow", [128, NH0, 128])
        qbd = two(sb, "qbd", [128, KT, 4, 128])
        expo = two(sb, "expo", [128, NH0, 128])
        dmat = two(sb, "dmat", [128, NH0, 128])
        cmat = two(sb, "cmat", [128, NH0, 128])
        rsum = two(sb, "rsum", [128, NH0])
        den = two(sb, "den", [128, NH0])
        rden = two(sb, "rden", [128, NH0])
        h = sb("h", [128, B, D])
        hstats = sb("hstats", [128, B, 6])
        hmv = sb("hmv", [128, B, 2])
        hstd = sb("hstd", [128, B])
        hrstd = sb("hrstd", [128, B])
        score = [[ctx.enter_context(nc.psum_tensor(f"c_score{p}{k}", [128, 512], F32)) for k in range(KT)]
                 for p in range(2)]
        pv = [ctx.enter_context(nc.psum_tensor(f"c_pv{p}", [128, 512], F32)) for p in range(2)]
        loaded, q_ready, v_ready = two(sem, "loaded"), two(sem, "q_ready"), two(sem, "v_ready")
        score_ready, expo_ready, dmat_ready = two(sem, "score_ready"), two(sem, "expo_ready"), two(sem, "dmat_ready")
        cmat_ready, pv_ready, h_ready = two(sem, "cmat_ready"), two(sem, "pv_ready"), two(sem, "h_ready")
        hvar_ready, hstd_ready = sem("hvar_ready"), sem("hstd_ready")
        block = ctx.enter_context(nc.Block())

        @block.sync
        def _(sp):
            with sp.Fori(0, B // 2) as i:
                for p in range(2):
                    sp.wait_ge(score_ready[p], i + 1)
                    sp.dma_start(keyT[p][:], ctxT_dram[:, :, ds(i * 256 + p * 128, 128)]).then_inc(loaded[p], 16)
                    sp.wait_ge(v_ready[p], i + 1)
                    sp.dma_start(val[p][:].rearrange("p h d -> p (h d)"),
                                 ctx_dram[ds(i * 2 + p, 1)].rearrange("o p d -> (o p) d")).then_inc(loaded[p], 16)
                    sp.wait_ge(expo_ready[p], i + 1)
                    sp.dma_start(mrow[p][:].rearrange("p h t -> p (h t)"),
                                 m_dram.rearrange("(b h) t -> b (h t)", b=B)[ds(i * 2 + p, 1)]
                                 .broadcast_to([128, NH0 * 128])).then_inc(loaded[p], 16)

        @block.gpsimd
        def _(pool):
            for p in range(2):
                pool.sem_inc(v_ready[p], 1)
            for p in range(2):
                pool.memset(val1[p][:], 1.0)
            pool.drain()
            with pool.Fori(0, B // 2) as i:
                for p in range(2):
                    pool.wait_ge(score_ready[p], i + 1)
                    for k in range(KT):
                        last = pool.tensor_tensor(
                            qbd[p][:, k],
                            XNT[:, k, ds(i * 256 + p * 128, 128)].rearrange("p (o t) -> p o t", o=1)
                            .broadcast_to([128, 4, 128]),
                            cst[:, C_BD0:C_BD0 + 4].rearrange("p (h o) -> p h o", o=1).broadcast_to([128, 4, 128]),
                            ALU.mult)
                    last.then_inc(q_ready[p], 1)
                    pool.wait_ge(loaded[p], i * 48 + 48)
                    pool.wait_ge(pv_ready[p], i + 1)
                    pool.tensor_tensor(val1[p][:, :, 0:DH0], val[p][:],
                                       cst[:, C_ONE:C_ONE + 1].rearrange("p (a b) -> p a b", a=1)
                                       .broadcast_to([128, NH0, DH0]), ALU.mult).then_inc(v_ready[p], 1)

        @block.tensor
        def _(pe):
            for p in range(2):
                pe.sem_inc(score_ready[p], 1)
                pe.sem_inc(pv_ready[p], 1)
            with pe.Fori(0, B // 2) as i:
                for p in range(2):
                    pe.wait_ge(loaded[p], i * 48 + 48)
                    pe.wait_ge(q_ready[p], i + 1)
                    pe.wait_ge(cmat_ready[p], i + 1)
                    for k in range(KT):
                        last = pe.matmul(score[p][k][:], keyT[p][:, k], qbd[p][:, k], start=True, stop=True)
                    last.then_inc(score_ready[p], 1)
                for p in range(2):
                    pe.wait_ge(v_ready[p], i + 1 + 1)
                    pe.wait_ge(cmat_ready[p], i + 1 + 1)
                    pe.wait_ge(h_ready[p], i + 1)
                    for n in range(NH0):
                        last = pe.matmul(pv[p][:, n * 33:(n + 1) * 33], cmat[p][:, n], val1[p][:, n],
                                         start=True, stop=True)
                    last.then_inc(pv_ready[p], 1)

        @block.scalar
        def _(act):
            for p in range(2):
                act.sem_inc(dmat_ready[p], 1)
            with act.Fori(0, B // 2) as i:
                for p in range(2):
                    act.wait_ge(expo_ready[p], i + 1 + 1)
                    act.wait_ge(cmat_ready[p], i + 1)
                    act.activation(dmat[p][:], expo[p][:], ACT.Exp, scale=-1.0).then_inc(dmat_ready[p], 1)
            act.wait_ge(hvar_ready, 1)
            act.activation(hstd[:], hmv[:, :, 1], ACT.Sqrt, bias=cst[:, C_EPS:C_EPS + 1]).then_inc(hstd_ready, 1)

        @block.vector
        def _(dve):
            for p in range(2):
                dve.sem_inc(expo_ready[p], 1)
                dve.sem_inc(cmat_ready[p], 1)
                dve.sem_inc(h_ready[p], 1)
            with dve.Fori(0, B // 2) as i:
                for p in range(2):
                    dve.wait_ge(loaded[p], i * 48 + 48)
                    dve.wait_ge(dmat_ready[p], i + 1)
                    for n in range(NH0):
                        last = dve.scalar_tensor_tensor(
                            expo[p][:, n], mrow[p][:, n], AT[:, ds(i * 16 + p * 8 + n, 1)],
                            cst[:, C_PEN:C_PEN + 128], ALU.subtract, ALU.max)
                    last.then_inc(expo_ready[p], 1)
                for p in range(2):
                    dve.wait_ge(dmat_ready[p], i + 1 + 1)
                    dve.wait_ge(score_ready[p], i + 1 + 1)
                    dve.wait_ge(pv_ready[p], i + 1)
                    for k in range(KT):
                        last = dve.tensor_tensor(cmat[p][:, 4 * k:4 * k + 4].rearrange("p h t -> p (h t)"),
                                                 score[p][k][:],
                                                 dmat[p][:, 4 * k:4 * k + 4].rearrange("p h t -> p (h t)"), ALU.mult)
                    last.then_inc(cmat_ready[p], 1)
                for p in range(2):
                    dve.wait_ge(pv_ready[p], i + 1 + 1)
                    o = pv[p][:, 0:NH0 * 33].rearrange("p (h d) -> p h d", h=NH0)
                    dve.tensor_copy(rsum[p][:], o[:, :, DH0])
                    dve.drain()
                    dve.scalar_tensor_tensor(den[p][:], rsum[p][:], -1.0, rsum[p][:], ALU.mult, ALU.max)
                    dve.drain()
                    dve.tensor_tensor(rsum[p][:], den[p][:], ET[:, ds(i * 16 + p * 8, 8)], ALU.max)
                    dve.drain()
                    dve.tensor_scalar(den[p][:], rsum[p][:], CELL_EPS * ROOT0, None, ALU.add)
                    dve.drain()
                    dve.reciprocal(rden[p][:], den[p][:])
                    dve.drain()
                    dve.tensor_tensor(h[:, ds(i * 2 + p, 1), :].rearrange("p o (h d) -> p (o h) d", h=NH0),
                                      o[:, :, 0:DH0],
                                      rden[p][:].rearrange("p (h o) -> p h o", o=1).broadcast_to([128, NH0, DH0]),
                                      ALU.mult).then_inc(h_ready[p], 1)
            dve.drain()
            with dve.Fori(0, B) as s:
                dve.bn_stats(hstats[:, ds(s, 1), :], h[:, ds(s, 1), :])
            dve.drain()
            for s in range(B):
                dve.bn_aggr(hmv[:, s, :], hstats[:, s, :])
            dve.drain().then_inc(hvar_ready, 1)
            dve.wait_ge(hstd_ready, 1)
            dve.reciprocal(hrstd[:], hstd[:])
            dve.drain()
            with dve.Fori(0, B) as s:
                dve.tensor_scalar(h[:, ds(s, 1), :], h[:, ds(s, 1), :], hmv[:, ds(s, 1), 0:1], hrstd[:, ds(s, 1)],
                                  ALU.subtract, ALU.mult)
            dve.drain()
            dve.tensor_tensor(h[:], h[:], ln_tanh.rearrange("p (o d) -> p o d", o=1).broadcast_to([128, B, D]),
                              ALU.mult)
            dve.drain()
            dve.tensor_tensor(X[:], X[:], h[:], ALU.add)


def attention(nc, X, XNT, ctxT_dram, mask_dram, w_dram, bq_dram, bv_dram, cst, tanh_col):
    HH = NH1 // 2
    with ExitStack() as ctx:
        sb = lambda n, s, d=F32: ctx.enter_context(nc.sbuf_tensor("a_" + n, s, d))
        sem = lambda n: ctx.enter_context(nc.semaphore("a_" + n))
        pb = lambda n: ctx.enter_context(nc.psum_tensor("a_" + n, [128, 512], F32))
        two = lambda f, n, *a: [f(f"{n}{p}", *a) for p in range(2)]
        w = sb("w", [128, 3, KT, D])
        bqk = sb("bqk", [128, 2, KT])
        bv = sb("bv", [128, D])
        keyT = sb("keyT", [128, KT, 256])
        msk = two(sb, "msk", [128, 128])
        msk1 = two(sb, "msk1", [128, 128])
        pen = two(sb, "pen", [128, 128])
        qT = sb("qT", [128, KT, 256])
        kT = sb("kT", [128, KT, 256])
        kbd = two(sb, "kbd", [128, KT, HH, 128])
        v1 = two(sb, "v1", [128, NH1, DH1 + 1])
        sc = two(sb, "sc", [128, HH, 128])
        mx = two(sb, "mx", [128, HH])
        pr = two(sb, "pr", [128, HH, 128])
        prT = two(sb, "prT", [128, 4, 128])
        rs = two(sb, "rs", [128, NH1])
        rs2 = two(sb, "rs2", [128, NH1])
        o_sb = two(sb, "o_sb", [128, D])
        proj = pb("proj")
        score = [[pb(f"score{q}{k}") for k in range(2)] for q in range(2)]
        turned = two(pb, "turned")
        out_ps = pb("out_ps")
        w_loaded, k_loaded, m_loaded = sem("w_loaded"), sem("k_loaded"), sem("m_loaded")
        proj_ready, proj_free, kbd_ready = sem("proj_ready"), sem("proj_free"), sem("kbd_ready")
        pen_ready = sem("pen_ready")
        score_ready, score_free, sub_ready = sem("score_ready"), sem("score_free"), sem("sub_ready")
        mx_ready, pr_ready, turned_ready, turned_free = sem("mx_ready"), sem("pr_ready"), sem("turned_ready"), sem("turned_free")
        pv_ready, out_free, ones_ready = sem("pv_ready"), sem("out_free"), sem("ones_ready")
        block = ctx.enter_context(nc.Block())
        PJ, HALF, TG = 6, 4, 8

        @block.sync
        def _(sp):
            sp.dma_start(w[:], w_dram.rearrange("w p k n -> p w k n")).then_inc(w_loaded, 16)
            sp.dma_start(bqk[:], bq_dram).then_inc(w_loaded, 16)
            sp.dma_start(bv[:], bv_dram.rearrange("(o n) -> o n", o=1).broadcast_to([128, D])).then_inc(w_loaded, 16)
            with sp.Fori(0, B // 2) as i:
                sp.wait_ge(proj_ready, i * PJ + 1)
                sp.dma_start(keyT[:], ctxT_dram[:, :, ds(i * 256, 256)]).then_inc(k_loaded, 16)
                sp.wait_ge(pen_ready, i * 2 + 1)
                for p in range(2):
                    sp.dma_start(msk[p][:], mask_dram[ds(i * 2 + p, 1)].rearrange("o q k -> (o q) k")
                                 ).then_inc(m_loaded, 16)

        @block.tensor
        def _(pe):
            for counter in (proj_ready, score_ready, turned_ready, pv_ready):
                pe.sem_inc(counter, 1)
            pe.wait_ge(w_loaded, 48)
            with pe.Fori(0, B // 2) as i:
                pe.wait_ge(k_loaded, i * 16 + 16)
                n = 0
                for which in range(2):
                    for m in range(KT):
                        pe.wait_ge(proj_free, i * PJ + n + 1)
                        for k in range(KT):
                            src = XNT[:, k, ds(i * 256, 256)] if which == 0 else keyT[:, k]
                            last = pe.matmul(proj[:, 0:256], w[:, which, k, m * 128:(m + 1) * 128], src,
                                             start=(k == 0), stop=(k == KT - 1))
                        last.then_inc(proj_ready, 1)
                        n += 1
                for p in range(2):
                    pe.wait_ge(proj_free, i * PJ + n + 1)
                    for k in range(KT):
                        last = pe.matmul(proj[:, 0:256], keyT[:, k, p * 128:(p + 1) * 128], w[:, 2, k],
                                         start=(k == 0), stop=(k == KT - 1))
                    last.then_inc(proj_ready, 1)
                    n += 1

                def scores(u):
                    p, q = u // 2, u % 2
                    pe.wait_ge(kbd_ready, i * HALF + u + 1 + 1)
                    pe.wait_ge(score_free, i * HALF + u + 1)
                    for g in range(2):
                        last = pe.matmul(score[u % 2][g][:], qT[:, q, p * 128:(p + 1) * 128],
                                         kbd[p][:, q, 4 * g:4 * g + 4], start=True, stop=True)
                    last.then_inc(score_ready, 1)

                def values(u):
                    p, q = u // 2, u % 2
                    pe.wait_ge(pr_ready, i * HALF + u + 1 + 1)
                    if q == 0:
                        pe.wait_ge(out_free, i * 2 + p + 1)
                    for g in range(2):
                        n = u * 2 + g
                        pe.wait_ge(turned_free, i * TG + n + 1)
                        for j in range(4):
                            last = pe.transpose(turned[g][:, j * 128:(j + 1) * 128], pr[u % 2][:, 4 * g + j],
                                                cst[:, C_ID:C_ID + 128])
                        last.then_inc(turned_ready, 1)
                    for g in range(2):
                        n = u * 2 + g
                        pe.wait_ge(turned_free, i * TG + n + 3)
                        for j in range(4):
                            hd = q * HH + 4 * g + j
                            last = pe.matmul(out_ps[:, hd * 17:(hd + 1) * 17], prT[g][:, j], v1[p][:, hd],
                                             start=True, stop=True)
                        last.then_inc(pv_ready, 1)

                scores(0)
                scores(1)
                values(0)
                scores(2)
                values(1)
                scores(3)
                values(2)
                values(3)

        @block.gpsimd
        def _(pool):
            pool.sem_inc(pen_ready, 1)
            pool.sem_inc(kbd_ready, 1)
            for p in range(2):
                pool.memset(v1[p][:], 1.0)
            pool.drain().then_inc(ones_ready, 1)
            with pool.Fori(0, B // 2) as i:
                for p in range(2):
                    pool.wait_ge(m_loaded, i * 32 + 32)
                    if p == 0:
                        pool.wait_ge(score_free, i * HALF + 2)
                    pool.tensor_tensor(msk1[p][:], msk[p][:], cst[:, C_ONE:C_ONE + 1].broadcast_to([128, 128]), ALU.subtract)
                    pool.drain()
                    pool.tensor_scalar(pen[p][:], msk1[p][:], 10000.0, None, ALU.mult).then_inc(pen_ready, 1)
                pool.wait_ge(proj_free, i * PJ + 4 + 1)
                for p in range(2):
                    for q in range(KT):
                        pool.tensor_tensor(
                            kbd[p][:, q],
                            kT[:, q, p * 128:(p + 1) * 128].rearrange("p (o t) -> p o t", o=1)
                            .broadcast_to([128, HH, 128]),
                            cst[:, C_BD1:C_BD1 + HH].rearrange("p (h o) -> p h o", o=1).broadcast_to([128, HH, 128]),
                            ALU.mult).then_inc(kbd_ready, 1)

        @block.scalar
        def _(act):
            act.sem_inc(proj_free, 1)
            act.sem_inc(pr_ready, 1)
            act.wait_ge(w_loaded, 48)
            act.sem_inc(turned_free, 2)
            with act.Fori(0, B // 2) as i:
                for which in range(2):
                    for m in range(KT):
                        act.wait_ge(proj_ready, i * PJ + which * 2 + m + 1 + 1)
                        if which == 0 and m == 0:
                            act.wait_ge(score_ready, i * HALF + 1)
                        if which == 1 and m == 0:
                            act.wait_ge(kbd_ready, i * HALF + 1)
                        dst = qT if which == 0 else kT
                        act.activation(dst[:, m], proj[:, 0:256], ACT.Identity, bias=bqk[:, which, m:m + 1]
                                       ).then_inc(proj_free, 1)

                def exps(u):
                    act.wait_ge(sub_ready, i * HALF + u + 1)
                    act.wait_ge(turned_ready, i * TG + 2 * u + 1)
                    act.activation(pr[u % 2][:], sc[u % 2][:], ACT.Exp, scale=1.0 / math.sqrt(DH1)).then_inc(pr_ready, 1)

                def turn(u):
                    for g in range(2):
                        n = u * 2 + g
                        act.wait_ge(turned_ready, i * TG + n + 1 + 1)
                        act.wait_ge(pv_ready, i * TG + max(n - 1, 0) + 1)
                        act.copy(prT[g][:].rearrange("p h t -> p (h t)"), turned[g][:]).then_inc(turned_free, 1)

                for u in range(HALF):
                    exps(u)
                    turn(u)

        @block.vector
        def _(dve):
            dve.sem_inc(out_free, 1)
            dve.wait_ge(w_loaded, 48)
            dve.sem_inc(score_free, 2)
            dve.wait_ge(ones_ready, 1)
            with dve.Fori(0, B // 2) as i:
                for p in range(2):
                    dve.wait_ge(proj_ready, i * PJ + 5 + p + 1)
                    dve.wait_ge(pv_ready, i * TG + 1)
                    dve.tensor_tensor(v1[p][:, :, 0:DH1], proj[:, 0:256].rearrange("p (h d) -> p h d", h=NH1),
                                      bv[:].rearrange("p (h d) -> p h d", h=NH1), ALU.add).then_inc(proj_free, 1)

                def soft(u):
                    p = u // 2
                    dve.wait_ge(score_ready, i * HALF + u + 1 + 1)
                    dve.wait_ge(pen_ready, i * 2 + p + 1 + 1)
                    if u >= 2:
                        dve.wait_ge(pr_ready, i * HALF + u - 1 + 1)
                    else:
                        dve.wait_ge(pr_ready, i * HALF + 1)
                    for g in range(2):
                        last = dve.scalar_tensor_tensor(
                            sc[u % 2][:, 4 * g:4 * g + 4], pen[p][:].rearrange("p (o t) -> p o t", o=1)
                            .broadcast_to([128, 4, 128]), math.sqrt(DH1),
                            score[u % 2][g][:].rearrange("p (h t) -> p h t", h=4), ALU.mult, ALU.add)
                    last.then_inc(score_free, 1)
                    dve.drain()
                    dve.tensor_reduce(mx[u % 2][:], sc[u % 2][:], AX.X, ALU.max)
                    dve.drain()
                    dve.tensor_tensor(sc[u % 2][:], sc[u % 2][:],
                                      mx[u % 2][:].rearrange("p (h o) -> p h o", o=1).broadcast_to([128, HH, 128]),
                                      ALU.subtract).then_inc(sub_ready, 1)

                def finish(p):
                    dve.wait_ge(pv_ready, i * TG + 4 * p + 4 + 1)
                    o = out_ps[:, 0:NH1 * 17].rearrange("p (h d) -> p h d", h=NH1)
                    dve.reciprocal(rs[p][:], o[:, :, DH1])
                    dve.drain()
                    dve.tensor_scalar(rs2[p][:], rs[p][:], tanh_col, None, ALU.mult)
                    dve.drain()
                    dve.tensor_tensor(o_sb[p][:].rearrange("p (h d) -> p h d", h=NH1), o[:, :, 0:DH1],
                                      rs2[p][:].rearrange("p (h o) -> p h o", o=1).broadcast_to([128, NH1, DH1]),
                                      ALU.mult).then_inc(out_free, 1)
                    dve.drain()
                    dve.tensor_tensor(X[:, ds(i * 2 + p, 1), :], X[:, ds(i * 2 + p, 1), :],
                                      o_sb[p][:].rearrange("p (o d) -> p o d", o=1), ALU.add)

                soft(0)
                soft(1)
                soft(2)
                finish(0)
                soft(3)
                finish(1)


def top1(dve, src, oh, mx, rev, shape):
    bc = lambda a: a.rearrange("p g (k o) -> p g k o", o=1).broadcast_to(shape)
    dve.tensor_reduce(mx, src, AX.X, ALU.max)
    dve.drain()
    dve.tensor_tensor(oh, src, bc(mx), ALU.is_equal)
    dve.drain()
    dve.tensor_tensor(oh, oh, rev, ALU.mult)
    dve.drain()
    dve.tensor_reduce(mx, oh, AX.X, ALU.max)
    dve.drain()
    dve.tensor_tensor(oh, oh, bc(mx), ALU.is_equal)
    dve.drain()


def route0(nc, XNT, rw_dram, bias_dram, cst, CW, tanh_col):
    with ExitStack() as ctx:
        sb = lambda n, s, d=F32: ctx.enter_context(nc.sbuf_tensor("r0_" + n, s, d))
        sem = lambda n: ctx.enter_context(nc.semaphore("r0_" + n))
        rw = sb("rw", [128, KT, E0])
        eb = sb("eb", [128, E0])
        lg, oh0, oh1, l2, tmp = (sb(n, [128, B, 1, E0]) for n in ("lg", "oh0", "oh1", "l2", "tmp"))
        scratch = sb("scratch", [128, B, 1])
        m1, m2, e2, w1, w2 = (sb(n, [128, B, 1]) for n in ("m1", "m2", "e2", "w1", "w2"))
        ps = ctx.enter_context(nc.psum_tensor("r0_ps", [128, 512], F32))
        loaded, logits_ready, diff_ready, exp_ready = sem("loaded"), sem("logits_ready"), sem("diff_ready"), sem("exp_ready")
        block = ctx.enter_context(nc.Block())

        @block.sync
        def _(sp):
            sp.dma_start(rw[:], rw_dram).then_inc(loaded, 16)
            sp.dma_start(eb[:], bias_dram.rearrange("(o n) -> o n", o=1).broadcast_to([128, E0])).then_inc(loaded, 16)
            sp.wait_ge(loaded, 32)

        @block.tensor
        def _(pe):
            pe.wait_ge(loaded, 32)
            for s in range(B):
                for k in range(KT):
                    last = pe.matmul(ps[:, s * E0:(s + 1) * E0], XNT[:, k, s * 128:(s + 1) * 128], rw[:, k],
                                     start=(k == 0), stop=(k == KT - 1))
            last.then_inc(logits_ready, 1)

        @block.scalar
        def _(act):
            act.wait_ge(diff_ready, 1)
            act.activation(e2[:], w1[:], ACT.Exp).then_inc(exp_ready, 1)

        @block.vector
        def _(dve):
            dve.wait_ge(loaded, 32)
            dve.wait_ge(logits_ready, 1)
            shape = [128, B, 1, E0]
            rev = cst[:, C_REV:C_REV + E0].rearrange("p (a b e) -> p a b e", a=1, b=1).broadcast_to(shape)
            bc = lambda a: a.rearrange("p g (k o) -> p g k o", o=1).broadcast_to(shape)
            dve.tensor_tensor(lg[:], ps[:, 0:B * E0].rearrange("p (s b e) -> p s b e", s=B, b=1),
                              eb[:].rearrange("p (a b e) -> p a b e", a=1, b=1).broadcast_to(shape), ALU.add)
            dve.drain()
            dve.tensor_reduce(m1[:], lg[:], AX.X, ALU.max)
            top1(dve, lg[:], oh0[:], scratch[:], rev, shape)
            dve.scalar_tensor_tensor(l2[:].rearrange("p s b e -> p (s b e)"), oh0[:].rearrange("p s b e -> p (s b e)"),
                                     -BIG, lg[:].rearrange("p s b e -> p (s b e)"), ALU.mult, ALU.add)
            dve.drain()
            dve.tensor_reduce(m2[:], l2[:], AX.X, ALU.max)
            top1(dve, l2[:], oh1[:], scratch[:], rev, shape)
            dve.tensor_tensor(w1[:], m2[:], m1[:], ALU.subtract)
            dve.drain().then_inc(diff_ready, 1)
            dve.wait_ge(exp_ready, 1)
            dve.tensor_scalar(m1[:], e2[:], 1.0, None, ALU.add)
            dve.drain()
            dve.reciprocal(m2[:], m1[:])
            dve.drain()
            dve.tensor_scalar(w1[:], m2[:], tanh_col, None, ALU.mult)
            dve.drain()
            dve.tensor_tensor(w2[:], w1[:], e2[:], ALU.mult)
            dve.drain()
            dve.tensor_tensor(tmp[:], oh0[:], bc(w1[:]), ALU.mult)
            dve.tensor_tensor(l2[:], oh1[:], bc(w2[:]), ALU.mult)
            dve.drain()
            dve.tensor_tensor(CW[:, :, NSH0:NB0], tmp[:].rearrange("p s b e -> p s (b e)"),
                              l2[:].rearrange("p s b e -> p s (b e)"), ALU.add)
            dve.memset(CW[:, :, 0:NSH0], 1.0)
            dve.drain()
            dve.tensor_scalar(CW[:, :, 0:NSH0], CW[:, :, 0:NSH0], tanh_col, None, ALU.mult)


def route1(nc, XNT, rw_dram, bias_dram, cst, comb_dram):
    with ExitStack() as ctx:
        sb = lambda n, s, d=F32: ctx.enter_context(nc.sbuf_tensor("r1_" + n, s, d))
        sem = lambda n: ctx.enter_context(nc.semaphore("r1_" + n))
        rw = sb("rw", [128, KT, E1])
        eb = sb("eb", [128, E1])
        sg, sbias, cur, oh, sel = (sb(n, [128, B, E1]) for n in ("sg", "sbias", "cur", "oh", "sel"))
        comb = sb("comb", [128, E1, B])
        combT = sb("combT", [128, 2, 128])
        g1, g2, gs, goh, gsel, gtmp = (sb(n, [128, B, G1]) for n in ("g1", "g2", "gs", "goh", "gsel", "gtmp"))
        one = sb("one", [128, B, 1])
        one2 = sb("one2", [128, B, 1])
        ps = ctx.enter_context(nc.psum_tensor("r1_ps", [128, 512], F32))
        ps2 = ctx.enter_context(nc.psum_tensor("r1_ps2", [128, 512], F32))
        loaded, logits_ready, sig_ready, comb_ready = sem("loaded"), sem("logits_ready"), sem("sig_ready"), sem("comb_ready")
        turned_ready, combT_ready, stored = sem("turned_ready"), sem("combT_ready"), sem("stored")
        block = ctx.enter_context(nc.Block())

        @block.sync
        def _(sp):
            sp.dma_start(rw[:], rw_dram).then_inc(loaded, 16)
            sp.dma_start(eb[:], bias_dram.rearrange("(o n) -> o n", o=1).broadcast_to([128, E1])).then_inc(loaded, 16)
            sp.wait_ge(loaded, 32)
            sp.wait_ge(combT_ready, 1)
            sp.dma_start(comb_dram.rearrange("(x e) (s t) -> (e s) x t", x=2, s=B), combT[:]).then_inc(stored, 16)
            sp.wait_ge(stored, 16)

        @block.tensor
        def _(pe):
            pe.wait_ge(loaded, 32)
            for s in range(B):
                for k in range(KT):
                    last = pe.matmul(ps[:, s * E1:(s + 1) * E1], XNT[:, k, s * 128:(s + 1) * 128], rw[:, k],
                                     start=(k == 0), stop=(k == KT - 1))
            last.then_inc(logits_ready, 1)
            pe.wait_ge(comb_ready, 1)
            for x in range(2):
                last = pe.transpose(ps2[:, x * 128:(x + 1) * 128],
                                    comb[:, 8 * x:8 * x + 8, :].rearrange("p e s -> p (e s)"),
                                    cst[:, C_ID:C_ID + 128])
            last.then_inc(turned_ready, 1)

        @block.scalar
        def _(act):
            act.wait_ge(logits_ready, 1)
            act.activation(sg[:].rearrange("p s e -> p (s e)"), ps[:, 0:B * E1], ACT.Sigmoid).then_inc(sig_ready, 1)

        @block.vector
        def _(dve):
            dve.wait_ge(loaded, 32)
            dve.wait_ge(sig_ready, 1)
            in_groups = lambda a: a[:].rearrange("p s (g e) -> p s g e", g=G1)
            whole = lambda a: a[:].rearrange("p s (o e) -> p s o e", o=1)
            flat = lambda a: a[:].rearrange("p s e -> p (s e)")
            gshape, wshape, groups = [128, B, G1, EPG], [128, B, 1, E1], [128, B, 1, G1]
            rev = lambda n, sh: cst[:, C_REV:C_REV + n].rearrange("p (a b e) -> p a b e", a=1, b=1).broadcast_to(sh)
            dve.tensor_tensor(sbias[:], sg[:], eb[:].rearrange("p (o e) -> p o e", o=1).broadcast_to([128, B, E1]),
                              ALU.add)
            dve.drain()
            dve.tensor_reduce(g1[:], in_groups(sbias), AX.X, ALU.max)
            top1(dve, in_groups(sbias), in_groups(oh), gtmp[:], rev(EPG, gshape), gshape)
            dve.scalar_tensor_tensor(flat(cur), flat(oh), -BIG, flat(sbias), ALU.mult, ALU.add)
            dve.drain()
            dve.tensor_reduce(g2[:], in_groups(cur), AX.X, ALU.max)
            dve.drain()
            dve.tensor_tensor(gs[:], g1[:], g2[:], ALU.add)
            dve.drain()
            top1(dve, whole(gs), whole(gsel), one[:], rev(G1, groups), groups)
            dve.scalar_tensor_tensor(flat(gs), flat(gsel), -BIG, flat(gs), ALU.mult, ALU.add)
            dve.drain()
            top1(dve, whole(gs), whole(goh), one[:], rev(G1, groups), groups)
            dve.tensor_tensor(gsel[:], gsel[:], goh[:], ALU.add)
            dve.drain()
            dve.tensor_scalar(gs[:], gsel[:], 1.0, BIG, ALU.subtract, ALU.mult)
            dve.drain()
            dve.tensor_tensor(in_groups(cur), in_groups(sbias),
                              gs[:].rearrange("p s (g o) -> p s g o", o=1).broadcast_to(gshape), ALU.add)
            dve.drain()
            for n in range(4):
                dst = sel if n == 0 else oh
                top1(dve, whole(cur), whole(dst), one[:], rev(E1, wshape), wshape)
                if n < 3:
                    dve.scalar_tensor_tensor(flat(cur), flat(dst), -BIG, flat(cur), ALU.mult, ALU.add)
                if n > 0:
                    dve.tensor_tensor(sel[:], sel[:], oh[:], ALU.add)
                dve.drain()
            dve.tensor_tensor(sel[:], sel[:], sg[:], ALU.mult)
            dve.drain()
            dve.tensor_reduce(one[:], whole(sel), AX.X, ALU.add)
            dve.drain()
            dve.tensor_scalar(one2[:], one[:], 1e-20, None, ALU.add)
            dve.drain()
            dve.reciprocal(one[:], one2[:])
            dve.drain()
            dve.tensor_tensor(comb[:].rearrange("p e s -> p s e"), sel[:], one[:].broadcast_to([128, B, E1]),
                              ALU.mult).then_inc(comb_ready, 1)
            dve.wait_ge(turned_ready, 1)
            dve.tensor_copy(combT[:].rearrange("p x t -> p (x t)"), ps2[:, 0:256]).then_inc(combT_ready, 1)


def feed_forward(nc, tag, X, XNT, w_dram, nblocks, CW, tanh_col, comb_dram, one):
    with ExitStack() as ctx:
        sb = lambda n, s, d=F32: ctx.enter_context(nc.sbuf_tensor(tag + n, s, d))
        sem = lambda n: ctx.enter_context(nc.semaphore(tag + n))
        pb = lambda n: ctx.enter_context(nc.psum_tensor(tag + n, [128, 512], F32))
        WN = 6 * HID
        xhi = sb("xhi", [128, KT, T], F32R)
        xlo = sb("xlo", [128, KT, T], F32R)
        raw = sb("raw", [128, WN])
        whi = [sb(f"whi{p}", [128, WN], F32R) for p in range(2)]
        wlo = [sb(f"wlo{p}", [128, WN], F32R) for p in range(2)]
        act_g = [sb(f"act_g{p}", [128, 512]) for p in range(2)]
        hid = [sb(f"hid{p}", [128, 512]) for p in range(2)]
        hhi = [sb(f"hhi{p}", [128, 512], F32R) for p in range(2)]
        hlo = [sb(f"hlo{p}", [128, 512], F32R) for p in range(2)]
        cb = sb("cb", [128, HT, 512]) if comb_dram is not None else None
        gate = [pb(f"gate{p}") for p in range(2)]
        up = [pb(f"up{p}") for p in range(2)]
        y = [[pb(f"y{p}{j}") for j in range(2)] for p in range(2)]
        x_ready, w_loaded, w_split, w_used = sem("x_ready"), sem("w_loaded"), sem("w_split"), sem("w_used")
        whi_ready = sem("whi_ready")
        gu_ready, gu_free, silu_ready = sem("gu_ready"), sem("gu_free"), sem("silu_ready")
        hid_ready, hhi_ready, hlo_ready = sem("hid_ready"), sem("hhi_ready"), sem("hlo_ready")
        h_used, y_ready, y_free = sem("h_used"), sem("y_ready"), sem("y_free")
        cb_loaded, cb_used, xh_ready = sem("cb_loaded"), sem("cb_used"), sem("xh_ready")
        block = ctx.enter_context(nc.Block())
        gate_cols = lambda k, ht: slice(k * HID + ht * 128, k * HID + (ht + 1) * 128)
        up_cols = lambda k, ht: slice((KT + k) * HID + ht * 128, (KT + k) * HID + (ht + 1) * 128)
        down_cols = lambda ht: slice(2 * KT * HID + ht * D, 2 * KT * HID + (ht + 1) * D)

        def over_blocks(eng, body):
            pairs = nblocks // 2
            if pairs > 1:
                with eng.Fori(0, pairs) as i:
                    for p in range(2):
                        body(i * 2 + p, p)
                done = 2 * pairs
            else:
                done = 0
            for b in range(done, nblocks):
                body(b, b % 2)

        @block.sync
        def _(sp):
            def load(b, p):
                sp.wait_ge(w_split, b + 1)
                src = w_dram[ds(b, 1)].rearrange("o p n -> (o p) n")
                sp.dma_start(raw[:], src).then_inc(w_loaded, 16)
                if comb_dram is not None and b >= 1:
                    with sp.Fori(0, NCH) as c:
                        sp.wait_ge(cb_used, c + NCH * (b - 1) + 1)
                        for half in range(2):
                            e0 = (b - 1) * EPB + half
                            rows = comb_dram.rearrange("(o ht two) t -> o ht two t", o=1, two=2)[
                                :, (b - 1) * HT:b * HT, half, ds(c * 512, 512)]
                            sp.dma_start(cb[64 * half:64 * half + 64], rows.broadcast_to([64, HT, 512])
                                         ).then_inc(cb_loaded, 16)
            over_blocks(sp, load)

        @block.gpsimd
        def _(pool):
            pool.sem_inc(w_split, 1)
            def split(b, p):
                pool.wait_ge(w_loaded, b * 16 + 16)
                pool.wait_ge(w_used, b + 1)
                pool.tensor_tensor(whi[p][:], raw[:], one.broadcast_to([128, WN]), ALU.mult)
                pool.drain()
                pool.tensor_tensor(wlo[p][:], raw[:], whi[p][:].bitcast(F32), ALU.subtract).then_inc(w_split, 1)
            over_blocks(pool, split)

        @block.tensor
        def _(pe):
            pe.sem_inc(w_used, 2)
            pe.sem_inc(h_used, 2)
            pe.wait_ge(x_ready, 1)

            def chunk(b, p, c):
                n = b * NCH + c
                u0 = n * HT

                def gate_up(ht, q):
                    pe.wait_ge(gu_free, u0 + ht + 1)
                    for out, cols in ((gate, gate_cols), (up, up_cols)):
                        m = 0
                        for k in range(KT):
                            for w, x in ((whi, xhi), (whi, xlo), (wlo, xhi)):
                                last = pe.matmul(out[q][:], w[p][:, cols(k, ht)], x[:, k, ds(c * 512, 512)],
                                                 start=(m == 0), stop=(m == 3 * KT - 1))
                                m += 1
                    last.then_inc(gu_ready, 1)

                def down(ht, q):
                    pe.wait_ge(hhi_ready, u0 + ht + 1)
                    if ht == 0:
                        pe.wait_ge(y_free, n + 1)
                    for part in range(2):
                        if part == 1:
                            pe.wait_ge(hlo_ready, u0 + ht + 1)
                        for j in range(CH):
                            for w in ((whi, wlo) if part == 0 else (whi,)):
                                h = hhi if part == 0 else hlo
                                first = ht == 0 and part == 0 and w is whi and j % 2 == 0
                                last = pe.matmul(y[p][j // 2][:, (j % 2) * D:(j % 2 + 1) * D],
                                                 h[q][:, j * 128:(j + 1) * 128], w[p][:, down_cols(ht)],
                                                 start=first, stop=(ht == HT - 1 and part == 1),
                                                 skip_group_check=True)
                    last.then_inc(h_used, 1)

                pe.wait_ge(w_split, b + 1 + 1)
                gate_up(0, 0)
                for ht in range(1, HT):
                    gate_up(ht, ht % 2)
                    down(ht - 1, (ht - 1) % 2)
                down(HT - 1, (HT - 1) % 2)

            def one_block(b, p):
                with pe.Fori(0, NCH) as c:
                    chunk(b, p, c)
                pe.drain().then_inc(w_used, 1)
            over_blocks(pe, one_block)

        @block.scalar
        def _(act):
            with act.Fori(0, NCH) as c:
                act.copy(xhi[:, :, ds(c * 512, 512)], XNT[:, :, ds(c * 512, 512)]).then_inc(xh_ready, 1)

            def one_block(b, p):
                with act.Fori(0, NCH) as c:
                    for ht in range(HT):
                        q = ht % 2
                        u = (b * NCH + c) * HT + ht
                        act.wait_ge(gu_ready, u + 1)
                        act.activation(act_g[q][:], gate[q][:], ACT.Silu).then_inc(silu_ready, 1)
                        act.wait_ge(hid_ready, u + 1)
                        act.wait_ge(h_used, u + 1)
                        act.copy(hhi[q][:], hid[q][:]).then_inc(hhi_ready, 1)
            over_blocks(act, one_block)

        @block.vector
        def _(dve):
            dve.sem_inc(cb_used, 1)
            dve.sem_inc(gu_free, 2)
            dve.sem_inc(y_free, 1)
            dve.wait_ge(xh_ready, NCH)
            dve.tensor_tensor(xlo[:], XNT[:], xhi[:].bitcast(F32), ALU.subtract).then_inc(x_ready, 1)

            def one_block(b, p):
                with dve.Fori(0, NCH) as c:
                    n = b * NCH + c
                    for ht in range(HT):
                        q = ht % 2
                        u = n * HT + ht
                        dve.wait_ge(silu_ready, u + 1)
                        dve.tensor_tensor(hid[q][:], act_g[q][:], up[q][:], ALU.mult).then_inc(gu_free, 1)
                        if comb_dram is not None and b >= 1:
                            dve.drain()
                            if ht == 0:
                                dve.wait_ge(cb_loaded, (n - NCH) * 32 + 32)
                            last = dve.tensor_tensor(hid[q][:], hid[q][:], cb[:, ht], ALU.mult)
                            if ht == HT - 1:
                                last.then_inc(cb_used, 1)
                        dve.drain().then_inc(hid_ready, 1)
                        dve.wait_ge(hhi_ready, u + 1)
                        dve.tensor_tensor(hlo[q][:], hid[q][:], hhi[q][:].bitcast(F32), ALU.subtract
                                          ).then_inc(hlo_ready, 1)
                    dve.wait_ge(h_used, (n + 1) * HT + 2)
                    for j in range(CH):
                        xs = X[:, ds(c * CH + j, 1), :].rearrange("p o d -> p (o d)")
                        scale = tanh_col if CW is None else CW[:, ds(c * CH + j, 1), ds(b, 1)].rearrange("p a b -> p (a b)")
                        last = dve.scalar_tensor_tensor(xs, y[p][j // 2][:, (j % 2) * D:(j % 2 + 1) * D], scale, xs,
                                                        ALU.mult, ALU.add)
                    last.then_inc(y_free, 1)
            over_blocks(dve, one_block)


def program(nc, x, ctx_in, ctxT, mask, consts, g_xattn, g_ffn, wg, bg_i, bg_f, ln_scale, rw0, eb0, w0,
            wqkv, bqk, bv, rw1, eb1, w1, out):
    m_dram = nc.dram_tensor("m_rows", (128, 128), F32, kind="Internal").ap()
    comb_dram = nc.dram_tensor("comb_rows", (E1, T), F32, kind="Internal").ap()
    with ExitStack() as ctx:
        sb = lambda n, s, d=F32: ctx.enter_context(nc.sbuf_tensor(n, s, d))
        X = sb("X", [128, B, D])
        XNT = sb("XNT", [128, KT, T])
        cst = sb("cst", [128, C_END])
        g_in = sb("g_in", [128, 4])
        g_tanh = sb("g_tanh", [128, 4])
        lns = sb("lns", [128, D])
        ln_tanh = sb("ln_tanh", [128, D])
        CW = sb("CW", [128, B, NB0])

        with nc.semaphore("p_loaded") as loaded, nc.semaphore("p_tanh") as tanh_ready, nc.Block() as block:
            @block.sync
            def _(sp):
                sp.dma_start(X[:], x.rearrange("b p d -> p b d")).then_inc(loaded, 16)
                sp.dma_start(cst[:], consts).then_inc(loaded, 16)
                sp.dma_start(g_in[:, 0:2], g_xattn.rearrange("(o n) -> o n", o=1).broadcast_to([128, 2])).then_inc(loaded, 16)
                sp.dma_start(g_in[:, 2:4], g_ffn.rearrange("(o n) -> o n", o=1).broadcast_to([128, 2])).then_inc(loaded, 16)
                sp.dma_start(lns[:], ln_scale.rearrange("(o n) -> o n", o=1).broadcast_to([128, D])).then_inc(loaded, 16)
                sp.wait_ge(loaded, 80)

            @block.scalar
            def _(act):
                act.wait_ge(loaded, 80)
                act.activation(g_tanh[:], g_in[:], ACT.Tanh).then_inc(tanh_ready, 1)

            @block.vector
            def _(dve):
                dve.wait_ge(loaded, 80)
                dve.wait_ge(tanh_ready, 1)
                dve.tensor_scalar(ln_tanh[:], lns[:], g_tanh[:, 0:1], None, ALU.mult)

        norm_transpose(nc, "n0_", X, XNT, cst)
        with ExitStack() as ctx0:
            AT = ctx0.enter_context(nc.sbuf_tensor("AT", [128, 128], F32))
            ET = ctx0.enter_context(nc.sbuf_tensor("ET", [128, 128], F32))
            with (nc.sbuf_tensor("ctxT_all", [128, KT, T], F32) as ctxT_all,
                  nc.sbuf_tensor("wg_sb", [128, 3 * KT, 16], F32) as wg_sb,
                  nc.sbuf_tensor("bg_sb", [128, 16], F32) as bg_sb):
                def run_loads(sp, loaded):
                    with nc.allow_non_contiguous_dma(reason="small"):
                        sp.dma_start(ctxT_all[:], ctxT).then_inc(loaded, 16)
                        sp.dma_start(wg_sb[:], wg).then_inc(loaded, 16)
                        sp.dma_start(bg_sb[:, 0:8], bg_i.rearrange("(o n) -> o n", o=1).broadcast_to([128, 8])).then_inc(loaded, 16)
                        sp.dma_start(bg_sb[:, 8:16], bg_f.rearrange("(o n) -> o n", o=1).broadcast_to([128, 8])).then_inc(loaded, 16)
                    return 4
                gates(nc, XNT, ctxT_all, cst, wg_sb, bg_sb, AT[:], ET[:], m_dram, run_loads)
            cell(nc, X, XNT, ctxT, ctx_in, m_dram, cst, AT, ET, ln_tanh[:])
        norm_transpose(nc, "n1_", X, XNT, cst)
        route0(nc, XNT, rw0, eb0, cst, CW, g_tanh[:, 2:3])
        feed_forward(nc, "f0_", X, XNT, w0, NB0, CW, None, None, cst[:, C_ONE:C_ONE + 1])
        norm_transpose(nc, "n2_", X, XNT, cst)
        attention(nc, X, XNT, ctxT, mask, wqkv, bqk, bv, cst, g_tanh[:, 1:2])
        norm_transpose(nc, "n3_", X, XNT, cst)
        route1(nc, XNT, rw1, eb1, cst, comb_dram)
        feed_forward(nc, "f1_", X, XNT, w1, NB1, None, g_tanh[:, 3:4], comb_dram, cst[:, C_ONE:C_ONE + 1])

        with nc.semaphore("stored") as stored, nc.Block() as block:
            @block.sync
            def _(sp):
                sp.dma_start(out.rearrange("b p d -> p b d"), X[:]).then_inc(stored, 16)
                sp.wait_ge(stored, 16)


def constants():
    c = np.zeros((128, C_END), np.float32)
    p = np.arange(128)
    c[:, C_ID:C_ID + 128] = np.eye(128)
    c[:, C_PEN:C_PEN + 128] = np.where(p[None, :] >= p[:, None], 0.0, BIG)
    c[:, C_BD0:C_BD0 + 4] = p[:, None] // DH0 == np.arange(4)
    c[:, C_BD1:C_BD1 + 8] = p[:, None] // DH1 == np.arange(8)
    c[:, C_REV:C_REV + 16] = 16 - np.arange(16)
    c[:, C_EPS] = LN_EPS
    c[:, C_ONE] = 1.0
    c[:, C_LNR] = math.log(ROOT0)
    return c


def kernel(**inputs):
    import numpy as _np
    import concourse.bacc as _bacc
    from concourse import mybir as _mybir
    from concourse.bass_utils import run_bass_kernel_spmd as _run

    a = {k: _np.asarray(v) for k, v in inputs.items()}

    def rows(m):
        return m.reshape(-1, 128, m.shape[-1]).transpose(1, 0, 2)

    def ffn_block(gate, up, down):
        return _np.concatenate([rows(m).reshape(128, -1) for m in (gate, up, down)], axis=1)

    ctx_in = a["ctx_1024"]
    gate_w = _np.concatenate([a["L0_xattn_igate_w"], a["L0_xattn_fgate_w"]], axis=0)
    w0 = [ffn_block(a["L0_ffn_sw1"][i].T, a["L0_ffn_sw3"][i].T, a["L0_ffn_sw2"][i].T) for i in range(NSH0)]
    w0 += [ffn_block(a["L0_ffn_w1"][i].T, a["L0_ffn_w3"][i].T, a["L0_ffn_w2"][i].T) for i in range(E0)]
    w1 = [ffn_block(a["L1_ffn_shared_gate_w"].T, a["L1_ffn_shared_up_w"].T, a["L1_ffn_shared_down_w"].T)]
    for b in range(NB1 - 1):
        e = slice(b * EPB, (b + 1) * EPB)
        w1.append(ffn_block(a["L1_ffn_gate_w"][e].transpose(1, 0, 2).reshape(D, HID),
                            a["L1_ffn_up_w"][e].transpose(1, 0, 2).reshape(D, HID),
                            a["L1_ffn_down_w"][e].reshape(HID, D)))
    wqkv = _np.stack([rows(a["L1_xattn_" + n].T) for n in ("Wq", "Wk", "Wv")])
    bqk = _np.stack([a["L1_xattn_" + n].reshape(KT, 128).T for n in ("bq", "bk")], axis=1)
    feeds = [
        ("x", a["x"]), ("ctx_in", ctx_in), ("ctxT", rows(ctx_in.reshape(T, D).T)), ("mask", a["mask_BxSxS2_ff1"]),
        ("consts", constants()), ("g_xattn", a["g_xattn"]), ("g_ffn", a["g_ffn"]), ("wg", rows(gate_w.T)),
        ("bg_i", a["L0_xattn_igate_b"]), ("bg_f", a["L0_xattn_fgate_b"]), ("ln_scale", a["L0_xattn_ln_scale"]),
        ("rw0", rows(a["L0_ffn_router_w"].T)), ("eb0", a["L0_ffn_expert_bias"]), ("w0", _np.stack(w0)),
        ("wqkv", wqkv), ("bqk", bqk), ("bv", a["L1_xattn_bv"]),
        ("rw1", rows(a["L1_ffn_router_w"].T)), ("eb1", a["L1_ffn_correction_bias"]), ("w1", _np.stack(w1)),
    ]
    nc = _bacc.Bacc("TRN2", target_bir_lowering=False, num_devices=1)
    arrays, args = {}, []
    for name, v in feeds:
        v = _np.ascontiguousarray(v)
        arrays[f"in_{name}_dram"] = v
        args.append(nc.dram_tensor(f"in_{name}_dram", v.shape, _mybir.dt.from_np(v.dtype), kind="ExternalInput").ap())
    args.append(nc.dram_tensor("out_0_dram", (B, S, D), _mybir.dt.float32, kind="ExternalOutput").ap())
    program(nc, *args)
    r = _run(nc, [arrays], core_ids=[0])
    return r.results[0]["out_0_dram"]
```

```python
from contextlib import ExitStack
import math
import numpy as np
import concourse.bass as bass
from concourse import mybir

F32 = mybir.dt.float32
F32R = mybir.dt.float32r
U32 = mybir.dt.uint32
I32 = mybir.dt.int32
ALU = mybir.AluOpType
ACT = mybir.ActivationFunctionType
AX = mybir.AxisListType
ds = bass.ds

B, S, D = 16, 128, 256
KT = D // 128
T = B * S
CH = 4
NCH = B // CH
NH0, DH0 = 8, 32
NH1, DH1 = 16, 16
HID = 512
HT = HID // 128
E0, NSH0 = 8, 2
NB0 = E0 + NSH0
E1, H1 = 16, 64
EPB = HID // H1
NB1 = 1 + E1 // EPB
G1 = 4
EPG = E1 // G1
LN_EPS = 1e-5
CELL_EPS = 1e-6
ROOT0 = math.sqrt(DH0)
BIG = 1e30

NT = 2 * T // 128 + E0 - 1
_cols, C = 0, {}
for _name, _n in (("ID", 128), ("PEN", 128), ("BD0", 4), ("BD1", 8), ("REV", 16), ("EPS", 1), ("LNR", 1), ("ONE", 1),
                  ("TRI", 128), ("ONES", 128), ("KEEP", 128), ("STEP", B), ("TILE", NT)):
    C[_name] = _cols
    _cols += _n
C_ID, C_PEN, C_BD0, C_BD1, C_REV, C_EPS, C_LNR, C_ONE, C_TRI, C_ONES, C_KEEP, C_STEP, C_TILE = C.values()
C_END = _cols


def norm_transpose(nc, tag, X, XNT, cst, XN=None):
    with ExitStack() as ctx:
        sb = lambda n, s, d=F32: ctx.enter_context(nc.sbuf_tensor(tag + n, s, d))
        sem = lambda n: ctx.enter_context(nc.semaphore(tag + n))
        stats = sb("stats", [128, B, 6])
        mean_var = sb("mean_var", [128, B, 2])
        std = sb("std", [128, B])
        rstd = sb("rstd", [128, B])
        xn = XN if XN is not None else sb("xn", [128, B, D])
        turned = [[ctx.enter_context(nc.psum_tensor(f"{tag}tp{p}{k}", [128, 512], F32)) for k in range(KT)]
                  for p in range(2)]
        var_ready, std_ready, xn_ready = sem("var_ready"), sem("std_ready"), sem("xn_ready")
        turned_ready, turned_free = sem("turned_ready"), sem("turned_free")
        block = ctx.enter_context(nc.Block())

        @block.vector
        def _(dve):
            with dve.Fori(0, B) as s:
                dve.bn_stats(stats[:, ds(s, 1), :], X[:, ds(s, 1), :])
            dve.drain()
            for s in range(B):
                dve.bn_aggr(mean_var[:, s, :], stats[:, s, :])
            dve.drain().then_inc(var_ready, 1)
            dve.wait_ge(std_ready, 1)
            dve.reciprocal(rstd[:], std[:])
            dve.drain()
            for s in range(B):
                last = dve.tensor_scalar(xn[:, s, :], X[:, s, :], mean_var[:, s, 0:1], rstd[:, s:s + 1],
                                         ALU.subtract, ALU.mult)
                if s % CH == CH - 1:
                    last.then_inc(xn_ready, 1)

        @block.tensor
        def _(pe):
            for c in range(NCH):
                pe.wait_ge(xn_ready, c + 1)
                if c >= 2:
                    pe.wait_ge(turned_free, c - 1)
                for k in range(KT):
                    for j in range(CH):
                        last = pe.transpose(turned[c % 2][k][:, j * 128:(j + 1) * 128],
                                            xn[:, c * CH + j, k * 128:(k + 1) * 128], cst[:, C_ID:C_ID + 128])
                last.then_inc(turned_ready, 1)

        @block.scalar
        def _(act):
            act.wait_ge(var_ready, 1)
            act.activation(std[:], mean_var[:, :, 1], ACT.Sqrt, bias=cst[:, C_EPS:C_EPS + 1]).then_inc(std_ready, 1)
            for c in range(NCH):
                act.wait_ge(turned_ready, c + 1)
                for k in range(KT):
                    last = act.copy(XNT[:, k, c * 512:(c + 1) * 512], turned[c % 2][k][:])
                last.then_inc(turned_free, 1)


def gates(nc, XNT, ctxT, cst, wg, bg, AT, ET, m_dram, run_loads):
    with ExitStack() as ctx:
        sb = lambda n, s, d=F32: ctx.enter_context(nc.sbuf_tensor("g_" + n, s, d))
        sem = lambda n: ctx.enter_context(nc.semaphore("g_" + n))
        gate_tok = sb("gate_tok", [128, 2, B, NH0])
        gate_row = sb("gate_row", [128, 2, 128])
        absf, ef, lf, logf, ones = (sb(n, [128, 128]) for n in ("absf", "ef", "lf", "logf", "ones"))
        cs, a_row, m_row, ml, e_row = (sb(n, [128, 128]) for n in ("cs", "a_row", "m_row", "ml", "e_row"))
        gate_ps = ctx.enter_context(nc.psum_tensor("g_gate", [128, 512], F32))
        row_ps = ctx.enter_context(nc.psum_tensor("g_row", [128, 512], F32))
        tok_ps = ctx.enter_context(nc.psum_tensor("g_tok", [128, 512], F32))
        loaded, gate_ready, tok_ready, row_ready = sem("loaded"), sem("gate_ready"), sem("tok_ready"), sem("row_ready")
        abs_ready, ln_ready, max_ready, exp_ready = sem("abs_ready"), sem("ln_ready"), sem("max_ready"), sem("exp_ready")
        back_ready, m_stored, act_chain = sem("back_ready"), sem("m_stored"), sem("act_chain")
        block = ctx.enter_context(nc.Block())

        @block.sync
        def _(sp):
            n = run_loads(sp, loaded)
            sp.wait_ge(loaded, 16 * n)
            sp.wait_ge(max_ready, 1)
            sp.dma_start(m_dram, m_row[:]).then_inc(m_stored, 16)
            sp.wait_ge(m_stored, 16)

        @block.tensor
        def _(pe):
            pe.wait_ge(loaded, 16 * 4)
            for s in range(B):
                for k in range(3 * KT):
                    src = XNT if k < KT else ctxT
                    last = pe.matmul(gate_ps[:, s * 16:(s + 1) * 16], src[:, k % KT, s * 128:(s + 1) * 128],
                                     wg[:, k, :], start=(k == 0), stop=(k == 3 * KT - 1))
            last.then_inc(gate_ready, 1)
            pe.wait_ge(tok_ready, 1)
            for g in range(2):
                last = pe.transpose(row_ps[:, g * 128:(g + 1) * 128],
                                    gate_tok[:, g, :, :].rearrange("p s h -> p (s h)"), cst[:, C_ID:C_ID + 128])
            last.then_inc(row_ready, 1)
            pe.wait_ge(exp_ready, 1)
            pe.transpose(tok_ps[:, 0:128], a_row[:], cst[:, C_ID:C_ID + 128])
            pe.transpose(tok_ps[:, 128:256], e_row[:], cst[:, C_ID:C_ID + 128]).then_inc(back_ready, 1)

        @block.vector
        def _(dve):
            dve.memset(ones[:], 1.0)
            dve.wait_ge(loaded, 16 * 4)
            dve.wait_ge(gate_ready, 1)
            dve.tensor_tensor(gate_tok[:].rearrange("p g s h -> p s g h"),
                              gate_ps[:, 0:256].rearrange("p (s g h) -> p s g h", s=B, g=2),
                              bg[:].rearrange("p (o g h) -> p o g h", o=1, g=2).broadcast_to([128, B, 2, NH0]),
                              ALU.add).then_inc(tok_ready, 1)
            dve.wait_ge(row_ready, 1)
            dve.tensor_copy(gate_row[:].rearrange("p g t -> p (g t)"), row_ps[:, 0:256])
            dve.drain()
            ig, fg = gate_row[:, 0, :], gate_row[:, 1, :]
            dve.scalar_tensor_tensor(absf[:], fg, -1.0, fg, ALU.mult, ALU.max)
            dve.drain().then_inc(abs_ready, 1)
            dve.wait_ge(ln_ready, 1)
            dve.scalar_tensor_tensor(logf[:], fg, 0.0, lf[:], ALU.min, ALU.subtract)
            dve.drain()
            dve.tensor_tensor_scan(cs[:], ones[:], logf[:], 0.0, ALU.mult, ALU.add)
            dve.drain()
            dve.tensor_tensor(a_row[:], ig, cs[:], ALU.subtract)
            dve.drain()
            dve.tensor_tensor_scan(m_row[:], a_row[:], a_row[:], -3e38, ALU.max, ALU.max)
            dve.drain()
            dve.tensor_tensor(ml[:], cs[:], m_row[:], ALU.add)
            dve.drain().then_inc(max_ready, 1)
            dve.wait_ge(back_ready, 1)
            dve.tensor_copy(AT, tok_ps[:, 0:128])
            dve.tensor_copy(ET, tok_ps[:, 128:256])

        @block.scalar
        def _(act):
            act.wait_ge(abs_ready, 1)
            act.activation(ef[:], absf[:], ACT.Exp, scale=-1.0).then_inc(act_chain, 1)
            act.wait_ge(act_chain, 1)
            act.activation(lf[:], ef[:], ACT.Ln, bias=1.0).then_inc(ln_ready, 1)
            act.wait_ge(max_ready, 1)
            act.activation(e_row[:], ml[:], ACT.Exp, bias=cst[:, C_LNR:C_LNR + 1], scale=-1.0).then_inc(exp_ready, 1)


def cell(nc, X, XNT, ctxT_dram, ctx_dram, m_dram, cst, AT, ET, ln_tanh):
    with ExitStack() as ctx:
        sb = lambda n, s, d=F32: ctx.enter_context(nc.sbuf_tensor("c_" + n, s, d))
        sem = lambda n: ctx.enter_context(nc.semaphore("c_" + n))
        two = lambda f, n, *a: [f(f"{n}{p}", *a) for p in range(2)]
        keyT = two(sb, "keyT", [128, KT, 128])
        val = two(sb, "val", [128, NH0, DH0])
        val1 = two(sb, "val1", [128, NH0, DH0 + 1])
        mrow = two(sb, "mrow", [128, NH0, 128])
        qbd = two(sb, "qbd", [128, KT, 4, 128])
        expo = two(sb, "expo", [128, NH0, 128])
        dmat = two(sb, "dmat", [128, NH0, 128])
        cmat = two(sb, "cmat", [128, NH0, 128])
        rsum = two(sb, "rsum", [128, NH0])
        den = two(sb, "den", [128, NH0])
        rden = two(sb, "rden", [128, NH0])
        h = sb("h", [128, B, D])
        hstats = sb("hstats", [128, B, 6])
        hmv = sb("hmv", [128, B, 2])
        hstd = sb("hstd", [128, B])
        hrstd = sb("hrstd", [128, B])
        score = [[ctx.enter_context(nc.psum_tensor(f"c_score{p}{k}", [128, 512], F32)) for k in range(KT)]
                 for p in range(2)]
        pv = [ctx.enter_context(nc.psum_tensor(f"c_pv{p}", [128, 512], F32)) for p in range(2)]
        loaded, q_ready, v_ready = two(sem, "loaded"), two(sem, "q_ready"), two(sem, "v_ready")
        score_ready, expo_ready, dmat_ready = two(sem, "score_ready"), two(sem, "expo_ready"), two(sem, "dmat_ready")
        cmat_ready, pv_ready, h_ready = two(sem, "cmat_ready"), two(sem, "pv_ready"), two(sem, "h_ready")
        hvar_ready, hstd_ready = sem("hvar_ready"), sem("hstd_ready")
        block = ctx.enter_context(nc.Block())

        @block.sync
        def _(sp):
            with sp.Fori(0, B // 2) as i:
                for p in range(2):
                    sp.wait_ge(score_ready[p], i + 1)
                    sp.dma_start(keyT[p][:], ctxT_dram[:, :, ds(i * 256 + p * 128, 128)]).then_inc(loaded[p], 16)
                    sp.wait_ge(v_ready[p], i + 1)
                    sp.dma_start(val[p][:].rearrange("p h d -> p (h d)"),
                                 ctx_dram[ds(i * 2 + p, 1)].rearrange("o p d -> (o p) d")).then_inc(loaded[p], 16)
                    sp.wait_ge(expo_ready[p], i + 1)
                    sp.dma_start(mrow[p][:].rearrange("p h t -> p (h t)"),
                                 m_dram.rearrange("(b h) t -> b (h t)", b=B)[ds(i * 2 + p, 1)]
                                 .broadcast_to([128, NH0 * 128])).then_inc(loaded[p], 16)

        @block.gpsimd
        def _(pool):
            for p in range(2):
                pool.sem_inc(v_ready[p], 1)
            for p in range(2):
                pool.memset(val1[p][:], 1.0)
            pool.drain()
            with pool.Fori(0, B // 2) as i:
                for p in range(2):
                    pool.wait_ge(score_ready[p], i + 1)
                    for k in range(KT):
                        last = pool.tensor_tensor(
                            qbd[p][:, k],
                            XNT[:, k, ds(i * 256 + p * 128, 128)].rearrange("p (o t) -> p o t", o=1)
                            .broadcast_to([128, 4, 128]),
                            cst[:, C_BD0:C_BD0 + 4].rearrange("p (h o) -> p h o", o=1).broadcast_to([128, 4, 128]),
                            ALU.mult)
                    last.then_inc(q_ready[p], 1)
                    pool.wait_ge(loaded[p], i * 48 + 48)
                    pool.wait_ge(pv_ready[p], i + 1)
                    pool.tensor_tensor(val1[p][:, :, 0:DH0], val[p][:],
                                       cst[:, C_ONE:C_ONE + 1].rearrange("p (a b) -> p a b", a=1)
                                       .broadcast_to([128, NH0, DH0]), ALU.mult).then_inc(v_ready[p], 1)

        @block.tensor
        def _(pe):
            for p in range(2):
                pe.sem_inc(score_ready[p], 1)
                pe.sem_inc(pv_ready[p], 1)
            with pe.Fori(0, B // 2) as i:
                for p in range(2):
                    pe.wait_ge(loaded[p], i * 48 + 48)
                    pe.wait_ge(q_ready[p], i + 1)
                    pe.wait_ge(cmat_ready[p], i + 1)
                    for k in range(KT):
                        last = pe.matmul(score[p][k][:], keyT[p][:, k], qbd[p][:, k], start=True, stop=True)
                    last.then_inc(score_ready[p], 1)
                for p in range(2):
                    pe.wait_ge(v_ready[p], i + 1 + 1)
                    pe.wait_ge(cmat_ready[p], i + 1 + 1)
                    pe.wait_ge(h_ready[p], i + 1)
                    for n in range(NH0):
                        last = pe.matmul(pv[p][:, n * 33:(n + 1) * 33], cmat[p][:, n], val1[p][:, n],
                                         start=True, stop=True)
                    last.then_inc(pv_ready[p], 1)

        @block.scalar
        def _(act):
            for p in range(2):
                act.sem_inc(dmat_ready[p], 1)
            with act.Fori(0, B // 2) as i:
                for p in range(2):
                    act.wait_ge(expo_ready[p], i + 1 + 1)
                    act.wait_ge(cmat_ready[p], i + 1)
                    act.activation(dmat[p][:], expo[p][:], ACT.Exp, scale=-1.0).then_inc(dmat_ready[p], 1)
            act.wait_ge(hvar_ready, 1)
            act.activation(hstd[:], hmv[:, :, 1], ACT.Sqrt, bias=cst[:, C_EPS:C_EPS + 1]).then_inc(hstd_ready, 1)

        @block.vector
        def _(dve):
            for p in range(2):
                dve.sem_inc(expo_ready[p], 1)
                dve.sem_inc(cmat_ready[p], 1)
                dve.sem_inc(h_ready[p], 1)
            with dve.Fori(0, B // 2) as i:
                for p in range(2):
                    dve.wait_ge(loaded[p], i * 48 + 48)
                    dve.wait_ge(dmat_ready[p], i + 1)
                    for n in range(NH0):
                        last = dve.scalar_tensor_tensor(
                            expo[p][:, n], mrow[p][:, n], AT[:, ds(i * 16 + p * 8 + n, 1)],
                            cst[:, C_PEN:C_PEN + 128], ALU.subtract, ALU.max)
                    last.then_inc(expo_ready[p], 1)
                for p in range(2):
                    dve.wait_ge(dmat_ready[p], i + 1 + 1)
                    dve.wait_ge(score_ready[p], i + 1 + 1)
                    dve.wait_ge(pv_ready[p], i + 1)
                    for k in range(KT):
                        last = dve.tensor_tensor(cmat[p][:, 4 * k:4 * k + 4].rearrange("p h t -> p (h t)"),
                                                 score[p][k][:],
                                                 dmat[p][:, 4 * k:4 * k + 4].rearrange("p h t -> p (h t)"), ALU.mult)
                    last.then_inc(cmat_ready[p], 1)
                for p in range(2):
                    dve.wait_ge(pv_ready[p], i + 1 + 1)
                    o = pv[p][:, 0:NH0 * 33].rearrange("p (h d) -> p h d", h=NH0)
                    dve.tensor_copy(rsum[p][:], o[:, :, DH0])
                    dve.drain()
                    dve.scalar_tensor_tensor(den[p][:], rsum[p][:], -1.0, rsum[p][:], ALU.mult, ALU.max)
                    dve.drain()
                    dve.tensor_tensor(rsum[p][:], den[p][:], ET[:, ds(i * 16 + p * 8, 8)], ALU.max)
                    dve.drain()
                    dve.tensor_scalar(den[p][:], rsum[p][:], CELL_EPS * ROOT0, None, ALU.add)
                    dve.drain()
                    dve.reciprocal(rden[p][:], den[p][:])
                    dve.drain()
                    dve.tensor_tensor(h[:, ds(i * 2 + p, 1), :].rearrange("p o (h d) -> p (o h) d", h=NH0),
                                      o[:, :, 0:DH0],
                                      rden[p][:].rearrange("p (h o) -> p h o", o=1).broadcast_to([128, NH0, DH0]),
                                      ALU.mult).then_inc(h_ready[p], 1)
            dve.drain()
            with dve.Fori(0, B) as s:
                dve.bn_stats(hstats[:, ds(s, 1), :], h[:, ds(s, 1), :])
            dve.drain()
            for s in range(B):
                dve.bn_aggr(hmv[:, s, :], hstats[:, s, :])
            dve.drain().then_inc(hvar_ready, 1)
            dve.wait_ge(hstd_ready, 1)
            dve.reciprocal(hrstd[:], hstd[:])
            dve.drain()
            with dve.Fori(0, B) as s:
                dve.tensor_scalar(h[:, ds(s, 1), :], h[:, ds(s, 1), :], hmv[:, ds(s, 1), 0:1], hrstd[:, ds(s, 1)],
                                  ALU.subtract, ALU.mult)
            dve.drain()
            dve.tensor_tensor(h[:], h[:], ln_tanh.rearrange("p (o d) -> p o d", o=1).broadcast_to([128, B, D]),
                              ALU.mult)
            dve.drain()
            dve.tensor_tensor(X[:], X[:], h[:], ALU.add)


def attention(nc, X, XNT, ctxT_dram, mask_dram, w_dram, bq_dram, bv_dram, cst, tanh_col):
    HH = NH1 // 2
    with ExitStack() as ctx:
        sb = lambda n, s, d=F32: ctx.enter_context(nc.sbuf_tensor("a_" + n, s, d))
        sem = lambda n: ctx.enter_context(nc.semaphore("a_" + n))
        pb = lambda n: ctx.enter_context(nc.psum_tensor("a_" + n, [128, 512], F32))
        two = lambda f, n, *a: [f(f"{n}{p}", *a) for p in range(2)]
        w = sb("w", [128, 3, KT, D])
        bqk = sb("bqk", [128, 2, KT])
        bv = sb("bv", [128, D])
        keyT = two(sb, "keyT", [128, KT, 128])
        msk, msk1, pen = two(sb, "msk", [128, 128]), two(sb, "msk1", [128, 128]), two(sb, "pen", [128, 128])
        qT, kT = two(sb, "qT", [128, KT, 128]), two(sb, "kT", [128, KT, 128])
        kbd = two(sb, "kbd", [128, KT, HH, 128])
        v1 = two(sb, "v1", [128, NH1, DH1 + 1])
        sc = [[sb(f"sc{p}{q}", [128, HH, 128]) for q in range(2)] for p in range(2)]
        pr = [[sb(f"pr{p}{q}", [128, HH, 128]) for q in range(2)] for p in range(2)]
        mx = two(sb, "mx", [128, HH])
        prT = two(sb, "prT", [128, 4, 128])
        rs, rs2 = sb("rs", [128, NH1]), sb("rs2", [128, NH1])
        o_sb = sb("o_sb", [128, D])
        proj = pb("proj")
        score = [[pb(f"score{q}{k}") for k in range(2)] for q in range(2)]
        turned = two(pb, "turned")
        out_ps = pb("out_ps")
        w_loaded, ones_ready = sem("w_loaded"), sem("ones_ready")
        k_loaded, m_loaded = two(sem, "k_loaded"), two(sem, "m_loaded")
        proj_ready, qk_ready, v_ready = sem("proj_ready"), sem("qk_ready"), sem("v_ready")
        kbd_ready, pen_ready = sem("kbd_ready"), sem("pen_ready")
        score_ready, score_free = sem("score_ready"), sem("score_free")
        max_ready, sub_ready, pr_ready = sem("max_ready"), two(sem, "sub_ready"), sem("pr_ready")
        turned_ready, prT_ready, pv_ready, out_free = sem("turned_ready"), sem("prT_ready"), sem("pv_ready"), sem("out_free")
        block = ctx.enter_context(nc.Block())

        def wait(eng, counter, value):
            if not isinstance(value, int) or value > 0:
                eng.wait_ge(counter, value)

        def over(eng, body):
            body(0, 0)
            body(1, 1)
            with eng.Fori(0, (B - 4) // 2) as i:
                body(i * 2 + 2, 0)
                body(i * 2 + 3, 1)
            body(B - 2, 0)
            body(B - 1, 1)

        tokens = lambda s: ds(s * 128, 128) if not isinstance(s, int) else slice(s * 128, (s + 1) * 128)
        bc = lambda a, n: a.rearrange("p (h o) -> p h o", o=1).broadcast_to([128, a.shape[1], n])
        rep = lambda a, n: a.rearrange("p (o t) -> p o t", o=1).broadcast_to([128, n, a.shape[1]])

        @block.sync
        def _(sp):
            sp.dma_start(w[:], w_dram.rearrange("w p k n -> p w k n")).then_inc(w_loaded, 16)
            sp.dma_start(bqk[:], bq_dram).then_inc(w_loaded, 16)
            sp.dma_start(bv[:], bv_dram.rearrange("(o n) -> o n", o=1).broadcast_to([128, D])).then_inc(w_loaded, 16)

            def load(s, p):
                wait(sp, proj_ready, 2 * s - 2)
                sp.dma_start(keyT[p][:], ctxT_dram[:, :, tokens(s)]).then_inc(k_loaded[p], 16)
                wait(sp, pen_ready, s - 1)
                sp.dma_start(msk[p][:], mask_dram[ds(s, 1)].rearrange("o q k -> (o q) k")).then_inc(m_loaded[p], 16)
            over(sp, load)

        @block.tensor
        def _(pe):
            pe.wait_ge(w_loaded, 48)

            def project_qk(s, p, nth):
                wait(pe, k_loaded[p], nth * 16)
                wait(pe, v_ready, s)
                for which in range(2):
                    for m in range(KT):
                        at = (which * KT + m) * 128
                        for k in range(KT):
                            src = XNT[:, k, tokens(s)] if which == 0 else keyT[p][:, k]
                            last = pe.matmul(proj[:, at:at + 128], w[:, which, k, m * 128:(m + 1) * 128], src,
                                             start=(k == 0), stop=(k == KT - 1))
                last.then_inc(proj_ready, 1)

            def project_v(s, p):
                pe.wait_ge(qk_ready, s + 1)
                for k in range(KT):
                    last = pe.matmul(proj[:, 0:256], keyT[p][:, k], w[:, 2, k], start=(k == 0), stop=(k == KT - 1))
                last.then_inc(proj_ready, 1)

            def scores(s, p, q):
                pe.wait_ge(kbd_ready, 2 * s + q + 1)
                wait(pe, score_free, 2 * s + q - 1)
                for g in range(2):
                    last = pe.matmul(score[q][g][:], qT[p][:, q], kbd[p][:, q, 4 * g:4 * g + 4], start=True, stop=True)
                last.then_inc(score_ready, 1)

            def values(s, p, q):
                n = (2 * s + q) * 2
                pe.wait_ge(pr_ready, 2 * s + q + 1)
                for g in range(2):
                    wait(pe, prT_ready, n + g - 1)
                    for j in range(4):
                        last = pe.transpose(turned[g][:, j * 128:(j + 1) * 128], pr[p][q][:, 4 * g + j],
                                            cst[:, C_ID:C_ID + 128])
                    last.then_inc(turned_ready, 1)
                if q == 0:
                    pe.wait_ge(v_ready, s + 1)
                    wait(pe, out_free, s)
                for g in range(2):
                    pe.wait_ge(prT_ready, n + g + 1)
                    for j in range(4):
                        hd = q * HH + 4 * g + j
                        last = pe.matmul(out_ps[:, hd * 17:(hd + 1) * 17], prT[g][:, j], v1[p][:, hd],
                                         start=True, stop=True)
                    last.then_inc(pv_ready, 1)

            def body(s, p, nth):
                first, end = isinstance(s, int) and s == 0, isinstance(s, int) and s == B - 1
                scores(s, p, 0)
                if not end:
                    project_qk(s + 1, 1 - p, nth)
                if not first:
                    values(s - 1, 1 - p, 0)
                if not end:
                    project_v(s + 1, 1 - p)
                scores(s, p, 1)
                if not first:
                    values(s - 1, 1 - p, 1)

            project_qk(0, 0, 1)
            project_v(0, 0)
            body(0, 0, 1)
            body(1, 1, 2)
            with pe.Fori(0, (B - 4) // 2) as i:
                body(i * 2 + 2, 0, i + 2)
                body(i * 2 + 3, 1, i + 3)
            body(B - 2, 0, B // 2)
            body(B - 1, 1, None)
            values(B - 1, 1, 0)
            values(B - 1, 1, 1)

        @block.gpsimd
        def _(pool):
            for p in range(2):
                pool.memset(v1[p][:], 1.0)
            pool.drain().then_inc(ones_ready, 1)

            def prepare(s, p, nth):
                pool.wait_ge(m_loaded[p], nth * 16)
                wait(pool, score_free, 2 * s - 2)
                pool.tensor_tensor(msk1[p][:], msk[p][:], cst[:, C_ONE:C_ONE + 1].broadcast_to([128, 128]),
                                   ALU.subtract)
                pool.drain()
                pool.tensor_scalar(pen[p][:], msk1[p][:], 10000.0, None, ALU.mult).then_inc(pen_ready, 1)
                pool.wait_ge(qk_ready, s + 1)
                wait(pool, score_ready, 2 * s - 2)
                for q in range(KT):
                    pool.tensor_tensor(kbd[p][:, q], rep(kT[p][:, q], HH), bc(cst[:, C_BD1:C_BD1 + HH], 128),
                                       ALU.mult).then_inc(kbd_ready, 1)

            def subtract(s, p):
                pool.wait_ge(max_ready, s + 1)
                pool.tensor_tensor(sc[p][1][:], sc[p][1][:], bc(mx[1][:], 128), ALU.subtract).then_inc(sub_ready[1], 1)

            prepare(0, 0, 1)
            prepare(1, 1, 1)
            subtract(0, 0)
            with pool.Fori(0, (B - 2) // 2) as i:
                prepare(i * 2 + 2, 0, i + 2)
                subtract(i * 2 + 1, 1)
                prepare(i * 2 + 3, 1, i + 2)
                subtract(i * 2 + 2, 0)
            subtract(B - 1, 1)

        @block.scalar
        def _(act):
            act.wait_ge(w_loaded, 48)

            def keep_qk(s, p):
                act.wait_ge(proj_ready, 2 * s + 1)
                wait(act, score_ready, 2 * s - 2)
                wait(act, kbd_ready, 2 * s - 2)
                for which, dst in ((0, qT), (1, kT)):
                    for m in range(KT):
                        at = (which * KT + m) * 128
                        last = act.activation(dst[p][:, m], proj[:, at:at + 128], ACT.Identity,
                                              bias=bqk[:, which, m:m + 1])
                last.then_inc(qk_ready, 1)

            def exps(s, p, q):
                act.wait_ge(sub_ready[q], s + 1)
                wait(act, turned_ready, 4 * s + 2 * q - 6)
                act.activation(pr[p][q][:], sc[p][q][:], ACT.Exp, scale=1.0 / math.sqrt(DH1)).then_inc(pr_ready, 1)

            def turn(s, q):
                for g in range(2):
                    n = 4 * s + 2 * q + g
                    act.wait_ge(turned_ready, n + 1)
                    wait(act, pv_ready, n - 1)
                    act.copy(prT[g][:].rearrange("p h t -> p (h t)"), turned[g][:]).then_inc(prT_ready, 1)

            def body(s, p):
                if not isinstance(s, int) or s < B - 1:
                    keep_qk(s + 1, 1 - p)
                if not isinstance(s, int) or s > 0:
                    turn(s - 1, 0)
                    turn(s - 1, 1)
                exps(s, p, 0)
                exps(s, p, 1)

            keep_qk(0, 0)
            over(act, body)
            turn(B - 1, 0)
            turn(B - 1, 1)

        @block.vector
        def _(dve):
            dve.wait_ge(w_loaded, 48)
            dve.wait_ge(ones_ready, 1)

            def keep_v(s, p):
                dve.wait_ge(proj_ready, 2 * s + 2)
                wait(dve, pv_ready, 4 * s - 4)
                dve.tensor_tensor(v1[p][:, :, 0:DH1], proj[:, 0:256].rearrange("p (h d) -> p h d", h=NH1),
                                  bv[:].rearrange("p (h d) -> p h d", h=NH1), ALU.add).then_inc(v_ready, 1)

            def soft(s, p, q):
                dve.wait_ge(score_ready, 2 * s + q + 1)
                dve.wait_ge(pen_ready, s + 1)
                wait(dve, pr_ready, 2 * s + q - 3)
                if q == 1:
                    wait(dve, sub_ready[1], s)
                for g in range(2):
                    last = dve.scalar_tensor_tensor(sc[p][q][:, 4 * g:4 * g + 4], rep(pen[p][:], 4), math.sqrt(DH1),
                                                    score[q][g][:].rearrange("p (h t) -> p h t", h=4),
                                                    ALU.mult, ALU.add)
                last.then_inc(score_free, 1)
                dve.drain()
                red = dve.tensor_reduce(mx[q][:], sc[p][q][:], AX.X, ALU.max)
                if q == 1:
                    red.then_inc(max_ready, 1)
                else:
                    dve.drain()
                    dve.tensor_tensor(sc[p][q][:], sc[p][q][:], bc(mx[q][:], 128), ALU.subtract).then_inc(sub_ready[0], 1)

            def finish(s):
                dve.wait_ge(pv_ready, 4 * s + 4)
                o = out_ps[:, 0:NH1 * 17].rearrange("p (h d) -> p h d", h=NH1)
                dve.reciprocal(rs[:], o[:, :, DH1])
                dve.drain()
                dve.tensor_scalar(rs2[:], rs[:], tanh_col, None, ALU.mult)
                dve.drain()
                dve.tensor_tensor(o_sb[:].rearrange("p (h d) -> p h d", h=NH1), o[:, :, 0:DH1], bc(rs2[:], DH1),
                                  ALU.mult).then_inc(out_free, 1)
                dve.drain()
                xs = X[:, ds(s, 1), :].rearrange("p o d -> p (o d)")
                dve.tensor_tensor(xs, xs, o_sb[:], ALU.add)

            def body(s, p):
                soft(s, p, 0)
                soft(s, p, 1)
                if not isinstance(s, int) or s < B - 1:
                    keep_v(s + 1, 1 - p)
                if not isinstance(s, int) or s > 0:
                    finish(s - 1)

            keep_v(0, 0)
            over(dve, body)
            finish(B - 1)


def top1(dve, src, oh, mx, rev, shape):
    bc = lambda a: a.rearrange("p g (k o) -> p g k o", o=1).broadcast_to(shape)
    dve.tensor_reduce(mx, src, AX.X, ALU.max)
    dve.drain()
    dve.tensor_tensor(oh, src, bc(mx), ALU.is_equal)
    dve.drain()
    dve.tensor_tensor(oh, oh, rev, ALU.mult)
    dve.drain()
    dve.tensor_reduce(mx, oh, AX.X, ALU.max)
    dve.drain()
    dve.tensor_tensor(oh, oh, bc(mx), ALU.is_equal)
    dve.drain()


def route0(nc, XNT, rw_dram, bias_dram, cst, slots, slot_weight, tile_expert, tanh_col):
    with ExitStack() as ctx:
        sb = lambda n, s, d=F32: ctx.enter_context(nc.sbuf_tensor("r0_" + n, s, d))
        sem = lambda n: ctx.enter_context(nc.semaphore("r0_" + n))
        rw = sb("rw", [128, KT, E0])
        eb = sb("eb", [128, E0])
        lg, oh0, oh1, l2 = (sb(n, [128, B, 1, E0]) for n in ("lg", "oh0", "oh1", "l2"))
        scratch, m1, m2, e2, w1 = (sb(n, [128, B, 1]) for n in ("scratch", "m1", "m2", "e2", "w1"))
        chosen, total, running, pos = (sb(n, [128, E0, B]) for n in ("chosen", "total", "running", "pos"))
        over = sb("over", [128, E0, B])
        ntile, tile_end, base = (sb(n, [128, E0]) for n in ("ntile", "tile_end", "base"))
        slot_f = sb("slot_f", [128, B, 2])
        ended = sb("ended", [1, NT, E0])
        expert_f, expert_c = sb("expert_f", [1, NT]), sb("expert_c", [1, NT])
        ps = ctx.enter_context(nc.psum_tensor("r0_ps", [128, 512], F32))
        count_ps = ctx.enter_context(nc.psum_tensor("r0_count", [128, 512], F32))
        loaded, logits_ready, diff_ready, exp_ready = sem("loaded"), sem("logits_ready"), sem("diff_ready"), sem("exp_ready")
        chosen_ready, counts_ready = sem("chosen_ready"), sem("counts_ready")
        block = ctx.enter_context(nc.Block())

        @block.sync
        def _(sp):
            sp.dma_start(rw[:], rw_dram).then_inc(loaded, 16)
            sp.dma_start(eb[:], bias_dram.rearrange("(o n) -> o n", o=1).broadcast_to([128, E0])).then_inc(loaded, 16)
            sp.wait_ge(loaded, 32)

        @block.tensor
        def _(pe):
            pe.wait_ge(loaded, 32)
            for s in range(B):
                for k in range(KT):
                    last = pe.matmul(ps[:, s * E0:(s + 1) * E0], XNT[:, k, s * 128:(s + 1) * 128], rw[:, k],
                                     start=(k == 0), stop=(k == KT - 1))
            last.then_inc(logits_ready, 1)
            pe.wait_ge(chosen_ready, 1)
            flat = chosen[:].rearrange("p e s -> p (e s)")
            pe.matmul(count_ps[:, 0:128], cst[:, C_TRI:C_TRI + 128], flat, start=True, stop=True)
            pe.matmul(count_ps[:, 128:256], cst[:, C_ONES:C_ONES + 128], flat, start=True, stop=True
                      ).then_inc(counts_ready, 1)

        @block.scalar
        def _(act):
            act.wait_ge(diff_ready, 1)
            act.activation(e2[:], w1[:], ACT.Exp).then_inc(exp_ready, 1)

        @block.vector
        def _(dve):
            dve.wait_ge(loaded, 32)
            dve.wait_ge(logits_ready, 1)
            shape = [128, B, 1, E0]
            rev = cst[:, C_REV:C_REV + E0].rearrange("p (a b e) -> p a b e", a=1, b=1).broadcast_to(shape)
            flat = lambda a: a[:].rearrange("p s b e -> p (s b e)")
            dve.tensor_tensor(lg[:], ps[:, 0:B * E0].rearrange("p (s b e) -> p s b e", s=B, b=1),
                              eb[:].rearrange("p (a b e) -> p a b e", a=1, b=1).broadcast_to(shape), ALU.add)
            dve.drain()
            dve.tensor_reduce(m1[:], lg[:], AX.X, ALU.max)
            top1(dve, lg[:], oh0[:], scratch[:], rev, shape)
            dve.scalar_tensor_tensor(flat(l2), flat(oh0), -BIG, flat(lg), ALU.mult, ALU.add)
            dve.drain()
            dve.tensor_reduce(m2[:], l2[:], AX.X, ALU.max)
            top1(dve, l2[:], oh1[:], scratch[:], rev, shape)
            dve.tensor_tensor(chosen[:].rearrange("p e s -> p s e"), oh0[:].rearrange("p s b e -> p s (b e)"),
                              oh1[:].rearrange("p s b e -> p s (b e)"), ALU.add).then_inc(chosen_ready, 1)
            dve.tensor_tensor(w1[:], m2[:], m1[:], ALU.subtract)
            dve.drain().then_inc(diff_ready, 1)
            dve.wait_ge(exp_ready, 1)
            dve.tensor_scalar(m1[:], e2[:], 1.0, None, ALU.add)
            dve.drain()
            dve.reciprocal(m2[:], m1[:])
            dve.drain()
            dve.tensor_scalar(slot_weight[:, :, 0:1], m2[:], tanh_col, None, ALU.mult)
            dve.drain()
            dve.tensor_tensor(slot_weight[:, :, 1:2], slot_weight[:, :, 0:1], e2[:], ALU.mult)
            dve.wait_ge(counts_ready, 1)
            cols = lambda a: a[:].rearrange("p e s -> p (e s)")
            dve.tensor_copy(cols(total), count_ps[:, 128:256])
            dve.drain()
            dve.tensor_tensor_scan(cols(running), cst[:, C_KEEP:C_KEEP + 128], cols(total), 0.0, ALU.mult, ALU.add)
            dve.drain()
            dve.tensor_tensor(over[:], running[:, :, B - 1:B].broadcast_to([128, E0, B]),
                              cst[:, C_STEP:C_STEP + B].rearrange("p (o j) -> p o j", o=1).broadcast_to([128, E0, B]),
                              ALU.is_gt)
            dve.drain()
            dve.tensor_reduce(ntile[:], over[:], AX.X, ALU.add)
            dve.drain()
            dve.tensor_tensor_scan(tile_end[:], cst[:, C_ONES:C_ONES + E0], ntile[:], 0.0, ALU.mult, ALU.add)
            dve.drain()
            dve.tensor_tensor(base[:], tile_end[:], ntile[:], ALU.subtract)
            dve.tensor_tensor(running[:], running[:], total[:], ALU.subtract)
            dve.drain()
            dve.scalar_tensor_tensor(running[:], base[:].rearrange("p (e o) -> p e o", o=1).broadcast_to([128, E0, B]),
                                     128.0, running[:], ALU.mult, ALU.add)
            dve.drain()
            dve.tensor_tensor(cols(pos), count_ps[:, 0:128], cols(running), ALU.add)
            dve.drain()
            for k, oh in enumerate((oh0, oh1)):
                dve.tensor_tensor(total[:].rearrange("p e s -> p s e") if k == 0 else over[:].rearrange("p e s -> p s e"),
                                  oh[:].rearrange("p s b e -> p s (b e)"), pos[:].rearrange("p e s -> p s e"), ALU.mult)
            dve.drain()
            for k, part in enumerate((total, over)):
                dve.tensor_reduce(slot_f[:, :, k:k + 1].rearrange("p s k -> p (s k)"), part[:].rearrange("p e s -> p s e"),
                                  AX.X, ALU.add)
            dve.tensor_tensor(ended[:], cst[0:1, C_TILE:C_TILE + NT].rearrange("p (i o) -> p i o", o=1)
                              .broadcast_to([1, NT, E0]),
                              tile_end[0:1, :].rearrange("p (o e) -> p o e", o=1).broadcast_to([1, NT, E0]), ALU.is_ge)
            dve.drain()
            dve.tensor_copy(slots[:], slot_f[:].rearrange("p s k -> p k s"))
            dve.tensor_reduce(expert_f[:], ended[:], AX.X, ALU.add)
            dve.drain()
            dve.tensor_scalar(expert_c[:], expert_f[:], float(E0 - 1), None, ALU.min)
            dve.drain()
            dve.tensor_copy(tile_expert[:], expert_c[:])


def routed_tiles(nc, W, w_dram, first_late, xg_dram, yg_dram, tile_expert, cst):
    with ExitStack() as ctx:
        sb = lambda n, s, d=F32: ctx.enter_context(nc.sbuf_tensor("t_" + n, s, d))
        sem = lambda n: ctx.enter_context(nc.semaphore("t_" + n))
        pb = lambda n: ctx.enter_context(nc.psum_tensor("t_" + n, [128, 512], F32))
        two = lambda f, n, *a: [f(f"{n}{p}", *a) for p in range(2)]
        x = two(sb, "x", [128, D])
        xT = two(sb, "xT", [128, KT, 128])
        act_g = two(sb, "act_g", [128, HID])
        hid = two(sb, "hid", [128, HID])
        hidT = two(sb, "hidT", [128, HT, 128])
        y = two(sb, "y", [128, D])
        gate, up, y_ps = two(pb, "gate"), two(pb, "up"), two(pb, "y_ps")
        x_turned, h_turned = pb("x_turned"), pb("h_turned")
        w_loaded = sem("w_loaded")
        x_loaded, y_stored = two(sem, "x_loaded"), two(sem, "y_stored")
        xt_ready, xT_ready, gate_ready, up_ready = sem("xt_ready"), sem("xT_ready"), sem("gate_ready"), sem("up_ready")
        silu_ready, hid_ready, ht_ready, hidT_ready = sem("silu_ready"), sem("hid_ready"), sem("ht_ready"), sem("hidT_ready")
        down_ready, y_ready = sem("down_ready"), sem("y_ready")
        block = ctx.enter_context(nc.Block())

        def wait(eng, counter, value):
            if not isinstance(value, int) or value > 0:
                eng.wait_ge(counter, value)

        def over(eng, body):
            body(0, 0, 1)
            body(1, 1, 2 - 1)
            pairs = (NT - 5) // 2
            with eng.Fori(0, pairs) as j:
                body(j * 2 + 2, 0, j + 2)
                body(j * 2 + 3, 1, j + 2)
            for i in range(2 + 2 * pairs, NT):
                body(i, i % 2, i // 2 + 1)

        inside = lambda i, n: not isinstance(i, int) or i < n

        @block.sync
        def _(sp):
            for e in range(first_late, E0):
                sp.dma_start(W[:, e, :], w_dram[NSH0 + e]).then_inc(w_loaded, 16)

            def load(i, p):
                wait(sp, xt_ready, i - 1)
                sp.dma_start(x[p][:], xg_dram[ds(i * 128, 128), :]).then_inc(x_loaded[p], 16)

            def body(i, p, nth):
                if inside(i, NT - 2):
                    load(i + 2, p)
                sp.wait_ge(y_ready, i + 1)
                sp.dma_start(yg_dram[ds(i * 128, 128), :], y[p][:]).then_inc(y_stored[p], 16)
            load(0, 0)
            load(1, 1)
            over(sp, body)
            for p in range(2):
                sp.wait_ge(y_stored[p], 16 * ((NT + 1 - p) // 2))

        @block.tensor
        def _(pe):
            def turn_x(i, p, nth):
                pe.wait_ge(x_loaded[p], nth * 16)
                wait(pe, xT_ready, i)
                for k in range(KT):
                    last = pe.transpose(x_turned[:, k * 128:(k + 1) * 128], x[p][:, k * 128:(k + 1) * 128],
                                        cst[:, C_ID:C_ID + 128])
                last.then_inc(xt_ready, 1)

            def product(i, p, out, part, ready, e):
                if part == 0:
                    pe.wait_ge(xT_ready, i + 1)
                wait(pe, hid_ready, i - 1)
                for k in range(KT):
                    at = (part * KT + k) * HID
                    last = pe.matmul(out[p][:], xT[p][:, k], W[:, ds(e, 1), at:at + HID],
                                     start=(k == 0), stop=(k == KT - 1))
                last.then_inc(ready, 1)

            def turn_hidden(i, p):
                pe.wait_ge(hid_ready, i + 1)
                wait(pe, hidT_ready, i)
                for h in range(HT):
                    last = pe.transpose(h_turned[:, h * 128:(h + 1) * 128], hid[p][:, h * 128:(h + 1) * 128],
                                        cst[:, C_ID:C_ID + 128])
                last.then_inc(ht_ready, 1)

            def down(i, p, e):
                pe.wait_ge(hidT_ready, i + 1)
                wait(pe, y_ready, i - 1)
                for h in range(HT):
                    at = 2 * KT * HID + h * D
                    last = pe.matmul(y_ps[p][:, 0:D], hidT[p][:, h], W[:, ds(e, 1), at:at + D],
                                     start=(h == 0), stop=(h == HT - 1))
                last.then_inc(down_ready, 1)

            expert = lambda i: pe.value_load(tile_expert[0:1, ds(i, 1)], min_val=0, max_val=E0 - 1)

            def body(i, p, nth):
                e = expert(i)
                if inside(i, NT - 1):
                    e_next = expert(i + 1)
                    product(i + 1, 1 - p, gate, 0, gate_ready, e_next)
                turn_hidden(i, p)
                if inside(i, NT - 1):
                    product(i + 1, 1 - p, up, 1, up_ready, e_next)
                if inside(i, NT - 2):
                    turn_x(i + 2, p, nth + 1)
                down(i, p, e)

            pe.wait_ge(w_loaded, 16 * (E0 - first_late))
            turn_x(0, 0, 1)
            turn_x(1, 1, 1)
            e0 = expert(0)
            product(0, 0, gate, 0, gate_ready, e0)
            product(0, 0, up, 1, up_ready, e0)
            over(pe, body)

        @block.scalar
        def _(act):
            def body(i, p, nth):
                act.wait_ge(gate_ready, i + 1)
                wait(act, hid_ready, i - 1)
                act.activation(act_g[p][:], gate[p][:], ACT.Silu).then_inc(silu_ready, 1)
                act.wait_ge(ht_ready, i + 1)
                wait(act, down_ready, i - 1)
                act.copy(hidT[p][:].rearrange("p h t -> p (h t)"), h_turned[:]).then_inc(hidT_ready, 1)
            over(act, body)

        @block.vector
        def _(dve):
            def keep_x(i, p):
                dve.wait_ge(xt_ready, i + 1)
                wait(dve, up_ready, i - 1)
                dve.tensor_copy(xT[p][:].rearrange("p k t -> p (k t)"), x_turned[:, 0:D]).then_inc(xT_ready, 1)

            def body(i, p, nth):
                dve.wait_ge(silu_ready, i + 1)
                dve.wait_ge(up_ready, i + 1)
                wait(dve, ht_ready, i - 1)
                dve.tensor_tensor(hid[p][:], act_g[p][:], up[p][:], ALU.mult).then_inc(hid_ready, 1)
                if inside(i, NT - 2):
                    keep_x(i + 2, p)
                dve.wait_ge(down_ready, i + 1)
                wait(dve, y_stored[p], (nth - 1) * 16)
                dve.tensor_scalar(y[p][:], y_ps[p][:, 0:D], 1.0, None, ALU.mult).then_inc(y_ready, 1)
            keep_x(0, 0)
            keep_x(1, 1)
            over(dve, body)


def combine(nc, X, yg_dram, slots, slot_weight):
    GROUP = 8
    with ExitStack() as ctx:
        picked = ctx.enter_context(nc.sbuf_tensor("m_picked", [128, 2 * B, D], F32))
        gathered = [ctx.enter_context(nc.semaphore(f"m_gathered{g}")) for g in range(2 * B // GROUP)]
        block = ctx.enter_context(nc.Block())

        @block.gpsimd
        def _(pool):
            for n in range(2 * B):
                s, k = n // 2, n % 2
                pool.indirect_dma_start(picked[:, n, :], None, yg_dram,
                                        bass.IndirectOffsetOnAxis(ap=slots[:, k, s:s + 1], axis=0)
                                        ).then_inc(gathered[n // GROUP], 16)

        @block.vector
        def _(dve):
            for g in range(2 * B // GROUP):
                dve.wait_ge(gathered[g], 16 * GROUP)
                for k in range(2):
                    for n in range(g * GROUP + k, (g + 1) * GROUP, 2):
                        s = n // 2
                        dve.scalar_tensor_tensor(X[:, s, :], picked[:, n, :], slot_weight[:, s, k:k + 1], X[:, s, :],
                                                 ALU.mult, ALU.add)
                    dve.drain()


def route1(nc, XNT, rw_dram, bias_dram, cst, comb_dram):
    with ExitStack() as ctx:
        sb = lambda n, s, d=F32: ctx.enter_context(nc.sbuf_tensor("r1_" + n, s, d))
        sem = lambda n: ctx.enter_context(nc.semaphore("r1_" + n))
        rw = sb("rw", [128, KT, E1])
        eb = sb("eb", [128, E1])
        sg, sbias, cur, oh, sel = (sb(n, [128, B, E1]) for n in ("sg", "sbias", "cur", "oh", "sel"))
        comb = sb("comb", [128, E1, B])
        combT = sb("combT", [128, 2, 128])
        g1, g2, gs, goh, gsel, gtmp = (sb(n, [128, B, G1]) for n in ("g1", "g2", "gs", "goh", "gsel", "gtmp"))
        one = sb("one", [128, B, 1])
        one2 = sb("one2", [128, B, 1])
        ps = ctx.enter_context(nc.psum_tensor("r1_ps", [128, 512], F32))
        ps2 = ctx.enter_context(nc.psum_tensor("r1_ps2", [128, 512], F32))
        loaded, logits_ready, sig_ready, comb_ready = sem("loaded"), sem("logits_ready"), sem("sig_ready"), sem("comb_ready")
        turned_ready, combT_ready, stored = sem("turned_ready"), sem("combT_ready"), sem("stored")
        block = ctx.enter_context(nc.Block())

        @block.sync
        def _(sp):
            sp.dma_start(rw[:], rw_dram).then_inc(loaded, 16)
            sp.dma_start(eb[:], bias_dram.rearrange("(o n) -> o n", o=1).broadcast_to([128, E1])).then_inc(loaded, 16)
            sp.wait_ge(loaded, 32)
            sp.wait_ge(combT_ready, 1)
            sp.dma_start(comb_dram.rearrange("(x e) (s t) -> (e s) x t", x=2, s=B), combT[:]).then_inc(stored, 16)
            sp.wait_ge(stored, 16)

        @block.tensor
        def _(pe):
            pe.wait_ge(loaded, 32)
            for s in range(B):
                for k in range(KT):
                    last = pe.matmul(ps[:, s * E1:(s + 1) * E1], XNT[:, k, s * 128:(s + 1) * 128], rw[:, k],
                                     start=(k == 0), stop=(k == KT - 1))
            last.then_inc(logits_ready, 1)
            pe.wait_ge(comb_ready, 1)
            for x in range(2):
                last = pe.transpose(ps2[:, x * 128:(x + 1) * 128],
                                    comb[:, 8 * x:8 * x + 8, :].rearrange("p e s -> p (e s)"),
                                    cst[:, C_ID:C_ID + 128])
            last.then_inc(turned_ready, 1)

        @block.scalar
        def _(act):
            act.wait_ge(logits_ready, 1)
            act.activation(sg[:].rearrange("p s e -> p (s e)"), ps[:, 0:B * E1], ACT.Sigmoid).then_inc(sig_ready, 1)

        @block.vector
        def _(dve):
            dve.wait_ge(loaded, 32)
            dve.wait_ge(sig_ready, 1)
            in_groups = lambda a: a[:].rearrange("p s (g e) -> p s g e", g=G1)
            whole = lambda a: a[:].rearrange("p s (o e) -> p s o e", o=1)
            flat = lambda a: a[:].rearrange("p s e -> p (s e)")
            gshape, wshape, groups = [128, B, G1, EPG], [128, B, 1, E1], [128, B, 1, G1]
            rev = lambda n, sh: cst[:, C_REV:C_REV + n].rearrange("p (a b e) -> p a b e", a=1, b=1).broadcast_to(sh)
            dve.tensor_tensor(sbias[:], sg[:], eb[:].rearrange("p (o e) -> p o e", o=1).broadcast_to([128, B, E1]),
                              ALU.add)
            dve.drain()
            dve.tensor_reduce(g1[:], in_groups(sbias), AX.X, ALU.max)
            top1(dve, in_groups(sbias), in_groups(oh), gtmp[:], rev(EPG, gshape), gshape)
            dve.scalar_tensor_tensor(flat(cur), flat(oh), -BIG, flat(sbias), ALU.mult, ALU.add)
            dve.drain()
            dve.tensor_reduce(g2[:], in_groups(cur), AX.X, ALU.max)
            dve.drain()
            dve.tensor_tensor(gs[:], g1[:], g2[:], ALU.add)
            dve.drain()
            top1(dve, whole(gs), whole(gsel), one[:], rev(G1, groups), groups)
            dve.scalar_tensor_tensor(flat(gs), flat(gsel), -BIG, flat(gs), ALU.mult, ALU.add)
            dve.drain()
            top1(dve, whole(gs), whole(goh), one[:], rev(G1, groups), groups)
            dve.tensor_tensor(gsel[:], gsel[:], goh[:], ALU.add)
            dve.drain()
            dve.tensor_scalar(gs[:], gsel[:], 1.0, BIG, ALU.subtract, ALU.mult)
            dve.drain()
            dve.tensor_tensor(in_groups(cur), in_groups(sbias),
                              gs[:].rearrange("p s (g o) -> p s g o", o=1).broadcast_to(gshape), ALU.add)
            dve.drain()
            for n in range(4):
                dst = sel if n == 0 else oh
                top1(dve, whole(cur), whole(dst), one[:], rev(E1, wshape), wshape)
                if n < 3:
                    dve.scalar_tensor_tensor(flat(cur), flat(dst), -BIG, flat(cur), ALU.mult, ALU.add)
                if n > 0:
                    dve.tensor_tensor(sel[:], sel[:], oh[:], ALU.add)
                dve.drain()
            dve.tensor_tensor(sel[:], sel[:], sg[:], ALU.mult)
            dve.drain()
            dve.tensor_reduce(one[:], whole(sel), AX.X, ALU.add)
            dve.drain()
            dve.tensor_scalar(one2[:], one[:], 1e-20, None, ALU.add)
            dve.drain()
            dve.reciprocal(one[:], one2[:])
            dve.drain()
            dve.tensor_tensor(comb[:].rearrange("p e s -> p s e"), sel[:], one[:].broadcast_to([128, B, E1]),
                              ALU.mult).then_inc(comb_ready, 1)
            dve.wait_ge(turned_ready, 1)
            dve.tensor_copy(combT[:].rearrange("p x t -> p (x t)"), ps2[:, 0:256]).then_inc(combT_ready, 1)


class BesideShared:

    def __init__(self, ctx, nc, XN, W, w_dram, first_late, under_tokens, xg_dram, slots):
        self.XN, self.W, self.w_dram, self.first_late, self.under_tokens = XN, W, w_dram, first_late, under_tokens
        self.xg_dram, self.slots = xg_dram, slots
        self.scattered = ctx.enter_context(nc.semaphore("e_scattered"))
        self.w_loaded = ctx.enter_context(nc.semaphore("e_w_loaded"))

    def pool(self, pool):
        for s in range(B):
            for k in range(2):
                pool.indirect_dma_start(self.xg_dram, bass.IndirectOffsetOnAxis(ap=self.slots[:, k, s:s + 1], axis=0),
                                        self.XN[:, s, :], None).then_inc(self.scattered, 16)
        pool.wait_ge(self.scattered, 16 * 2 * B)

    def sync(self, sp):
        for e in range(self.under_tokens, self.first_late):
            sp.dma_start(self.W[:, e, :], self.w_dram[NSH0 + e]).then_inc(self.w_loaded, 16)
        sp.wait_ge(self.scattered, 16 * 2 * B)
        for e in range(self.under_tokens):
            sp.dma_start(self.W[:, e, :], self.w_dram[NSH0 + e]).then_inc(self.w_loaded, 16)
        sp.wait_ge(self.w_loaded, 16 * self.first_late)


def feed_forward(nc, tag, X, XNT, w_dram, nblocks, tanh_col, comb_dram, one, place=None, extra=None):
    with ExitStack() as ctx:
        sb = lambda n, s, d=F32: ctx.enter_context(nc.sbuf_tensor(tag + n, s, d))
        sem = lambda n: ctx.enter_context(nc.semaphore(tag + n))
        pb = lambda n: ctx.enter_context(nc.psum_tensor(tag + n, [128, 512], F32))
        WN = 6 * HID
        xhi = sb("xhi", [128, KT, T], F32R)
        xlo = sb("xlo", [128, KT, T], F32R)
        plain = place if place is not None else sb("plain", [128, WN + 4 * 512])
        raw = plain[:, 0:WN]
        whi = [sb(f"whi{p}", [128, WN], F32R) for p in range(2)]
        wlo = [sb(f"wlo{p}", [128, WN], F32R) for p in range(2)]
        act_g = [plain[:, WN + p * 512:WN + (p + 1) * 512] for p in range(2)]
        hid = [plain[:, WN + (2 + p) * 512:WN + (3 + p) * 512] for p in range(2)]
        hhi = [sb(f"hhi{p}", [128, 512], F32R) for p in range(2)]
        hlo = [sb(f"hlo{p}", [128, 512], F32R) for p in range(2)]
        cb = sb("cb", [128, HT, 512]) if comb_dram is not None else None
        gate = [pb(f"gate{p}") for p in range(2)]
        up = [pb(f"up{p}") for p in range(2)]
        y = [[pb(f"y{p}{j}") for j in range(2)] for p in range(2)]
        x_ready, w_loaded, w_split, w_used = sem("x_ready"), sem("w_loaded"), sem("w_split"), sem("w_used")
        whi_ready = sem("whi_ready")
        gu_ready, gu_free, silu_ready = sem("gu_ready"), sem("gu_free"), sem("silu_ready")
        hid_ready, hhi_ready, hlo_ready = sem("hid_ready"), sem("hhi_ready"), sem("hlo_ready")
        h_used, y_ready, y_free = sem("h_used"), sem("y_ready"), sem("y_free")
        cb_loaded, cb_used, xh_ready = sem("cb_loaded"), sem("cb_used"), sem("xh_ready")
        block = ctx.enter_context(nc.Block())
        gate_cols = lambda k, ht: slice(k * HID + ht * 128, k * HID + (ht + 1) * 128)
        up_cols = lambda k, ht: slice((KT + k) * HID + ht * 128, (KT + k) * HID + (ht + 1) * 128)
        down_cols = lambda ht: slice(2 * KT * HID + ht * D, 2 * KT * HID + (ht + 1) * D)

        def over_blocks(eng, body):
            pairs = nblocks // 2
            if pairs > 1:
                with eng.Fori(0, pairs) as i:
                    for p in range(2):
                        body(i * 2 + p, p)
                done = 2 * pairs
            else:
                done = 0
            for b in range(done, nblocks):
                body(b, b % 2)

        @block.sync
        def _(sp):
            def load(b, p):
                sp.wait_ge(w_split, b + 1)
                src = w_dram[ds(b, 1)].rearrange("o p n -> (o p) n")
                sp.dma_start(raw, src).then_inc(w_loaded, 16)
                if comb_dram is not None and b >= 1:
                    with sp.Fori(0, NCH) as c:
                        sp.wait_ge(cb_used, c + NCH * (b - 1) + 1)
                        for half in range(2):
                            e0 = (b - 1) * EPB + half
                            rows = comb_dram.rearrange("(o ht two) t -> o ht two t", o=1, two=2)[
                                :, (b - 1) * HT:b * HT, half, ds(c * 512, 512)]
                            sp.dma_start(cb[64 * half:64 * half + 64], rows.broadcast_to([64, HT, 512])
                                         ).then_inc(cb_loaded, 16)
            over_blocks(sp, load)
            if extra is not None:
                extra.sync(sp)

        @block.gpsimd
        def _(pool):
            pool.sem_inc(w_split, 1)
            def split(b, p):
                pool.wait_ge(w_loaded, b * 16 + 16)
                pool.wait_ge(w_used, b + 1)
                pool.tensor_tensor(whi[p][:], raw, one.broadcast_to([128, WN]), ALU.mult)
                pool.drain()
                pool.tensor_tensor(wlo[p][:], raw, whi[p][:].bitcast(F32), ALU.subtract).then_inc(w_split, 1)
            over_blocks(pool, split)
            if extra is not None:
                extra.pool(pool)

        @block.tensor
        def _(pe):
            pe.sem_inc(w_used, 2)
            pe.sem_inc(h_used, 2)
            pe.wait_ge(x_ready, 1)

            def chunk(b, p, c):
                n = b * NCH + c
                u0 = n * HT

                def gate_up(ht, q):
                    pe.wait_ge(gu_free, u0 + ht + 1)
                    for out, cols in ((gate, gate_cols), (up, up_cols)):
                        m = 0
                        for k in range(KT):
                            for w, x in ((whi, xhi), (whi, xlo), (wlo, xhi)):
                                last = pe.matmul(out[q][:], w[p][:, cols(k, ht)], x[:, k, ds(c * 512, 512)],
                                                 start=(m == 0), stop=(m == 3 * KT - 1))
                                m += 1
                    last.then_inc(gu_ready, 1)

                def down(ht, q):
                    pe.wait_ge(hhi_ready, u0 + ht + 1)
                    if ht == 0:
                        pe.wait_ge(y_free, n + 1)
                    for part in range(2):
                        if part == 1:
                            pe.wait_ge(hlo_ready, u0 + ht + 1)
                        for j in range(CH):
                            for w in ((whi, wlo) if part == 0 else (whi,)):
                                h = hhi if part == 0 else hlo
                                first = ht == 0 and part == 0 and w is whi and j % 2 == 0
                                last = pe.matmul(y[p][j // 2][:, (j % 2) * D:(j % 2 + 1) * D],
                                                 h[q][:, j * 128:(j + 1) * 128], w[p][:, down_cols(ht)],
                                                 start=first, stop=(ht == HT - 1 and part == 1),
                                                 skip_group_check=True)
                    last.then_inc(h_used, 1)

                pe.wait_ge(w_split, b + 1 + 1)
                gate_up(0, 0)
                for ht in range(1, HT):
                    gate_up(ht, ht % 2)
                    down(ht - 1, (ht - 1) % 2)
                down(HT - 1, (HT - 1) % 2)

            def one_block(b, p):
                with pe.Fori(0, NCH) as c:
                    chunk(b, p, c)
                pe.drain().then_inc(w_used, 1)
            over_blocks(pe, one_block)

        @block.scalar
        def _(act):
            with act.Fori(0, NCH) as c:
                act.copy(xhi[:, :, ds(c * 512, 512)], XNT[:, :, ds(c * 512, 512)]).then_inc(xh_ready, 1)

            def one_block(b, p):
                with act.Fori(0, NCH) as c:
                    for ht in range(HT):
                        q = ht % 2
                        u = (b * NCH + c) * HT + ht
                        act.wait_ge(gu_ready, u + 1)
                        act.activation(act_g[q], gate[q][:], ACT.Silu).then_inc(silu_ready, 1)
                        act.wait_ge(hid_ready, u + 1)
                        act.wait_ge(h_used, u + 1)
                        act.copy(hhi[q][:], hid[q]).then_inc(hhi_ready, 1)
            over_blocks(act, one_block)

        @block.vector
        def _(dve):
            dve.sem_inc(cb_used, 1)
            dve.sem_inc(gu_free, 2)
            dve.sem_inc(y_free, 1)
            dve.wait_ge(xh_ready, NCH)
            dve.tensor_tensor(xlo[:], XNT[:], xhi[:].bitcast(F32), ALU.subtract).then_inc(x_ready, 1)

            def one_block(b, p):
                with dve.Fori(0, NCH) as c:
                    n = b * NCH + c
                    for ht in range(HT):
                        q = ht % 2
                        u = n * HT + ht
                        dve.wait_ge(silu_ready, u + 1)
                        dve.tensor_tensor(hid[q], act_g[q], up[q][:], ALU.mult).then_inc(gu_free, 1)
                        if comb_dram is not None and b >= 1:
                            dve.drain()
                            if ht == 0:
                                dve.wait_ge(cb_loaded, (n - NCH) * 32 + 32)
                            last = dve.tensor_tensor(hid[q], hid[q], cb[:, ht], ALU.mult)
                            if ht == HT - 1:
                                last.then_inc(cb_used, 1)
                        dve.drain().then_inc(hid_ready, 1)
                        dve.wait_ge(hhi_ready, u + 1)
                        dve.tensor_tensor(hlo[q][:], hid[q], hhi[q][:].bitcast(F32), ALU.subtract
                                          ).then_inc(hlo_ready, 1)
                    dve.wait_ge(h_used, (n + 1) * HT + 2)
                    for j in range(CH):
                        xs = X[:, ds(c * CH + j, 1), :].rearrange("p o d -> p (o d)")
                        last = dve.scalar_tensor_tensor(xs, y[p][j // 2][:, (j % 2) * D:(j % 2 + 1) * D], tanh_col, xs,
                                                        ALU.mult, ALU.add)
                    last.then_inc(y_free, 1)
            over_blocks(dve, one_block)


def program(nc, x, ctx_in, ctxT, mask, consts, g_xattn, g_ffn, wg, bg_i, bg_f, ln_scale, rw0, eb0, w0,
            wqkv, bqk, bv, rw1, eb1, w1, out):
    m_dram = nc.dram_tensor("m_rows", (128, 128), F32, kind="Internal").ap()
    xg_dram = nc.dram_tensor("slot_tokens", (NT * 128, D), F32, kind="Internal").ap()
    yg_dram = nc.dram_tensor("slot_outputs", (NT * 128, D), F32, kind="Internal").ap()
    comb_dram = nc.dram_tensor("comb_rows", (E1, T), F32, kind="Internal").ap()
    with ExitStack() as ctx:
        sb = lambda n, s, d=F32: ctx.enter_context(nc.sbuf_tensor(n, s, d))
        X = sb("X", [128, B, D])
        cst = sb("cst", [128, C_END])
        g_in = sb("g_in", [128, 4])
        g_tanh = sb("g_tanh", [128, 4])
        lns = sb("lns", [128, D])
        ln_tanh = sb("ln_tanh", [128, D])
        zeros = sb("zeros", [128, D])

        zeroed = ctx.enter_context(nc.semaphore("p_zeroed"))
        slots_zeroed = ctx.enter_context(nc.semaphore("p_slots_zeroed"))
        with nc.semaphore("p_loaded") as loaded, nc.semaphore("p_tanh") as tanh_ready, nc.Block() as block:
            @block.gpsimd
            def _(pool):
                pool.memset(zeros[:], 0.0).then_inc(zeroed, 1)

            @block.sync
            def _(sp):
                sp.dma_start(X[:], x.rearrange("b p d -> p b d")).then_inc(loaded, 16)
                sp.dma_start(cst[:], consts).then_inc(loaded, 16)
                sp.dma_start(g_in[:, 0:2], g_xattn.rearrange("(o n) -> o n", o=1).broadcast_to([128, 2])).then_inc(loaded, 16)
                sp.dma_start(g_in[:, 2:4], g_ffn.rearrange("(o n) -> o n", o=1).broadcast_to([128, 2])).then_inc(loaded, 16)
                sp.wait_ge(zeroed, 1)
                sp.dma_start(xg_dram.rearrange("(i p) d -> p i d", p=128),
                             zeros[:].rearrange("p (o d) -> p o d", o=1).broadcast_to([128, NT, D])
                             ).then_inc(slots_zeroed, 16)
                sp.dma_start(lns[:], ln_scale.rearrange("(o n) -> o n", o=1).broadcast_to([128, D])).then_inc(loaded, 16)
                sp.wait_ge(loaded, 80)
                sp.wait_ge(slots_zeroed, 16)

            @block.scalar
            def _(act):
                act.wait_ge(loaded, 80)
                act.activation(g_tanh[:], g_in[:], ACT.Tanh).then_inc(tanh_ready, 1)

            @block.vector
            def _(dve):
                dve.wait_ge(loaded, 80)
                dve.wait_ge(tanh_ready, 1)
                dve.tensor_scalar(ln_tanh[:], lns[:], g_tanh[:, 0:1], None, ALU.mult)

        with ExitStack() as ctx0:
            sb0 = lambda n, s, d=F32: ctx0.enter_context(nc.sbuf_tensor(n, s, d))
            XNT, AT, ET = sb0("XNT0", [128, KT, T]), sb0("AT", [128, 128]), sb0("ET", [128, 128])
            norm_transpose(nc, "n0_", X, XNT, cst)
            with (nc.sbuf_tensor("ctxT_all", [128, KT, T], F32) as ctxT_all,
                  nc.sbuf_tensor("wg_sb", [128, 3 * KT, 16], F32) as wg_sb,
                  nc.sbuf_tensor("bg_sb", [128, 16], F32) as bg_sb):
                def run_loads(sp, loaded):
                    sp.dma_start(ctxT_all[:], ctxT).then_inc(loaded, 16)
                    sp.dma_start(wg_sb[:], wg).then_inc(loaded, 16)
                    sp.dma_start(bg_sb[:, 0:8], bg_i.rearrange("(o n) -> o n", o=1).broadcast_to([128, 8])).then_inc(loaded, 16)
                    sp.dma_start(bg_sb[:, 8:16], bg_f.rearrange("(o n) -> o n", o=1).broadcast_to([128, 8])).then_inc(loaded, 16)
                    return 4
                gates(nc, XNT, ctxT_all, cst, wg_sb, bg_sb, AT[:], ET[:], m_dram, run_loads)
            cell(nc, X, XNT, ctxT, ctx_in, m_dram, cst, AT, ET, ln_tanh[:])

        with ExitStack() as ctx1:
            W = ctx1.enter_context(nc.sbuf_tensor("W", [128, E0, 6 * HID], F32))
            slots = ctx1.enter_context(nc.sbuf_tensor("slots", [128, 2, B], U32))
            slot_weight = ctx1.enter_context(nc.sbuf_tensor("slot_weight", [128, B, 2], F32))
            tile_expert = ctx1.enter_context(nc.sbuf_tensor("tile_expert", [1, NT], I32))
            under_tokens, first_late = 2, 5
            head = W[:, 0:under_tokens, :].rearrange("p e n -> p (e n)")
            tail = W[:, first_late:E0, :].rearrange("p e n -> p (e n)")
            XN = head[:, 0:B * D].rearrange("p (s d) -> p s d", s=B)
            XNT = tail[:, 0:KT * T].rearrange("p (k t) -> p k t", k=KT)
            norm_transpose(nc, "n1_", X, XNT, cst, XN)
            route0(nc, XNT, rw0, eb0, cst, slots, slot_weight, tile_expert, g_tanh[:, 2:3])
            beside = BesideShared(ctx1, nc, XN, W, w0, first_late, under_tokens, xg_dram, slots)
            feed_forward(nc, "f0_", X, XNT, w0, NSH0, g_tanh[:, 2:3], None, cst[:, C_ONE:C_ONE + 1],
                         place=tail[:, KT * T:], extra=beside)
            routed_tiles(nc, W, w0, first_late, xg_dram, yg_dram, tile_expert, cst)
            combine(nc, X, yg_dram, slots, slot_weight)

        with nc.sbuf_tensor("XNT1", [128, KT, T], F32) as XNT:
            norm_transpose(nc, "n2_", X, XNT, cst)
            attention(nc, X, XNT, ctxT, mask, wqkv, bqk, bv, cst, g_tanh[:, 1:2])
            norm_transpose(nc, "n3_", X, XNT, cst)
            route1(nc, XNT, rw1, eb1, cst, comb_dram)
            feed_forward(nc, "f1_", X, XNT, w1, NB1, g_tanh[:, 3:4], comb_dram, cst[:, C_ONE:C_ONE + 1])

        with nc.semaphore("stored") as stored, nc.Block() as block:
            @block.sync
            def _(sp):
                sp.dma_start(out.rearrange("b p d -> p b d"), X[:]).then_inc(stored, 16)
                sp.wait_ge(stored, 16)


def constants():
    c = np.zeros((128, C_END), np.float32)
    p = np.arange(128)
    c[:, C_ID:C_ID + 128] = np.eye(128)
    c[:, C_PEN:C_PEN + 128] = np.where(p[None, :] >= p[:, None], 0.0, BIG)
    c[:, C_BD0:C_BD0 + 4] = p[:, None] // DH0 == np.arange(4)
    c[:, C_BD1:C_BD1 + 8] = p[:, None] // DH1 == np.arange(8)
    c[:, C_REV:C_REV + 16] = 16 - np.arange(16)
    c[:, C_EPS] = LN_EPS
    c[:, C_ONE] = 1.0
    c[:, C_TRI:C_TRI + 128] = p[:, None] < p[None, :]
    c[:, C_ONES:C_ONES + 128] = 1.0
    c[:, C_KEEP:C_KEEP + 128] = p[None, :] % B != 0
    c[:, C_STEP:C_STEP + B] = 128 * np.arange(B)
    c[:, C_TILE:C_TILE + NT] = np.arange(NT)
    c[:, C_LNR] = math.log(ROOT0)
    return c


def kernel(**inputs):
    import numpy as _np
    import concourse.bacc as _bacc
    from concourse import mybir as _mybir
    from concourse.bass_utils import run_bass_kernel_spmd as _run

    a = {k: _np.asarray(v) for k, v in inputs.items()}

    def rows(m):
        return m.reshape(-1, 128, m.shape[-1]).transpose(1, 0, 2)

    def ffn_block(gate, up, down):
        return _np.concatenate([rows(m).reshape(128, -1) for m in (gate, up, down)], axis=1)

    ctx_in = a["ctx_1024"]
    gate_w = _np.concatenate([a["L0_xattn_igate_w"], a["L0_xattn_fgate_w"]], axis=0)
    w0 = [ffn_block(a["L0_ffn_sw1"][i].T, a["L0_ffn_sw3"][i].T, a["L0_ffn_sw2"][i].T) for i in range(NSH0)]
    w0 += [ffn_block(a["L0_ffn_w1"][i].T, a["L0_ffn_w3"][i].T, a["L0_ffn_w2"][i].T) for i in range(E0)]
    w1 = [ffn_block(a["L1_ffn_shared_gate_w"].T, a["L1_ffn_shared_up_w"].T, a["L1_ffn_shared_down_w"].T)]
    for b in range(NB1 - 1):
        e = slice(b * EPB, (b + 1) * EPB)
        w1.append(ffn_block(a["L1_ffn_gate_w"][e].transpose(1, 0, 2).reshape(D, HID),
                            a["L1_ffn_up_w"][e].transpose(1, 0, 2).reshape(D, HID),
                            a["L1_ffn_down_w"][e].reshape(HID, D)))
    wqkv = _np.stack([rows(a["L1_xattn_" + n].T) for n in ("Wq", "Wk", "Wv")])
    bqk = _np.stack([a["L1_xattn_" + n].reshape(KT, 128).T for n in ("bq", "bk")], axis=1)
    feeds = [
        ("x", a["x"]), ("ctx_in", ctx_in), ("ctxT", rows(ctx_in.reshape(T, D).T)), ("mask", a["mask_BxSxS2_ff1"]),
        ("consts", constants()), ("g_xattn", a["g_xattn"]), ("g_ffn", a["g_ffn"]), ("wg", rows(gate_w.T)),
        ("bg_i", a["L0_xattn_igate_b"]), ("bg_f", a["L0_xattn_fgate_b"]), ("ln_scale", a["L0_xattn_ln_scale"]),
        ("rw0", rows(a["L0_ffn_router_w"].T)), ("eb0", a["L0_ffn_expert_bias"]), ("w0", _np.stack(w0)),
        ("wqkv", wqkv), ("bqk", bqk), ("bv", a["L1_xattn_bv"]),
        ("rw1", rows(a["L1_ffn_router_w"].T)), ("eb1", a["L1_ffn_correction_bias"]), ("w1", _np.stack(w1)),
    ]
    nc = _bacc.Bacc("TRN2", target_bir_lowering=False, num_devices=1)
    arrays, args = {}, []
    for name, v in feeds:
        v = _np.ascontiguousarray(v)
        arrays[f"in_{name}_dram"] = v
        args.append(nc.dram_tensor(f"in_{name}_dram", v.shape, _mybir.dt.from_np(v.dtype), kind="ExternalInput").ap())
    args.append(nc.dram_tensor("out_0_dram", (B, S, D), _mybir.dt.float32, kind="ExternalOutput").ap())
    program(nc, *args)
    r = _run(nc, [arrays], core_ids=[0])
    return r.results[0]["out_0_dram"]
```

```python
from contextlib import ExitStack
import math
import numpy as np
import concourse.bass as bass
from concourse import mybir

F32 = mybir.dt.float32
F32R = mybir.dt.float32r
U32 = mybir.dt.uint32
I32 = mybir.dt.int32
ALU = mybir.AluOpType
ACT = mybir.ActivationFunctionType
AX = mybir.AxisListType
ds = bass.ds

B, S, D = 16, 128, 256
KT = D // 128
T = B * S
CH = 4
NCH = B // CH
NH0, DH0 = 8, 32
NH1, DH1 = 16, 16
HID = 512
HT = HID // 128
E0, NSH0 = 8, 2
NB0 = E0 + NSH0
E1, H1 = 16, 64
EPB = HID // H1
NB1 = 1 + E1 // EPB
G1 = 4
EPG = E1 // G1
LN_EPS = 1e-5
CELL_EPS = 1e-6
ROOT0 = math.sqrt(DH0)
BIG = 1e30

WN = 6 * HID

NT = 2 * T // 128 + E0 - 1
_cols, C = 0, {}
for _name, _n in (("ID", 128), ("PEN", 128), ("BD0", 4), ("BD1", 8), ("REV", 16), ("EPS", 1), ("LNR", 1), ("ONE", 1),
                  ("TRI", 128), ("ONES", 128), ("KEEP", 128), ("STEP", B), ("TILE", NT)):
    C[_name] = _cols
    _cols += _n
C_ID, C_PEN, C_BD0, C_BD1, C_REV, C_EPS, C_LNR, C_ONE, C_TRI, C_ONES, C_KEEP, C_STEP, C_TILE = C.values()
C_END = _cols


def norm_transpose(nc, tag, X, XNT, cst, XN=None, halves=None, beside=None,
                   products=None):
    half = CH // 2
    with ExitStack() as ctx:
        sb = lambda n, s, d=F32: ctx.enter_context(nc.sbuf_tensor(tag + n, s, d))
        sem = lambda n: ctx.enter_context(nc.semaphore(tag + n))
        stats = sb("stats", [128, B, 6])
        mean_var = sb("mean_var", [128, B, 2])
        std = sb("std", [128, B])
        rstd = sb("rstd", [128, B])
        shift = sb("shift", [128, B])
        xn = XN if XN is not None else sb("xn", [128, B, D])
        turned = [[ctx.enter_context(nc.psum_tensor(f"{tag}tp{p}{k}", [128, 512], F32)) for k in range(KT)]
                  for p in range(2)]
        var_ready, std_ready, rstd_ready = sem("var_ready"), sem("std_ready"), sem("rstd_ready")
        xn_dve, xn_act = sem("xn_dve"), sem("xn_act")
        turned_ready, hi_ready, turned_free = sem("turned_ready"), sem("hi_ready"), sem("turned_free")
        block = ctx.enter_context(nc.Block())

        if beside is not None:
            @block.sync
            def _(sp):
                beside.sync(sp)

            @block.gpsimd
            def _(pool):
                beside.pool(pool)

        @block.vector
        def _(dve):
            def finish(c):
                dve.wait_ge(std_ready, c + 1)
                dve.reciprocal(rstd[:, c * CH:(c + 1) * CH], std[:, c * CH:(c + 1) * CH])
                dve.drain()
                dve.scalar_tensor_tensor(shift[:, c * CH:(c + 1) * CH], mean_var[:, c * CH:(c + 1) * CH, 0], -1.0,
                                         rstd[:, c * CH:(c + 1) * CH], ALU.mult, ALU.mult).then_inc(rstd_ready, 1)
                for s in range(c * CH, c * CH + half):
                    last = dve.tensor_scalar(xn[:, s, :], X[:, s, :], mean_var[:, s, 0:1], rstd[:, s:s + 1],
                                             ALU.subtract, ALU.mult)
                last.then_inc(xn_dve, 1)

            def low_halves(c):
                dve.wait_ge(hi_ready, c + 1)
                for k in range(KT):
                    last = dve.tensor_tensor(halves[1][:, k, c * 512:(c + 1) * 512], turned[c % 2][k][:],
                                             halves[0][:, k, c * 512:(c + 1) * 512].bitcast(F32), ALU.subtract)
                last.then_inc(turned_free, 1)

            for c in range(NCH + 1):
                if c < NCH:
                    for s in range(c * CH, (c + 1) * CH):
                        dve.bn_stats(stats[:, s, :], X[:, s, :])
                    dve.drain()
                    for s in range(c * CH, (c + 1) * CH):
                        dve.bn_aggr(mean_var[:, s, :], stats[:, s, :])
                    dve.drain().then_inc(var_ready, 1)
                if c >= 1:
                    finish(c - 1)
                if c >= 2 and halves is not None:
                    low_halves(c - 2)
            if halves is not None:
                low_halves(NCH - 1)

        @block.tensor
        def _(pe):
            if products is not None:
                products.before(pe)
            for c in range(NCH + 1):
                if c < NCH:
                    pe.wait_ge(xn_dve, c + 1)
                    pe.wait_ge(xn_act, c + 1)
                    if c >= 2:
                        pe.wait_ge(turned_free, c - 1)
                    for k in range(KT):
                        for j in range(CH):
                            last = pe.transpose(turned[c % 2][k][:, j * 128:(j + 1) * 128],
                                                xn[:, c * CH + j, k * 128:(k + 1) * 128], cst[:, C_ID:C_ID + 128])
                    last.then_inc(turned_ready, 1)
                if c >= 1 and products is not None:
                    pe.wait_ge(turned_free, c)
                    products.chunk(pe, c - 1)

        @block.scalar
        def _(act):
            def normalise(c):
                act.wait_ge(rstd_ready, c + 1)
                for s in range(c * CH + half, (c + 1) * CH):
                    last = act.activation(xn[:, s, :], X[:, s, :], ACT.Identity, bias=shift[:, s:s + 1],
                                          scale=rstd[:, s:s + 1])
                last.then_inc(xn_act, 1)

            def keep(c):
                act.wait_ge(turned_ready, c + 1)
                dst = XNT if halves is None else halves[0]
                for k in range(KT):
                    last = act.copy(dst[:, k, c * 512:(c + 1) * 512], turned[c % 2][k][:])
                last.then_inc(turned_free if halves is None else hi_ready, 1)

            for c in range(NCH + 2):
                if c < NCH:
                    act.wait_ge(var_ready, c + 1)
                    act.activation(std[:, c * CH:(c + 1) * CH], mean_var[:, c * CH:(c + 1) * CH, 1], ACT.Sqrt,
                                   bias=cst[:, C_EPS:C_EPS + 1]).then_inc(std_ready, 1)
                if 1 <= c <= NCH:
                    normalise(c - 1)
                if c >= 2:
                    keep(c - 2)


class RouterLogits:

    def __init__(self, logits, halves, rw, rw_ready):
        self.logits, self.halves, self.rw, self.rw_ready = logits, halves, rw, rw_ready

    def before(self, pe):
        pe.wait_ge(self.rw_ready, 1)

    def chunk(self, pe, c):
        E = self.rw.shape[3]
        hi, lo = self.halves
        for s in range(c * CH, (c + 1) * CH):
            at = 2 * s * E
            for k in range(KT):
                tokens = slice(s * 128, (s + 1) * 128)
                pe.matmul(self.logits[:, at:at + 2 * E], hi[:, k, tokens], self.rw[:, :, k, :],
                          start=(s == 0 and k == 0), stop=False, skip_group_check=True)
                pe.matmul(self.logits[:, at:at + E], lo[:, k, tokens], self.rw[:, 0, k, :],
                          start=False, stop=(k == KT - 1), skip_group_check=True)


class GateProducts:

    def __init__(self, ctx, nc, gate_ps, XNT, ctxT, wg, loaded, blank, blank_ready, xg_dram, slots_blank):
        self.blank, self.blank_ready, self.xg_dram, self.slots_blank = blank, blank_ready, xg_dram, slots_blank
        self.gate_ps, self.XNT, self.ctxT, self.wg, self.loaded = gate_ps, XNT, ctxT, wg, loaded
        self.w_ctx = ctx.enter_context(nc.sbuf_tensor("wg_ctx", [128, KT, 16], F32))
        self.added = ctx.enter_context(nc.semaphore("wg_added"))

    def sync(self, sp):
        sp.wait_ge(self.blank_ready, 1)
        sp.dma_start(self.xg_dram.rearrange("(i p) d -> p i d", p=128), self.blank[:]).then_inc(self.slots_blank, 16)

    def pool(self, pool):
        pool.wait_ge(self.loaded, 16 * 4)
        pool.tensor_tensor(self.w_ctx[:], self.wg[:, KT:2 * KT], self.wg[:, 2 * KT:3 * KT], ALU.add
                           ).then_inc(self.added, 1)

    def products(self, pe, sequences, src, w, first, last):
        for s in sequences:
            for k in range(KT):
                pe.matmul(self.gate_ps[:, s * 16:(s + 1) * 16], src[:, k, s * 128:(s + 1) * 128], w[:, k, :],
                          start=(first and s == 0 and k == 0), stop=(last and k == KT - 1), skip_group_check=True)

    def before(self, pe):
        pe.wait_ge(self.added, 1)
        self.products(pe, range(B), self.ctxT, self.w_ctx, True, False)

    def chunk(self, pe, c):
        self.products(pe, range(c * CH, (c + 1) * CH), self.XNT, self.wg, False, True)


def gates(nc, gate_ps, cst, bg, AT, ET, m_dram):
    with ExitStack() as ctx:
        sb = lambda n, s, d=F32: ctx.enter_context(nc.sbuf_tensor("g_" + n, s, d))
        sem = lambda n: ctx.enter_context(nc.semaphore("g_" + n))
        gate_tok = sb("gate_tok", [128, 2, B, NH0])
        gate_row = sb("gate_row", [128, 2, 128])
        absf, ef, lf, logf, ones = (sb(n, [128, 128]) for n in ("absf", "ef", "lf", "logf", "ones"))
        cs, a_row, m_row, ml, e_row = (sb(n, [128, 128]) for n in ("cs", "a_row", "m_row", "ml", "e_row"))
        row_ps = ctx.enter_context(nc.psum_tensor("g_row", [128, 512], F32))
        tok_ps = ctx.enter_context(nc.psum_tensor("g_tok", [128, 512], F32))
        tok_ready, row_ready = sem("tok_ready"), sem("row_ready")
        abs_ready, ln_ready, max_ready, exp_ready = sem("abs_ready"), sem("ln_ready"), sem("max_ready"), sem("exp_ready")
        back_ready, m_stored, act_chain = sem("back_ready"), sem("m_stored"), sem("act_chain")
        block = ctx.enter_context(nc.Block())

        @block.sync
        def _(sp):
            sp.wait_ge(max_ready, 1)
            sp.dma_start(m_dram, m_row[:]).then_inc(m_stored, 16)
            sp.wait_ge(m_stored, 16)

        @block.tensor
        def _(pe):
            pe.wait_ge(tok_ready, 1)
            for g in range(2):
                last = pe.transpose(row_ps[:, g * 128:(g + 1) * 128],
                                    gate_tok[:, g, :, :].rearrange("p s h -> p (s h)"), cst[:, C_ID:C_ID + 128])
            last.then_inc(row_ready, 1)
            pe.wait_ge(exp_ready, 1)
            pe.transpose(tok_ps[:, 0:128], a_row[:], cst[:, C_ID:C_ID + 128])
            pe.transpose(tok_ps[:, 128:256], e_row[:], cst[:, C_ID:C_ID + 128]).then_inc(back_ready, 1)

        @block.vector
        def _(dve):
            dve.memset(ones[:], 1.0)
            dve.tensor_tensor(gate_tok[:].rearrange("p g s h -> p s g h"),
                              gate_ps[:, 0:256].rearrange("p (s g h) -> p s g h", s=B, g=2),
                              bg[:].rearrange("p (o g h) -> p o g h", o=1, g=2).broadcast_to([128, B, 2, NH0]),
                              ALU.add).then_inc(tok_ready, 1)
            dve.wait_ge(row_ready, 1)
            dve.tensor_copy(gate_row[:].rearrange("p g t -> p (g t)"), row_ps[:, 0:256])
            dve.drain()
            ig, fg = gate_row[:, 0, :], gate_row[:, 1, :]
            dve.scalar_tensor_tensor(absf[:], fg, -1.0, fg, ALU.mult, ALU.max)
            dve.drain().then_inc(abs_ready, 1)
            dve.wait_ge(ln_ready, 1)
            dve.scalar_tensor_tensor(logf[:], fg, 0.0, lf[:], ALU.min, ALU.subtract)
            dve.drain()
            dve.tensor_tensor_scan(cs[:], ones[:], logf[:], 0.0, ALU.mult, ALU.add)
            dve.drain()
            dve.tensor_tensor(a_row[:], ig, cs[:], ALU.subtract)
            dve.drain()
            dve.tensor_tensor_scan(m_row[:], a_row[:], a_row[:], -3e38, ALU.max, ALU.max)
            dve.drain()
            dve.tensor_tensor(ml[:], cs[:], m_row[:], ALU.add)
            dve.drain().then_inc(max_ready, 1)
            dve.wait_ge(back_ready, 1)
            dve.tensor_copy(AT, tok_ps[:, 0:128])
            dve.tensor_scalar(ET, tok_ps[:, 128:256], CELL_EPS * ROOT0, None, ALU.add)

        @block.scalar
        def _(act):
            act.wait_ge(abs_ready, 1)
            act.activation(ef[:], absf[:], ACT.Exp, scale=-1.0).then_inc(act_chain, 1)
            act.wait_ge(act_chain, 1)
            act.activation(lf[:], ef[:], ACT.Ln, bias=1.0).then_inc(ln_ready, 1)
            act.wait_ge(max_ready, 1)
            act.activation(e_row[:], ml[:], ACT.Exp, bias=cst[:, C_LNR:C_LNR + 1], scale=-1.0).then_inc(exp_ready, 1)


def cell(nc, X, XNT, ctxT_dram, ctx_dram, m_dram, cst, AT, ET, g_in, g_tanh, lns, ln_tanh,
         slots_blank):
    with ExitStack() as ctx:
        sb = lambda n, s, d=F32: ctx.enter_context(nc.sbuf_tensor("c_" + n, s, d))
        sem = lambda n: ctx.enter_context(nc.semaphore("c_" + n))
        two = lambda f, n, *a: [f(f"{n}{p}", *a) for p in range(2)]
        keyT = two(sb, "keyT", [128, KT, 128])
        val = two(sb, "val", [128, NH0, DH0])
        val1 = two(sb, "val1", [128, NH0, DH0 + 1])
        mrow = two(sb, "mrow", [128, NH0, 128])
        qbd = two(sb, "qbd", [128, KT, 4, 128])
        expo = two(sb, "expo", [128, NH0, 128])
        dmat = two(sb, "dmat", [128, NH0, 128])
        cmat = two(sb, "cmat", [128, NH0, 128])
        rsum, den, rden = sb("rsum", [128, NH0]), sb("den", [128, NH0]), sb("rden", [128, NH0])
        h = sb("h", [128, B, D])
        hstats = sb("hstats", [128, B, 6])
        hmv = sb("hmv", [128, B, 2])
        hstd = sb("hstd", [128, B])
        hrstd = sb("hrstd", [128, B])
        score = [[ctx.enter_context(nc.psum_tensor(f"c_score{p}{k}", [128, 512], F32)) for k in range(KT)]
                 for p in range(2)]
        pv = [ctx.enter_context(nc.psum_tensor(f"c_pv{p}", [128, 512], F32)) for p in range(2)]
        k_loaded, v_loaded, m_loaded = two(sem, "k_loaded"), two(sem, "v_loaded"), two(sem, "m_loaded")
        q_ready, v_ready, score_ready, expo_ready = sem("q_ready"), sem("v_ready"), sem("score_ready"), sem("expo_ready")
        dmat_ready, cmat_ready, pv_ready, h_ready = sem("dmat_ready"), sem("cmat_ready"), sem("pv_ready"), sem("h_ready")
        tanh_ready, hvar_ready, hstd_ready = sem("tanh_ready"), sem("hvar_ready"), sem("hstd_ready")
        block = ctx.enter_context(nc.Block())

        def wait(eng, counter, value):
            if not isinstance(value, int) or value > 0:
                eng.wait_ge(counter, value)

        def over(eng, body):
            body(0, 0, 1)
            body(1, 1, 1)
            with eng.Fori(0, (B - 4) // 2) as i:
                body(i * 2 + 2, 0, i + 2)
                body(i * 2 + 3, 1, i + 2)
            body(B - 2, 0, B // 2)
            body(B - 1, 1, B // 2)

        after = lambda p, nth: (1 - p, nth + p)
        inside = lambda s, n: not isinstance(s, int) or s < n
        tokens = lambda s: ds(s * 128, 128) if not isinstance(s, int) else slice(s * 128, (s + 1) * 128)

        @block.sync
        def _(sp):
            def load(s, p, nth):
                wait(sp, expo_ready, s - 1)
                sp.dma_start(mrow[p][:].rearrange("p h t -> p (h t)"),
                             m_dram.rearrange("(b h) t -> b (h t)", b=B)[ds(s, 1)]
                             .broadcast_to([128, NH0 * 128])).then_inc(m_loaded[p], 16)
                wait(sp, score_ready, s - 1)
                sp.dma_start(keyT[p][:], ctxT_dram[:, :, tokens(s)]).then_inc(k_loaded[p], 16)
                wait(sp, v_ready, s - 1)
                sp.dma_start(val[p][:].rearrange("p h d -> p (h d)"),
                             ctx_dram[ds(s, 1)].rearrange("o p d -> (o p) d")).then_inc(v_loaded[p], 16)
            over(sp, load)
            sp.wait_ge(slots_blank, 16)

        @block.gpsimd
        def _(pool):
            for p in range(2):
                pool.memset(val1[p][:], 1.0)
            pool.drain()

            def prepare(s, p, nth):
                wait(pool, score_ready, s - 1)
                for k in range(KT):
                    last = pool.tensor_tensor(
                        qbd[p][:, k],
                        XNT[:, k, tokens(s)].rearrange("p (o t) -> p o t", o=1).broadcast_to([128, 4, 128]),
                        cst[:, C_BD0:C_BD0 + 4].rearrange("p (h o) -> p h o", o=1).broadcast_to([128, 4, 128]),
                        ALU.mult)
                last.then_inc(q_ready, 1)
                pool.wait_ge(v_loaded[p], nth * 16)
                wait(pool, pv_ready, s - 1)
                pool.tensor_tensor(val1[p][:, :, 0:DH0], val[p][:],
                                   cst[:, C_ONE:C_ONE + 1].rearrange("p (a b) -> p a b", a=1)
                                   .broadcast_to([128, NH0, DH0]), ALU.mult).then_inc(v_ready, 1)
            over(pool, prepare)

        @block.tensor
        def _(pe):
            def scores(s, p, nth):
                pe.wait_ge(k_loaded[p], nth * 16)
                pe.wait_ge(q_ready, s + 1)
                wait(pe, cmat_ready, s - 1)
                for k in range(KT):
                    last = pe.matmul(score[p][k][:], keyT[p][:, k], qbd[p][:, k], start=True, stop=True)
                last.then_inc(score_ready, 1)

            def body(s, p, nth):
                if inside(s, B - 1):
                    scores(s + 1, *after(p, nth))
                pe.wait_ge(v_ready, s + 1)
                pe.wait_ge(cmat_ready, s + 1)
                wait(pe, h_ready, s - 1)
                for n in range(NH0):
                    last = pe.matmul(pv[p][:, n * 33:(n + 1) * 33], cmat[p][:, n], val1[p][:, n],
                                     start=True, stop=True)
                last.then_inc(pv_ready, 1)
            scores(0, 0, 1)
            over(pe, body)

        @block.scalar
        def _(act):
            act.activation(g_tanh[:], g_in[:], ACT.Tanh).then_inc(tanh_ready, 1)

            def decay(s, p, nth):
                act.wait_ge(expo_ready, s + 1)
                wait(act, cmat_ready, s - 1)
                act.activation(dmat[p][:], expo[p][:], ACT.Exp, scale=-1.0).then_inc(dmat_ready, 1)
            over(act, decay)
            act.wait_ge(hvar_ready, 1)
            act.activation(hstd[:], hmv[:, :, 1], ACT.Sqrt, bias=cst[:, C_EPS:C_EPS + 1]).then_inc(hstd_ready, 1)

        @block.vector
        def _(dve):
            def exponents(s, p, nth):
                dve.wait_ge(m_loaded[p], nth * 16)
                wait(dve, dmat_ready, s - 1)
                for n in range(NH0):
                    last = dve.scalar_tensor_tensor(
                        expo[p][:, n], mrow[p][:, n], AT[:, ds(s * 8 + n, 1)],
                        cst[:, C_PEN:C_PEN + 128], ALU.subtract, ALU.max)
                last.then_inc(expo_ready, 1)

            def finish(s, p):
                dve.wait_ge(pv_ready, s + 1)
                o = pv[p][:, 0:NH0 * 33].rearrange("p (h d) -> p h d", h=NH0)
                dve.tensor_copy(rsum[:], o[:, :, DH0])
                dve.drain()
                dve.scalar_tensor_tensor(den[:], rsum[:], -1.0, rsum[:], ALU.mult, ALU.max)
                dve.drain()
                dve.scalar_tensor_tensor(rsum[:], den[:], CELL_EPS * ROOT0, ET[:, ds(s * 8, 8)], ALU.add, ALU.max)
                dve.drain()
                dve.reciprocal(rden[:], rsum[:])
                dve.drain()
                dve.tensor_tensor(h[:, ds(s, 1), :].rearrange("p o (h d) -> p (o h) d", h=NH0), o[:, :, 0:DH0],
                                  rden[:].rearrange("p (h o) -> p h o", o=1).broadcast_to([128, NH0, DH0]),
                                  ALU.mult).then_inc(h_ready, 1)
                dve.drain()
                dve.bn_stats(hstats[:, ds(s, 1), :], h[:, ds(s, 1), :])

            def body(s, p, nth):
                if inside(s, B - 1):
                    exponents(s + 1, *after(p, nth))
                dve.wait_ge(dmat_ready, s + 1)
                dve.wait_ge(score_ready, s + 1)
                wait(dve, pv_ready, s - 1)
                for k in range(KT):
                    last = dve.tensor_tensor(cmat[p][:, 4 * k:4 * k + 4].rearrange("p h t -> p (h t)"),
                                             score[p][k][:],
                                             dmat[p][:, 4 * k:4 * k + 4].rearrange("p h t -> p (h t)"), ALU.mult)
                last.then_inc(cmat_ready, 1)
                if not isinstance(s, int) or s > 0:
                    finish(s - 1, 1 - p)

            dve.wait_ge(tanh_ready, 1)
            dve.tensor_scalar(ln_tanh[:], lns[:], g_tanh[:, 0:1], None, ALU.mult)
            exponents(0, 0, 1)
            over(dve, body)
            finish(B - 1, 1)
            dve.drain()
            for s in range(B):
                dve.bn_aggr(hmv[:, s, :], hstats[:, s, :])
            dve.drain().then_inc(hvar_ready, 1)
            for s in range(B):
                dve.scalar_tensor_tensor(h[:, s, :], h[:, s, :], hmv[:, s, 0:1], ln_tanh[:], ALU.subtract, ALU.mult)
            dve.wait_ge(hstd_ready, 1)
            dve.reciprocal(hrstd[:], hstd[:])
            dve.drain()
            for s in range(B):
                dve.scalar_tensor_tensor(X[:, s, :], h[:, s, :], hrstd[:, s:s + 1], X[:, s, :], ALU.mult, ALU.add)


def attention(nc, X, XNT, ctxT_dram, mask_dram, w_dram, bq_dram, bv_dram, cst, tanh_col):
    HH = NH1 // 2
    with ExitStack() as ctx:
        sb = lambda n, s, d=F32: ctx.enter_context(nc.sbuf_tensor("a_" + n, s, d))
        sem = lambda n: ctx.enter_context(nc.semaphore("a_" + n))
        pb = lambda n: ctx.enter_context(nc.psum_tensor("a_" + n, [128, 512], F32))
        two = lambda f, n, *a: [f(f"{n}{p}", *a) for p in range(2)]
        w = sb("w", [128, 3, KT, D])
        bqk = sb("bqk", [128, 2, KT])
        bv = sb("bv", [128, D])
        keyT = two(sb, "keyT", [128, KT, 128])
        msk, msk1, pen = two(sb, "msk", [128, 128]), two(sb, "msk1", [128, 128]), two(sb, "pen", [128, 128])
        qT, kT = two(sb, "qT", [128, KT, 128]), two(sb, "kT", [128, KT, 128])
        kbd = two(sb, "kbd", [128, KT, HH, 128])
        v1 = two(sb, "v1", [128, NH1, DH1 + 1])
        sc = [[sb(f"sc{p}{q}", [128, HH, 128]) for q in range(2)] for p in range(2)]
        pr = [[sb(f"pr{p}{q}", [128, HH, 128]) for q in range(2)] for p in range(2)]
        mx = two(sb, "mx", [128, HH])
        prT = two(sb, "prT", [128, 4, 128])
        rs, rs2 = sb("rs", [128, NH1]), sb("rs2", [128, NH1])
        o_sb = sb("o_sb", [128, D])
        proj = pb("proj")
        score = [[pb(f"score{q}{k}") for k in range(2)] for q in range(2)]
        turned = two(pb, "turned")
        out_ps = pb("out_ps")
        w_loaded, ones_ready = sem("w_loaded"), sem("ones_ready")
        k_loaded, m_loaded = two(sem, "k_loaded"), two(sem, "m_loaded")
        proj_ready, qk_ready, v_ready = sem("proj_ready"), sem("qk_ready"), sem("v_ready")
        kbd_ready, pen_ready = sem("kbd_ready"), sem("pen_ready")
        score_ready, score_free = sem("score_ready"), sem("score_free")
        max_ready, sub_ready, pr_ready = sem("max_ready"), two(sem, "sub_ready"), sem("pr_ready")
        turned_ready, prT_ready, pv_ready, out_free = sem("turned_ready"), sem("prT_ready"), sem("pv_ready"), sem("out_free")
        block = ctx.enter_context(nc.Block())

        def wait(eng, counter, value):
            if not isinstance(value, int) or value > 0:
                eng.wait_ge(counter, value)

        def over(eng, body):
            body(0, 0)
            body(1, 1)
            with eng.Fori(0, (B - 4) // 2) as i:
                body(i * 2 + 2, 0)
                body(i * 2 + 3, 1)
            body(B - 2, 0)
            body(B - 1, 1)

        tokens = lambda s: ds(s * 128, 128) if not isinstance(s, int) else slice(s * 128, (s + 1) * 128)
        bc = lambda a, n: a.rearrange("p (h o) -> p h o", o=1).broadcast_to([128, a.shape[1], n])
        rep = lambda a, n: a.rearrange("p (o t) -> p o t", o=1).broadcast_to([128, n, a.shape[1]])

        @block.sync
        def _(sp):
            sp.dma_start(w[:], w_dram.rearrange("w p k n -> p w k n")).then_inc(w_loaded, 16)
            sp.dma_start(bqk[:], bq_dram).then_inc(w_loaded, 16)
            sp.dma_start(bv[:], bv_dram.rearrange("(o n) -> o n", o=1).broadcast_to([128, D])).then_inc(w_loaded, 16)

            def load(s, p):
                wait(sp, proj_ready, 2 * s - 2)
                sp.dma_start(keyT[p][:], ctxT_dram[:, :, tokens(s)]).then_inc(k_loaded[p], 16)
                wait(sp, pen_ready, s - 1)
                sp.dma_start(msk[p][:], mask_dram[ds(s, 1)].rearrange("o q k -> (o q) k")).then_inc(m_loaded[p], 16)
            over(sp, load)

        @block.tensor
        def _(pe):
            pe.wait_ge(w_loaded, 48)

            def project_qk(s, p, nth):
                wait(pe, k_loaded[p], nth * 16)
                wait(pe, v_ready, s)
                for which in range(2):
                    for m in range(KT):
                        at = (which * KT + m) * 128
                        for k in range(KT):
                            src = XNT[:, k, tokens(s)] if which == 0 else keyT[p][:, k]
                            last = pe.matmul(proj[:, at:at + 128], w[:, which, k, m * 128:(m + 1) * 128], src,
                                             start=(k == 0), stop=(k == KT - 1))
                last.then_inc(proj_ready, 1)

            def project_v(s, p):
                pe.wait_ge(qk_ready, s + 1)
                for k in range(KT):
                    last = pe.matmul(proj[:, 0:256], keyT[p][:, k], w[:, 2, k], start=(k == 0), stop=(k == KT - 1))
                last.then_inc(proj_ready, 1)

            def scores(s, p, q):
                pe.wait_ge(kbd_ready, 2 * s + q + 1)
                wait(pe, score_free, 2 * s + q - 1)
                for g in range(2):
                    last = pe.matmul(score[q][g][:], qT[p][:, q], kbd[p][:, q, 4 * g:4 * g + 4], start=True, stop=True)
                last.then_inc(score_ready, 1)

            def values(s, p, q):
                n = (2 * s + q) * 2
                pe.wait_ge(pr_ready, 2 * s + q + 1)
                for g in range(2):
                    wait(pe, prT_ready, n + g - 1)
                    for j in range(4):
                        last = pe.transpose(turned[g][:, j * 128:(j + 1) * 128], pr[p][q][:, 4 * g + j],
                                            cst[:, C_ID:C_ID + 128])
                    last.then_inc(turned_ready, 1)
                if q == 0:
                    pe.wait_ge(v_ready, s + 1)
                    wait(pe, out_free, s)
                for g in range(2):
                    pe.wait_ge(prT_ready, n + g + 1)
                    for j in range(4):
                        hd = q * HH + 4 * g + j
                        last = pe.matmul(out_ps[:, hd * 17:(hd + 1) * 17], prT[g][:, j], v1[p][:, hd],
                                         start=True, stop=True)
                    last.then_inc(pv_ready, 1)

            def body(s, p, nth):
                first, end = isinstance(s, int) and s == 0, isinstance(s, int) and s == B - 1
                scores(s, p, 0)
                if not end:
                    project_qk(s + 1, 1 - p, nth)
                if not first:
                    values(s - 1, 1 - p, 0)
                if not end:
                    project_v(s + 1, 1 - p)
                scores(s, p, 1)
                if not first:
                    values(s - 1, 1 - p, 1)

            project_qk(0, 0, 1)
            project_v(0, 0)
            body(0, 0, 1)
            body(1, 1, 2)
            with pe.Fori(0, (B - 4) // 2) as i:
                body(i * 2 + 2, 0, i + 2)
                body(i * 2 + 3, 1, i + 3)
            body(B - 2, 0, B // 2)
            body(B - 1, 1, None)
            values(B - 1, 1, 0)
            values(B - 1, 1, 1)

        @block.gpsimd
        def _(pool):
            for p in range(2):
                pool.memset(v1[p][:], 1.0)
            pool.drain().then_inc(ones_ready, 1)

            def prepare(s, p, nth):
                pool.wait_ge(m_loaded[p], nth * 16)
                wait(pool, score_free, 2 * s - 2)
                pool.tensor_tensor(msk1[p][:], msk[p][:], cst[:, C_ONE:C_ONE + 1].broadcast_to([128, 128]),
                                   ALU.subtract)
                pool.drain()
                pool.tensor_scalar(pen[p][:], msk1[p][:], 10000.0, None, ALU.mult).then_inc(pen_ready, 1)
                pool.wait_ge(qk_ready, s + 1)
                wait(pool, score_ready, 2 * s - 2)
                for q in range(KT):
                    pool.tensor_tensor(kbd[p][:, q], rep(kT[p][:, q], HH), bc(cst[:, C_BD1:C_BD1 + HH], 128),
                                       ALU.mult).then_inc(kbd_ready, 1)

            def subtract(s, p):
                pool.wait_ge(max_ready, s + 1)
                pool.tensor_tensor(sc[p][1][:], sc[p][1][:], bc(mx[1][:], 128), ALU.subtract).then_inc(sub_ready[1], 1)

            prepare(0, 0, 1)
            prepare(1, 1, 1)
            subtract(0, 0)
            with pool.Fori(0, (B - 2) // 2) as i:
                prepare(i * 2 + 2, 0, i + 2)
                subtract(i * 2 + 1, 1)
                prepare(i * 2 + 3, 1, i + 2)
                subtract(i * 2 + 2, 0)
            subtract(B - 1, 1)

        @block.scalar
        def _(act):
            act.wait_ge(w_loaded, 48)

            def keep_qk(s, p):
                act.wait_ge(proj_ready, 2 * s + 1)
                wait(act, score_ready, 2 * s - 2)
                wait(act, kbd_ready, 2 * s - 2)
                for which, dst in ((0, qT), (1, kT)):
                    for m in range(KT):
                        at = (which * KT + m) * 128
                        last = act.activation(dst[p][:, m], proj[:, at:at + 128], ACT.Identity,
                                              bias=bqk[:, which, m:m + 1])
                last.then_inc(qk_ready, 1)

            def exps(s, p, q):
                act.wait_ge(sub_ready[q], s + 1)
                wait(act, turned_ready, 4 * s + 2 * q - 6)
                act.activation(pr[p][q][:], sc[p][q][:], ACT.Exp, scale=1.0 / math.sqrt(DH1)).then_inc(pr_ready, 1)

            def turn(s, q):
                for g in range(2):
                    n = 4 * s + 2 * q + g
                    act.wait_ge(turned_ready, n + 1)
                    wait(act, pv_ready, n - 1)
                    act.copy(prT[g][:].rearrange("p h t -> p (h t)"), turned[g][:]).then_inc(prT_ready, 1)

            def body(s, p):
                if not isinstance(s, int) or s < B - 1:
                    keep_qk(s + 1, 1 - p)
                if not isinstance(s, int) or s > 0:
                    turn(s - 1, 0)
                    turn(s - 1, 1)
                exps(s, p, 0)
                exps(s, p, 1)

            keep_qk(0, 0)
            over(act, body)
            turn(B - 1, 0)
            turn(B - 1, 1)

        @block.vector
        def _(dve):
            dve.wait_ge(w_loaded, 48)
            dve.wait_ge(ones_ready, 1)

            def keep_v(s, p):
                dve.wait_ge(proj_ready, 2 * s + 2)
                wait(dve, pv_ready, 4 * s - 4)
                dve.tensor_tensor(v1[p][:, :, 0:DH1], proj[:, 0:256].rearrange("p (h d) -> p h d", h=NH1),
                                  bv[:].rearrange("p (h d) -> p h d", h=NH1), ALU.add).then_inc(v_ready, 1)

            def soft(s, p, q):
                dve.wait_ge(score_ready, 2 * s + q + 1)
                dve.wait_ge(pen_ready, s + 1)
                wait(dve, pr_ready, 2 * s + q - 3)
                if q == 1:
                    wait(dve, sub_ready[1], s)
                for g in range(2):
                    last = dve.scalar_tensor_tensor(sc[p][q][:, 4 * g:4 * g + 4], rep(pen[p][:], 4), math.sqrt(DH1),
                                                    score[q][g][:].rearrange("p (h t) -> p h t", h=4),
                                                    ALU.mult, ALU.add)
                last.then_inc(score_free, 1)
                dve.drain()
                red = dve.tensor_reduce(mx[q][:], sc[p][q][:], AX.X, ALU.max)
                if q == 1:
                    red.then_inc(max_ready, 1)
                else:
                    dve.drain()
                    dve.tensor_tensor(sc[p][q][:], sc[p][q][:], bc(mx[q][:], 128), ALU.subtract).then_inc(sub_ready[0], 1)

            def finish(s):
                dve.wait_ge(pv_ready, 4 * s + 4)
                o = out_ps[:, 0:NH1 * 17].rearrange("p (h d) -> p h d", h=NH1)
                dve.reciprocal(rs[:], o[:, :, DH1])
                dve.drain()
                dve.tensor_scalar(rs2[:], rs[:], tanh_col, None, ALU.mult)
                dve.drain()
                dve.tensor_tensor(o_sb[:].rearrange("p (h d) -> p h d", h=NH1), o[:, :, 0:DH1], bc(rs2[:], DH1),
                                  ALU.mult).then_inc(out_free, 1)
                dve.drain()
                xs = X[:, ds(s, 1), :].rearrange("p o d -> p (o d)")
                dve.tensor_tensor(xs, xs, o_sb[:], ALU.add)

            def body(s, p):
                soft(s, p, 0)
                soft(s, p, 1)
                if not isinstance(s, int) or s < B - 1:
                    keep_v(s + 1, 1 - p)
                if not isinstance(s, int) or s > 0:
                    finish(s - 1)

            keep_v(0, 0)
            over(dve, body)
            finish(B - 1)


def top1(dve, src, oh, mx, rev, shape):
    bc = lambda a: a.rearrange("p g (k o) -> p g k o", o=1).broadcast_to(shape)
    dve.tensor_reduce(mx, src, AX.X, ALU.max)
    dve.drain()
    dve.tensor_tensor(oh, src, bc(mx), ALU.is_equal)
    dve.drain()
    dve.tensor_tensor(oh, oh, rev, ALU.mult)
    dve.drain()
    dve.tensor_reduce(mx, oh, AX.X, ALU.max)
    dve.drain()
    dve.tensor_tensor(oh, oh, bc(mx), ALU.is_equal)
    dve.drain()


def route0(nc, ps, bias_dram, cst, slots, slot_weight, tile_expert, tanh_col):
    with ExitStack() as ctx:
        sb = lambda n, s, d=F32: ctx.enter_context(nc.sbuf_tensor("r0_" + n, s, d))
        sem = lambda n: ctx.enter_context(nc.semaphore("r0_" + n))
        eb = sb("eb", [128, E0])
        lg, oh0, oh1, l2 = (sb(n, [128, B, 1, E0]) for n in ("lg", "oh0", "oh1", "l2"))
        scratch, m1, m2, e2, w1 = (sb(n, [128, B, 1]) for n in ("scratch", "m1", "m2", "e2", "w1"))
        chosen, total, running, pos = (sb(n, [128, E0, B]) for n in ("chosen", "total", "running", "pos"))
        over = sb("over", [128, E0, B])
        ntile, tile_end, base = (sb(n, [128, E0]) for n in ("ntile", "tile_end", "base"))
        slot_f = sb("slot_f", [128, B, 2])
        ended = sb("ended", [1, NT, E0])
        expert_f, expert_c = sb("expert_f", [1, NT]), sb("expert_c", [1, NT])
        count_ps = ctx.enter_context(nc.psum_tensor("r0_count", [128, 512], F32))
        loaded, diff_ready, exp_ready = sem("loaded"), sem("diff_ready"), sem("exp_ready")
        chosen_ready, counts_ready = sem("chosen_ready"), sem("counts_ready")
        block = ctx.enter_context(nc.Block())

        @block.sync
        def _(sp):
            sp.dma_start(eb[:], bias_dram.rearrange("(o n) -> o n", o=1).broadcast_to([128, E0])).then_inc(loaded, 16)
            sp.wait_ge(loaded, 16)

        @block.tensor
        def _(pe):
            pe.wait_ge(chosen_ready, 1)
            flat = chosen[:].rearrange("p e s -> p (e s)")
            pe.matmul(count_ps[:, 0:128], cst[:, C_TRI:C_TRI + 128], flat, start=True, stop=True)
            pe.matmul(count_ps[:, 128:256], cst[:, C_ONES:C_ONES + 128], flat, start=True, stop=True
                      ).then_inc(counts_ready, 1)

        @block.scalar
        def _(act):
            act.wait_ge(diff_ready, 1)
            act.activation(e2[:], w1[:], ACT.Exp).then_inc(exp_ready, 1)

        @block.vector
        def _(dve):
            dve.wait_ge(loaded, 16)
            shape = [128, B, 1, E0]
            rev = cst[:, C_REV:C_REV + E0].rearrange("p (a b e) -> p a b e", a=1, b=1).broadcast_to(shape)
            flat = lambda a: a[:].rearrange("p s b e -> p (s b e)")
            parts = ps[:, 0:2 * B * E0].rearrange("p (s b e) -> p s b e", s=B, b=2)
            dve.tensor_copy(l2[:], parts[:, :, 1:2, :])
            dve.drain()
            dve.tensor_tensor(oh0[:], l2[:], parts[:, :, 0:1, :], ALU.add)
            dve.drain()
            dve.tensor_tensor(lg[:], oh0[:],
                              eb[:].rearrange("p (a b e) -> p a b e", a=1, b=1).broadcast_to(shape), ALU.add)
            dve.drain()
            dve.tensor_reduce(m1[:], lg[:], AX.X, ALU.max)
            top1(dve, lg[:], oh0[:], scratch[:], rev, shape)
            dve.scalar_tensor_tensor(flat(l2), flat(oh0), -BIG, flat(lg), ALU.mult, ALU.add)
            dve.drain()
            dve.tensor_reduce(m2[:], l2[:], AX.X, ALU.max)
            top1(dve, l2[:], oh1[:], scratch[:], rev, shape)
            dve.tensor_tensor(chosen[:].rearrange("p e s -> p s e"), oh0[:].rearrange("p s b e -> p s (b e)"),
                              oh1[:].rearrange("p s b e -> p s (b e)"), ALU.add).then_inc(chosen_ready, 1)
            dve.tensor_tensor(w1[:], m2[:], m1[:], ALU.subtract)
            dve.drain().then_inc(diff_ready, 1)
            dve.wait_ge(exp_ready, 1)
            dve.tensor_scalar(m1[:], e2[:], 1.0, None, ALU.add)
            dve.drain()
            dve.reciprocal(m2[:], m1[:])
            dve.drain()
            dve.tensor_scalar(slot_weight[:, :, 0:1], m2[:], tanh_col, None, ALU.mult)
            dve.drain()
            dve.tensor_tensor(slot_weight[:, :, 1:2], slot_weight[:, :, 0:1], e2[:], ALU.mult)
            dve.wait_ge(counts_ready, 1)
            cols = lambda a: a[:].rearrange("p e s -> p (e s)")
            dve.tensor_copy(cols(total), count_ps[:, 128:256])
            dve.drain()
            dve.tensor_tensor_scan(cols(running), cst[:, C_KEEP:C_KEEP + 128], cols(total), 0.0, ALU.mult, ALU.add)
            dve.drain()
            dve.tensor_tensor(over[:], running[:, :, B - 1:B].broadcast_to([128, E0, B]),
                              cst[:, C_STEP:C_STEP + B].rearrange("p (o j) -> p o j", o=1).broadcast_to([128, E0, B]),
                              ALU.is_gt)
            dve.drain()
            dve.tensor_reduce(ntile[:], over[:], AX.X, ALU.add)
            dve.drain()
            dve.tensor_tensor_scan(tile_end[:], cst[:, C_ONES:C_ONES + E0], ntile[:], 0.0, ALU.mult, ALU.add)
            dve.drain()
            dve.tensor_tensor(base[:], tile_end[:], ntile[:], ALU.subtract)
            dve.tensor_tensor(running[:], running[:], total[:], ALU.subtract)
            dve.drain()
            dve.scalar_tensor_tensor(running[:], base[:].rearrange("p (e o) -> p e o", o=1).broadcast_to([128, E0, B]),
                                     128.0, running[:], ALU.mult, ALU.add)
            dve.drain()
            dve.tensor_tensor(cols(pos), count_ps[:, 0:128], cols(running), ALU.add)
            dve.drain()
            for k, oh in enumerate((oh0, oh1)):
                dve.tensor_tensor(total[:].rearrange("p e s -> p s e") if k == 0 else over[:].rearrange("p e s -> p s e"),
                                  oh[:].rearrange("p s b e -> p s (b e)"), pos[:].rearrange("p e s -> p s e"), ALU.mult)
            dve.drain()
            for k, part in enumerate((total, over)):
                dve.tensor_reduce(slot_f[:, :, k:k + 1].rearrange("p s k -> p (s k)"), part[:].rearrange("p e s -> p s e"),
                                  AX.X, ALU.add)
            dve.tensor_tensor(ended[:], cst[0:1, C_TILE:C_TILE + NT].rearrange("p (i o) -> p i o", o=1)
                              .broadcast_to([1, NT, E0]),
                              tile_end[0:1, :].rearrange("p (o e) -> p o e", o=1).broadcast_to([1, NT, E0]), ALU.is_ge)
            dve.drain()
            dve.tensor_copy(slots[:], slot_f[:].rearrange("p s k -> p k s"))
            dve.tensor_reduce(expert_f[:], ended[:], AX.X, ALU.add)
            dve.drain()
            dve.tensor_scalar(expert_c[:], expert_f[:], float(E0 - 1), None, ALU.min)
            dve.drain()
            dve.tensor_copy(tile_expert[:], expert_c[:])


def routed_tiles(nc, W, w_dram, first_late, xg_dram, y_dram, tile_expert, cst):
    with ExitStack() as ctx:
        sb = lambda n, s, d=F32: ctx.enter_context(nc.sbuf_tensor("t_" + n, s, d))
        sem = lambda n: ctx.enter_context(nc.semaphore("t_" + n))
        pb = lambda n: ctx.enter_context(nc.psum_tensor("t_" + n, [128, 512], F32))
        two = lambda f, n, *a: [f(f"{n}{p}", *a) for p in range(2)]
        x = two(sb, "x", [128, D + 1])
        next_dest, dest = two(sb, "next_dest", [128, 1], I32), two(sb, "dest", [128, 1], I32)
        xT = two(sb, "xT", [128, KT, 128])
        act_g = two(sb, "act_g", [128, HID])
        hid = two(sb, "hid", [128, HID])
        hidT = two(sb, "hidT", [128, HT, 128])
        y = two(sb, "y", [128, D])
        gate, up, y_ps = two(pb, "gate"), two(pb, "up"), two(pb, "y_ps")
        x_turned, h_turned = pb("x_turned"), pb("h_turned")
        w_loaded = sem("w_loaded")
        x_loaded, y_stored = two(sem, "x_loaded"), two(sem, "y_stored")
        xt_ready, xT_ready, gate_ready, up_ready = sem("xt_ready"), sem("xT_ready"), sem("gate_ready"), sem("up_ready")
        silu_ready, hid_ready, ht_ready, hidT_ready = sem("silu_ready"), sem("hid_ready"), sem("ht_ready"), sem("hidT_ready")
        down_ready, y_ready = sem("down_ready"), sem("y_ready")
        dest_ready, sent = sem("dest_ready"), sem("sent")
        block = ctx.enter_context(nc.Block())

        def wait(eng, counter, value):
            if not isinstance(value, int) or value > 0:
                eng.wait_ge(counter, value)

        def over(eng, body):
            body(0, 0, 1)
            body(1, 1, 2 - 1)
            pairs = (NT - 5) // 2
            with eng.Fori(0, pairs) as j:
                body(j * 2 + 2, 0, j + 2)
                body(j * 2 + 3, 1, j + 2)
            for i in range(2 + 2 * pairs, NT):
                body(i, i % 2, i // 2 + 1)

        inside = lambda i, n: not isinstance(i, int) or i < n

        @block.sync
        def _(sp):
            def load(i, p, nth):
                wait(sp, xt_ready, i - 1)
                wait(sp, dest_ready, i - 1)
                sp.dma_start(x[p][:], xg_dram[ds(i * 128, 128), :]).then_inc(x_loaded[p], 16)
                if isinstance(i, int) and i == 0:
                    for e in range(first_late, E0):
                        sp.dma_start(W[:, e, :], w_dram[NSH0 + e]).then_inc(w_loaded, 16)
            over(sp, load)

        @block.gpsimd
        def _(pool):
            def send(i, p, nth):
                pool.wait_ge(y_ready, i + 1)
                pool.sem_inc(sent, 1)
                pool.indirect_dma_start(y_dram, bass.IndirectOffsetOnAxis(ap=dest[p][:].bitcast(U32), axis=0), y[p][:],
                                        None).then_inc(y_stored[p], 16)
            over(pool, send)
            for p in range(2):
                pool.wait_ge(y_stored[p], 16 * ((NT + 1 - p) // 2))

        @block.tensor
        def _(pe):
            def turn_x(i, p, nth):
                pe.wait_ge(x_loaded[p], nth * 16)
                wait(pe, xT_ready, i)
                for k in range(KT):
                    last = pe.transpose(x_turned[:, k * 128:(k + 1) * 128], x[p][:, k * 128:(k + 1) * 128],
                                        cst[:, C_ID:C_ID + 128])
                last.then_inc(xt_ready, 1)

            def product(i, p, out, part, ready, e):
                if part == 0:
                    pe.wait_ge(xT_ready, i + 1)
                wait(pe, hid_ready, i - 1)
                for k in range(KT):
                    at = (part * KT + k) * HID
                    last = pe.matmul(out[p][:], xT[p][:, k], W[:, ds(e, 1), at:at + HID],
                                     start=(k == 0), stop=(k == KT - 1))
                last.then_inc(ready, 1)

            def turn_hidden(i, p):
                pe.wait_ge(hid_ready, i + 1)
                wait(pe, hidT_ready, i)
                for h in range(HT):
                    last = pe.transpose(h_turned[:, h * 128:(h + 1) * 128], hid[p][:, h * 128:(h + 1) * 128],
                                        cst[:, C_ID:C_ID + 128])
                last.then_inc(ht_ready, 1)

            def down(i, p, e):
                pe.wait_ge(hidT_ready, i + 1)
                wait(pe, y_ready, i - 1)
                for h in range(HT):
                    at = 2 * KT * HID + h * D
                    last = pe.matmul(y_ps[p][:, 0:D], hidT[p][:, h], W[:, ds(e, 1), at:at + D],
                                     start=(h == 0), stop=(h == HT - 1))
                last.then_inc(down_ready, 1)

            expert = lambda i: pe.value_load(tile_expert[0:1, ds(i, 1)], min_val=0, max_val=E0 - 1)

            def body(i, p, nth):
                e = expert(i)
                if inside(i, NT - 1):
                    e_next = expert(i + 1)
                    product(i + 1, 1 - p, gate, 0, gate_ready, e_next)
                turn_hidden(i, p)
                if inside(i, NT - 1):
                    product(i + 1, 1 - p, up, 1, up_ready, e_next)
                if inside(i, NT - 2):
                    turn_x(i + 2, p, nth + 1)
                down(i, p, e)

            turn_x(0, 0, 1)
            e0 = expert(0)
            pe.wait_ge(w_loaded, 16 * (E0 - first_late))
            product(0, 0, gate, 0, gate_ready, e0)
            product(0, 0, up, 1, up_ready, e0)
            turn_x(1, 1, 1)
            over(pe, body)

        @block.scalar
        def _(act):
            def body(i, p, nth):
                act.wait_ge(gate_ready, i + 1)
                wait(act, hid_ready, i - 1)
                act.activation(act_g[p][:], gate[p][:], ACT.Silu).then_inc(silu_ready, 1)
                act.wait_ge(ht_ready, i + 1)
                wait(act, down_ready, i - 1)
                act.copy(hidT[p][:].rearrange("p h t -> p (h t)"), h_turned[:]).then_inc(hidT_ready, 1)
            over(act, body)

        @block.vector
        def _(dve):
            def keep_x(i, p):
                dve.wait_ge(xt_ready, i + 1)
                wait(dve, up_ready, i - 1)
                dve.tensor_copy(xT[p][:].rearrange("p k t -> p (k t)"), x_turned[:, 0:D]).then_inc(xT_ready, 1)
                dve.tensor_copy(next_dest[p][:], x[p][:, D:D + 1].bitcast(I32)).then_inc(dest_ready, 1)

            def body(i, p, nth):
                dve.wait_ge(silu_ready, i + 1)
                dve.wait_ge(up_ready, i + 1)
                wait(dve, ht_ready, i - 1)
                dve.tensor_tensor(hid[p][:], act_g[p][:], up[p][:], ALU.mult).then_inc(hid_ready, 1)
                wait(dve, y_stored[p], (nth - 1) * 16)
                dve.tensor_copy(dest[p][:], next_dest[p][:])
                if inside(i, NT - 2):
                    dve.drain()
                    keep_x(i + 2, p)
                dve.wait_ge(down_ready, i + 1)
                dve.tensor_scalar(y[p][:], y_ps[p][:, 0:D], 1.0, None, ALU.mult)
                dve.drain().then_inc(y_ready, 1)
            keep_x(0, 0)
            keep_x(1, 1)
            dve.drain()
            over(dve, body)


def combine(nc, X, y_dram, slot_weight):
    with ExitStack() as ctx:
        picked = ctx.enter_context(nc.sbuf_tensor("m_picked", [128, 2, B, D], F32))
        loaded = [[ctx.enter_context(nc.semaphore(f"m_loaded{c}{k}")) for k in range(2)] for c in range(NCH)]
        block = ctx.enter_context(nc.Block())

        @block.sync
        def _(sp):
            rows = y_dram[0:2 * T, :].rearrange("(k s p) d -> p k s d", k=2, s=B)
            for c in range(NCH):
                for k in range(2):
                    part = slice(c * CH, (c + 1) * CH)
                    sp.dma_start(picked[:, k, part, :], rows[:, k, part, :]).then_inc(loaded[c][k], 16)

        @block.vector
        def _(dve):
            for c in range(NCH):
                for k in range(2):
                    dve.wait_ge(loaded[c][k], 16)
                    for s in range(c * CH, (c + 1) * CH):
                        dve.scalar_tensor_tensor(X[:, s, :], picked[:, k, s, :], slot_weight[:, s, k:k + 1],
                                                 X[:, s, :], ALU.mult, ALU.add)
                    dve.drain()


def route1(nc, ps, beside, bias_dram, cst, comb_dram):
    with ExitStack() as ctx:
        sb = lambda n, s, d=F32: ctx.enter_context(nc.sbuf_tensor("r1_" + n, s, d))
        sem = lambda n: ctx.enter_context(nc.semaphore("r1_" + n))
        eb = sb("eb", [128, E1])
        sg, sbias, cur, oh, sel = (sb(n, [128, B, E1]) for n in ("sg", "sbias", "cur", "oh", "sel"))
        comb = sb("comb", [128, E1, B])
        combT = sb("combT", [128, 2, 128])
        g1, g2, gs, goh, gsel, gtmp = (sb(n, [128, B, G1]) for n in ("g1", "g2", "gs", "goh", "gsel", "gtmp"))
        largest = sb("largest", [128, B, 8])
        logits = sb("logits", [128, B, E1])
        one = sb("one", [128, B, 1])
        one2 = sb("one2", [128, B, 1])
        ps2 = ctx.enter_context(nc.psum_tensor("r1_ps2", [128, 512], F32))
        loaded, logits_ready, sig_ready, comb_ready = sem("loaded"), sem("logits_ready"), sem("sig_ready"), sem("comb_ready")
        turned_ready, combT_ready, stored = sem("turned_ready"), sem("combT_ready"), sem("stored")
        block = ctx.enter_context(nc.Block())

        @block.sync
        def _(sp):
            sp.dma_start(eb[:], bias_dram.rearrange("(o n) -> o n", o=1).broadcast_to([128, E1])).then_inc(loaded, 16)
            beside.sync(sp)
            sp.wait_ge(loaded, 16)
            sp.wait_ge(combT_ready, 1)
            sp.dma_start(comb_dram.rearrange("(x e) (s t) -> (e s) x t", x=2, s=B), combT[:]).then_inc(stored, 16)
            sp.wait_ge(stored, 16)

        @block.gpsimd
        def _(pool):
            beside.pool(pool)

        @block.tensor
        def _(pe):
            pe.wait_ge(comb_ready, 1)
            for x in range(2):
                last = pe.transpose(ps2[:, x * 128:(x + 1) * 128],
                                    comb[:, 8 * x:8 * x + 8, :].rearrange("p e s -> p (e s)"),
                                    cst[:, C_ID:C_ID + 128])
            last.then_inc(turned_ready, 1)

        @block.scalar
        def _(act):
            act.wait_ge(logits_ready, 1)
            act.activation(sg[:], logits[:], ACT.Sigmoid).then_inc(sig_ready, 1)

        @block.vector
        def _(dve):
            dve.wait_ge(loaded, 16)
            parts = ps[:].rearrange("p (s b e) -> p s b e", s=B, b=2)
            dve.tensor_copy(cur[:], parts[:, :, 1, :])
            dve.drain()
            dve.tensor_tensor(logits[:], cur[:], parts[:, :, 0, :], ALU.add).then_inc(logits_ready, 1)
            dve.wait_ge(sig_ready, 1)
            in_groups = lambda a: a[:].rearrange("p s (g e) -> p s g e", g=G1)
            whole = lambda a: a[:].rearrange("p s (o e) -> p s o e", o=1)
            flat = lambda a: a[:].rearrange("p s e -> p (s e)")
            gshape, wshape, groups = [128, B, G1, EPG], [128, B, 1, E1], [128, B, 1, G1]
            rev = lambda n, sh: cst[:, C_REV:C_REV + n].rearrange("p (a b e) -> p a b e", a=1, b=1).broadcast_to(sh)
            dve.tensor_tensor(sbias[:], sg[:], eb[:].rearrange("p (o e) -> p o e", o=1).broadcast_to([128, B, E1]),
                              ALU.add)
            dve.drain()
            dve.tensor_reduce(g1[:], in_groups(sbias), AX.X, ALU.max)
            top1(dve, in_groups(sbias), in_groups(oh), gtmp[:], rev(EPG, gshape), gshape)
            dve.scalar_tensor_tensor(flat(cur), flat(oh), -BIG, flat(sbias), ALU.mult, ALU.add)
            dve.drain()
            dve.tensor_reduce(g2[:], in_groups(cur), AX.X, ALU.max)
            dve.drain()
            dve.tensor_tensor(gs[:], g1[:], g2[:], ALU.add)
            dve.drain()
            top1(dve, whole(gs), whole(gsel), one[:], rev(G1, groups), groups)
            dve.scalar_tensor_tensor(flat(gs), flat(gsel), -BIG, flat(gs), ALU.mult, ALU.add)
            dve.drain()
            top1(dve, whole(gs), whole(goh), one[:], rev(G1, groups), groups)
            dve.tensor_tensor(gsel[:], gsel[:], goh[:], ALU.add)
            dve.drain()
            dve.tensor_scalar(gs[:], gsel[:], 1.0, BIG, ALU.subtract, ALU.mult)
            dve.drain()
            dve.tensor_tensor(in_groups(cur), in_groups(sbias),
                              gs[:].rearrange("p s (g o) -> p s g o", o=1).broadcast_to(gshape), ALU.add)
            dve.drain()
            for s in range(B):
                dve.max(largest[:, s, :], cur[:, s, :])
            dve.drain()
            dve.memset(largest[:, :, 4:8], -BIG)
            dve.drain()
            for s in range(B):
                dve.match_replace(oh[:, s, :], largest[:, s, :], cur[:, s, :], BIG)
            dve.drain()
            dve.scalar_tensor_tensor(in_groups(sel), in_groups(oh), BIG,
                                     gsel[:].rearrange("p s (g o) -> p s g o", o=1).broadcast_to(gshape),
                                     ALU.is_equal, ALU.mult)
            dve.drain()
            dve.tensor_tensor(sel[:], sel[:], sg[:], ALU.mult)
            dve.drain()
            dve.tensor_reduce(one[:], whole(sel), AX.X, ALU.add)
            dve.drain()
            dve.tensor_scalar(one2[:], one[:], 1e-20, None, ALU.add)
            dve.drain()
            dve.reciprocal(one[:], one2[:])
            dve.drain()
            dve.tensor_tensor(comb[:].rearrange("p e s -> p s e"), sel[:], one[:].broadcast_to([128, B, E1]),
                              ALU.mult).then_inc(comb_ready, 1)
            dve.wait_ge(turned_ready, 1)
            dve.tensor_copy(combT[:].rearrange("p x t -> p (x t)"), ps2[:, 0:256]).then_inc(combT_ready, 1)


class Split:

    def __init__(self, ctx, nc, tag, one):
        self.one = one
        self.jobs = []
        self.loaded = [ctx.enter_context(nc.semaphore(f"{tag}_loaded{p}")) for p in range(3)]
        self.done = ctx.enter_context(nc.semaphore(tag + "_done"))

    def add(self, src, raw, hi, lo, slot, nth, after):
        self.jobs.append((src, raw, hi, lo, slot, nth, after))

    def part(self, jobs):
        return SplitPart(self, jobs)


class SplitPart:
    def __init__(self, split, jobs):
        self.split, self.jobs = split, jobs

    def sync(self, sp):
        for n in self.jobs:
            src, raw, hi, lo, slot, nth, after = self.split.jobs[n]
            if after:
                sp.wait_ge(self.split.done, after)
            sp.dma_start(raw, src).then_inc(self.split.loaded[slot], 16)

    def pool(self, pool):
        for n in self.jobs:
            src, raw, hi, lo, slot, nth, after = self.split.jobs[n]
            pool.wait_ge(self.split.loaded[slot], 16 * nth)
            pool.tensor_tensor(hi, raw, self.split.one.broadcast_to([128, raw.shape[1]]), ALU.mult)
            pool.drain()
            pool.tensor_tensor(lo, raw, hi.bitcast(F32), ALU.subtract).then_inc(self.split.done, 1)


class BesideShared:

    def __init__(self, ctx, nc, XN, W, w_dram, first_late, under_tokens, xg_dram, slots, home, slots_blank):
        self.home, self.slots_blank = home, slots_blank
        self.XN, self.W, self.w_dram, self.first_late, self.under_tokens = XN, W, w_dram, first_late, under_tokens
        self.xg_dram, self.slots = xg_dram, slots
        self.scattered = ctx.enter_context(nc.semaphore("e_scattered"))
        self.w_loaded = ctx.enter_context(nc.semaphore("e_w_loaded"))

    def pool(self, pool):
        pool.wait_ge(self.slots_blank, 16)
        for k in range(2):
            if k > 0:
                pool.wait_ge(self.scattered, 16 * k * B)
            pool.tensor_copy(self.XN[:, :, D:D + 1].bitcast(I32), self.home[:, k, :].rearrange("p (s o) -> p s o", o=1))
            pool.drain()
            for s in range(B):
                pool.indirect_dma_start(self.xg_dram, bass.IndirectOffsetOnAxis(ap=self.slots[:, k, s:s + 1], axis=0),
                                        self.XN[:, s, :], None).then_inc(self.scattered, 16)
        pool.wait_ge(self.scattered, 16 * 2 * B)

    def sync(self, sp):
        for e in range(self.under_tokens, self.first_late):
            sp.dma_start(self.W[:, e, :], self.w_dram[NSH0 + e]).then_inc(self.w_loaded, 16)
        sp.wait_ge(self.scattered, 16 * 2 * B)
        for e in range(self.under_tokens):
            sp.dma_start(self.W[:, e, :], self.w_dram[NSH0 + e]).then_inc(self.w_loaded, 16)
        sp.wait_ge(self.w_loaded, 16 * self.first_late)


def feed_forward(nc, tag, X, halves, whi, wlo, tanh_col, comb_dram, plain, extra=None):
    nblocks = len(whi)
    U = nblocks * HT
    UR = U - HT
    with ExitStack() as ctx:
        sb = lambda n, s, d=F32: ctx.enter_context(nc.sbuf_tensor(tag + n, s, d))
        sem = lambda n: ctx.enter_context(nc.semaphore(tag + n))
        pb = lambda n: ctx.enter_context(nc.psum_tensor(tag + n, [128, 512], F32))
        xhi, xlo = halves
        act_g = [plain[:, p * 512:(p + 1) * 512] for p in range(2)]
        hid = [plain[:, (2 + p) * 512:(3 + p) * 512] for p in range(2)]
        hhi = [sb(f"hhi{p}", [128, 512], F32R) for p in range(2)]
        hlo = [sb(f"hlo{p}", [128, 512], F32R) for p in range(2)]
        if comb_dram is not None:
            cb = [plain[:, 2048 * (1 + p):2048 * (2 + p)].rearrange("p (h t) -> p h t", h=HT) for p in range(2)]
        gate = [pb(f"gate{p}") for p in range(2)]
        up = [pb(f"up{p}") for p in range(2)]
        y = [[pb(f"y{p}{j}") for j in range(2)] for p in range(2)]
        gu_ready, gu_free, silu_ready = sem("gu_ready"), sem("gu_free"), sem("silu_ready")
        hid_ready, hhi_ready, hlo_ready = sem("hid_ready"), sem("hhi_ready"), sem("hlo_ready")
        h_used, y_free = sem("h_used"), sem("y_free")
        if comb_dram is not None:
            cb_loaded, cb_used = [sem(f"cb_loaded{p}") for p in range(2)], [sem(f"cb_used{p}") for p in range(2)]
        block = ctx.enter_context(nc.Block())
        gate_cols = lambda k, ht: slice(k * HID + ht * 128, k * HID + (ht + 1) * 128)
        up_cols = lambda k, ht: slice((KT + k) * HID + ht * 128, (KT + k) * HID + (ht + 1) * 128)
        down_cols = lambda ht: slice(2 * KT * HID + ht * D, 2 * KT * HID + (ht + 1) * D)

        def over_pairs(eng, body):
            with eng.Fori(0, NCH // 2) as i:
                body(i * 2)

        if comb_dram is not None or extra is not None:
            @block.sync
            def _(sp):
                if comb_dram is not None:
                    with sp.Fori(0, NCH) as c:
                        for b in range(1, nblocks):
                            slot = b - 1
                            sp.wait_ge(cb_used[slot], c + 1)
                            for h in range(EPB // HT):
                                rows = comb_dram.rearrange("(b ht two) t -> b ht two t", b=nblocks - 1, two=2)[
                                    slot:slot + 1, :, h, ds(c * 512, 512)]
                                sp.dma_start(cb[slot][64 * h:64 * h + 64], rows.broadcast_to([64, HT, 512])
                                             ).then_inc(cb_loaded[slot], 16)
                if extra is not None:
                    extra.sync(sp)

        if extra is not None:
            @block.gpsimd
            def _(pool):
                extra.pool(pool)

        @block.tensor
        def _(pe):
            pe.sem_inc(h_used, 2)

            def gate_up(c, n):
                b, ht, q = n // HT, n % HT, n % 2
                pe.wait_ge(gu_free, c * U + n + 1)
                for out, cols in ((gate, gate_cols), (up, up_cols)):
                    passes = [(w, x, k) for k in range(KT) for w, x in ((whi, xhi), (whi, xlo), (wlo, xhi))]
                    for m, (w, x, k) in enumerate(passes):
                        last = pe.matmul(out[q][:], w[b][:, cols(k, ht)], x[:, k, ds(c * 512, 512)],
                                         start=(m == 0), stop=(m == len(passes) - 1))
                last.then_inc(gu_ready, 1)

            def down(c, par, n):
                b, ht, q = n // HT, n % HT, n % 2
                if n == 0:
                    pe.wait_ge(y_free, c + 1)
                for part, h, ready in ((0, hhi, hhi_ready), (1, hlo, hlo_ready)):
                    pe.wait_ge(ready, c * U + n + 1)
                    for j in range(CH):
                        for w in ((whi, wlo) if part == 0 else (whi,)):
                            first = n == 0 and part == 0 and w is whi and j % 2 == 0
                            last = pe.matmul(y[par][j // 2][:, (j % 2) * D:(j % 2 + 1) * D],
                                             h[q][:, j * 128:(j + 1) * 128], w[b][:, down_cols(ht)],
                                             start=first, stop=(n == U - 1 and part == 1), skip_group_check=True)
                last.then_inc(h_used, 1)

            def pair(c):
                units = [(par, n) for par in range(2) for n in range(U)]
                gate_up(c, 0)
                for (par, n), (last_par, last_n) in zip(units[1:], units):
                    gate_up(c + par, n)
                    down(c + last_par, last_par, last_n)
                down(c + 1, 1, U - 1)
            over_pairs(pe, pair)

        @block.scalar
        def _(act):
            def pair(c):
                for par in range(2):
                    for n in range(U):
                        q = n % 2
                        u = (c + par) * U + n
                        act.wait_ge(gu_ready, u + 1)
                        act.activation(act_g[q], gate[q][:], ACT.Silu).then_inc(silu_ready, 1)
                        act.wait_ge(hid_ready, u + 1)
                        act.wait_ge(h_used, u + 1)
                        act.copy(hhi[q][:], hid[q]).then_inc(hhi_ready, 1)
            over_pairs(act, pair)

        @block.vector
        def _(dve):
            dve.sem_inc(gu_free, 2)
            dve.sem_inc(y_free, 2)
            if comb_dram is not None:
                for p in range(2):
                    dve.sem_inc(cb_used[p], 1)

            def unit(c, n):
                b, ht, q = n // HT, n % HT, n % 2
                u = c * U + n
                if comb_dram is None or b == 0:
                    dve.wait_ge(silu_ready, u + 1)
                    dve.tensor_tensor(hid[q], act_g[q], up[q][:], ALU.mult).then_inc(gu_free, 1)
                else:
                    dve.wait_ge(gu_ready, u + 1)
                    if ht == 0:
                        dve.wait_ge(cb_loaded[b - 1], c * 32 + 32)
                    last = dve.tensor_tensor(hid[q], up[q][:], cb[b - 1][:, ht], ALU.mult)
                    if ht == HT - 1:
                        last.then_inc(cb_used[b - 1], 1)
                    dve.drain()
                    dve.wait_ge(silu_ready, u + 1)
                    dve.tensor_tensor(hid[q], hid[q], act_g[q], ALU.mult).then_inc(gu_free, 1)
                dve.drain().then_inc(hid_ready, 1)
                dve.wait_ge(hhi_ready, u + 1)
                dve.tensor_tensor(hlo[q][:], hid[q], hhi[q][:].bitcast(F32), ALU.subtract).then_inc(hlo_ready, 1)

            def finish(c, par):
                dve.wait_ge(h_used, (c + 1) * U + 2)
                for j in range(CH):
                    xs = X[:, ds(c * CH + j, 1), :].rearrange("p o d -> p (o d)")
                    last = dve.scalar_tensor_tensor(xs, y[par][j // 2][:, (j % 2) * D:(j % 2 + 1) * D], tanh_col, xs,
                                                    ALU.mult, ALU.add)
                last.then_inc(y_free, 1)

            def pair(c):
                for n in range(U):
                    unit(c, n)
                for n in range(U):
                    unit(c + 1, n)
                    if n == 1:
                        finish(c, 0)
                finish(c + 1, 1)
            over_pairs(dve, pair)


def program(nc, x, ctx_in, ctxT, mask, consts, token_homes, slot_homes, g_xattn, g_ffn, wg, bg_i, bg_f, ln_scale, rw0, eb0, w0,
            wqkv, bqk, bv, rw1, eb1, w1, out):
    m_dram = nc.dram_tensor("m_rows", (128, 128), F32, kind="Internal").ap()
    xg_dram = nc.dram_tensor("slot_tokens", (NT * 128, D + 1), F32, kind="Internal").ap()
    y_dram = nc.dram_tensor("outputs", (2 * T + NT * 128, D), F32, kind="Internal").ap()
    comb_dram = nc.dram_tensor("comb_rows", (E1, T), F32, kind="Internal").ap()
    with ExitStack() as ctx:
        sb = lambda n, s, d=F32: ctx.enter_context(nc.sbuf_tensor(n, s, d))
        X = sb("X", [128, B, D])
        cst = sb("cst", [128, C_END])
        g_in = sb("g_in", [128, 4])
        g_tanh = sb("g_tanh", [128, 4])
        lns = sb("lns", [128, D])
        ln_tanh = sb("ln_tanh", [128, D])
        home = sb("home", [128, 2, B], I32)

        flat = lambda a: a.rearrange("p k e -> p (k e)")

        slots_blank = ctx.enter_context(nc.semaphore("p_slots_blank"))
        home_loaded = ctx.enter_context(nc.semaphore("p_home_loaded"))
        ctx0 = ctx.enter_context(ExitStack())
        sb0 = lambda n, s, d=F32: ctx0.enter_context(nc.sbuf_tensor(n, s, d))
        XNT, AT, ET = sb0("XNT0", [128, KT, T]), sb0("AT", [128, 128]), sb0("ET", [128, 128])
        ctxT_all, wg_sb, bg_sb = sb0("ctxT_all", [128, KT, T]), sb0("wg_sb", [128, 3 * KT, 16]), sb0("bg_sb", [128, 16])
        blank, slot_home = sb0("blank", [128, NT, D + 1]), sb0("slot_home", [128, NT], I32)
        blank_ready = ctx0.enter_context(nc.semaphore("p_blank_ready"))
        gates_loaded = ctx0.enter_context(nc.semaphore("p_gates_loaded"))
        with nc.semaphore("p_loaded") as loaded, nc.Block() as block:
            @block.gpsimd
            def _(pool):
                pool.memset(blank[:], 0.0)
                pool.wait_ge(home_loaded, 16)
                pool.drain()
                pool.tensor_copy(blank[:, :, D:D + 1].bitcast(I32), slot_home[:].rearrange("p (i o) -> p i o", o=1)
                                 ).then_inc(blank_ready, 1)

            @block.sync
            def _(sp):
                sp.dma_start(X[:], x.rearrange("b p d -> p b d")).then_inc(loaded, 16)
                sp.dma_start(cst[:], consts).then_inc(loaded, 16)
                row = lambda a, n: a.rearrange("(o n) -> o n", o=1).broadcast_to([128, n])
                sp.dma_start(g_in[:, 0:2], row(g_xattn, 2)).then_inc(loaded, 16)
                sp.dma_start(g_in[:, 2:4], row(g_ffn, 2)).then_inc(loaded, 16)
                sp.dma_start(lns[:], row(ln_scale, D)).then_inc(loaded, 16)
                sp.dma_start(wg_sb[:], wg).then_inc(gates_loaded, 16)
                sp.dma_start(bg_sb[:, 0:8], row(bg_i, 8)).then_inc(gates_loaded, 16)
                sp.dma_start(bg_sb[:, 8:16], row(bg_f, 8)).then_inc(gates_loaded, 16)
                sp.dma_start(ctxT_all[:], ctxT).then_inc(gates_loaded, 16)
                sp.dma_start(home[:], token_homes).then_inc(loaded, 16)
                sp.dma_start(slot_home[:], slot_homes).then_inc(home_loaded, 16)
                sp.wait_ge(loaded, 96)

        with nc.psum_tensor("gates", [128, 512], F32) as gate_ps:
            beside = GateProducts(ctx0, nc, gate_ps, XNT, ctxT_all, wg_sb, gates_loaded,
                                  blank, blank_ready, xg_dram, slots_blank)
            norm_transpose(nc, "n0_", X, XNT, cst, beside=beside, products=beside)
            gates(nc, gate_ps, cst, bg_sb, AT[:], ET[:], m_dram)
        cell(nc, X, XNT, ctxT, ctx_in, m_dram, cst, AT, ET, g_in, g_tanh, lns, ln_tanh, slots_blank)
        ctx0.close()

        with ExitStack() as ctx1:
            W = ctx1.enter_context(nc.sbuf_tensor("W", [128, E0, WN], F32))
            slots = ctx1.enter_context(nc.sbuf_tensor("slots", [128, 2, B], U32))
            slot_weight = ctx1.enter_context(nc.sbuf_tensor("slot_weight", [128, B, 2], F32))
            tile_expert = ctx1.enter_context(nc.sbuf_tensor("tile_expert", [1, NT], I32))
            under_tokens, first_late = 2, E0 - 1
            raw = [W[:, first_late - 1 - p, :] for p in range(2)]
            head = W[:, 0:under_tokens, :].rearrange("p e n -> p (e n)")
            XN = head[:, 0:B * (D + 1)].rearrange("p (s d) -> p s d", s=B)
            with ExitStack() as ctx2:
                half_of = lambda n, s: [ctx2.enter_context(nc.sbuf_tensor(f"{n}{h}", s, F32R)) for h in ("hi", "lo")]
                halves = half_of("x0", [128, KT, T])
                shared = [half_of(f"sw{b}", [128, WN]) for b in range(NSH0)]
                rw_raw = ctx2.enter_context(nc.sbuf_tensor("rw0_raw", [128, KT * E0], F32))
                rw = ctx2.enter_context(nc.sbuf_tensor("rw0_halves", [128, 2, KT, E0], F32R))
                split = Split(ctx2, nc, "s0", cst[:, C_ONE:C_ONE + 1])
                split.add(rw0.rearrange("p k e -> p (k e)"), rw_raw[:], flat(rw[:, 0]), flat(rw[:, 1]), 2, 1, 0)
                for b in range(NSH0):
                    split.add(w0[b], raw[b], shared[b][0][:], shared[b][1][:], b % 2, 1 + b // 2, 0)
                logits_bank = ctx2.enter_context(ExitStack())
                logits = logits_bank.enter_context(nc.psum_tensor("logits0", [128, 512], F32))
                norm_transpose(nc, "n1_", X, None, cst, XN[:, :, 0:D], halves, split.part([0, 1, 2]),
                               RouterLogits(logits, halves, rw, split.done))
                route0(nc, logits, eb0, cst, slots, slot_weight, tile_expert, g_tanh[:, 2:3])
                logits_bank.close()
                beside = BesideShared(ctx2, nc, XN, W, w0, first_late, under_tokens, xg_dram, slots, home, slots_blank)
                feed_forward(nc, "f0_", X, halves, [w[0] for w in shared], [w[1] for w in shared], g_tanh[:, 2:3],
                             None, W[:, first_late, :], extra=beside)
            routed_tiles(nc, W, w0, first_late, xg_dram, y_dram, tile_expert, cst)
            combine(nc, X, y_dram, slot_weight)

        with nc.sbuf_tensor("XNT1", [128, KT, T], F32) as XNT:
            norm_transpose(nc, "n2_", X, XNT, cst)
            attention(nc, X, XNT, ctxT, mask, wqkv, bqk, bv, cst, g_tanh[:, 1:2])

        with ExitStack() as ctx2:
            half_of = lambda n, s: [ctx2.enter_context(nc.sbuf_tensor(f"{n}{h}", s, F32R)) for h in ("hi", "lo")]
            halves = half_of("x1", [128, KT, T])
            blocks = [half_of(f"ew{b}", [128, WN]) for b in range(NB1)]
            raw = ctx2.enter_context(nc.sbuf_tensor("raw1", [128, 2, WN], F32))
            rw_raw = ctx2.enter_context(nc.sbuf_tensor("rw1_raw", [128, KT * E1], F32))
            rw = ctx2.enter_context(nc.sbuf_tensor("rw1_halves", [128, 2, KT, E1], F32R))
            split = Split(ctx2, nc, "s1", cst[:, C_ONE:C_ONE + 1])
            split.add(rw1.rearrange("p k e -> p (k e)"), rw_raw[:], flat(rw[:, 0]), flat(rw[:, 1]), 2, 1, 0)
            for b in range(NB1):
                split.add(w1[b], raw[:, b % 2, :], blocks[b][0][:], blocks[b][1][:], b % 2, 1 + b // 2,
                          b if b >= 2 else 0)
            with nc.psum_tensor("logits1", [128, 512], F32) as logits:
                norm_transpose(nc, "n3_", X, None, cst, None, halves, split.part([0, 1, 2]),
                               RouterLogits(logits, halves, rw, split.done))
                route1(nc, logits, split.part([3]), eb1, cst, comb_dram)
            feed_forward(nc, "f1_", X, halves, [w[0] for w in blocks], [w[1] for w in blocks], g_tanh[:, 3:4],
                         comb_dram, raw[:].rearrange("p r n -> p (r n)"))

        with nc.semaphore("stored") as stored, nc.Block() as block:
            @block.sync
            def _(sp):
                sp.dma_start(out.rearrange("b p d -> p b d"), X[:]).then_inc(stored, 16)
                sp.wait_ge(stored, 16)


def constants():
    c = np.zeros((128, C_END), np.float32)
    p = np.arange(128)
    c[:, C_ID:C_ID + 128] = np.eye(128)
    c[:, C_PEN:C_PEN + 128] = np.where(p[None, :] >= p[:, None], 0.0, BIG)
    c[:, C_BD0:C_BD0 + 4] = p[:, None] // DH0 == np.arange(4)
    c[:, C_BD1:C_BD1 + 8] = p[:, None] // DH1 == np.arange(8)
    c[:, C_REV:C_REV + 16] = 16 - np.arange(16)
    c[:, C_EPS] = LN_EPS
    c[:, C_ONE] = 1.0
    c[:, C_TRI:C_TRI + 128] = p[:, None] < p[None, :]
    c[:, C_ONES:C_ONES + 128] = 1.0
    c[:, C_KEEP:C_KEEP + 128] = p[None, :] % B != 0
    c[:, C_STEP:C_STEP + B] = 128 * np.arange(B)
    c[:, C_TILE:C_TILE + NT] = np.arange(NT)
    c[:, C_LNR] = math.log(ROOT0)
    return c


def kernel(**inputs):
    import numpy as _np
    import concourse.bacc as _bacc
    from concourse import mybir as _mybir
    from concourse.bass_utils import run_bass_kernel_spmd as _run

    a = {k: _np.asarray(v) for k, v in inputs.items()}

    def rows(m):
        return m.reshape(-1, 128, m.shape[-1]).transpose(1, 0, 2)

    def ffn_block(gate, up, down):
        return _np.concatenate([rows(m).reshape(128, -1) for m in (gate, up, down)], axis=1)

    ctx_in = a["ctx_1024"]
    gate_w = _np.concatenate([a["L0_xattn_igate_w"], a["L0_xattn_fgate_w"]], axis=0)
    w0 = [ffn_block(a["L0_ffn_sw1"][i].T, a["L0_ffn_sw3"][i].T, a["L0_ffn_sw2"][i].T) for i in range(NSH0)]
    w0 += [ffn_block(a["L0_ffn_w1"][i].T, a["L0_ffn_w3"][i].T, a["L0_ffn_w2"][i].T) for i in range(E0)]
    w1 = [ffn_block(a["L1_ffn_shared_gate_w"].T, a["L1_ffn_shared_up_w"].T, a["L1_ffn_shared_down_w"].T)]
    for b in range(NB1 - 1):
        e = slice(b * EPB, (b + 1) * EPB)
        w1.append(ffn_block(a["L1_ffn_gate_w"][e].transpose(1, 0, 2).reshape(D, HID),
                            a["L1_ffn_up_w"][e].transpose(1, 0, 2).reshape(D, HID),
                            a["L1_ffn_down_w"][e].reshape(HID, D)))
    wqkv = _np.stack([rows(a["L1_xattn_" + n].T) for n in ("Wq", "Wk", "Wv")])
    bqk = _np.stack([a["L1_xattn_" + n].reshape(KT, 128).T for n in ("bq", "bk")], axis=1)
    feeds = [
        ("x", a["x"]), ("ctx_in", ctx_in), ("ctxT", rows(ctx_in.reshape(T, D).T)), ("mask", a["mask_BxSxS2_ff1"]),
        ("consts", constants()),
        ("token_homes", _np.arange(2 * T, dtype=_np.int32).reshape(2, B, 128).transpose(2, 0, 1)),
        ("slot_homes", (2 * T + _np.arange(NT * 128, dtype=_np.int32)).reshape(NT, 128).T),
        ("g_xattn", a["g_xattn"]), ("g_ffn", a["g_ffn"]), ("wg", rows(gate_w.T)),
        ("bg_i", a["L0_xattn_igate_b"]), ("bg_f", a["L0_xattn_fgate_b"]), ("ln_scale", a["L0_xattn_ln_scale"]),
        ("rw0", rows(a["L0_ffn_router_w"].T)), ("eb0", a["L0_ffn_expert_bias"]), ("w0", _np.stack(w0)),
        ("wqkv", wqkv), ("bqk", bqk), ("bv", a["L1_xattn_bv"]),
        ("rw1", rows(a["L1_ffn_router_w"].T)), ("eb1", a["L1_ffn_correction_bias"]), ("w1", _np.stack(w1)),
    ]
    nc = _bacc.Bacc("TRN2", target_bir_lowering=False, num_devices=1)
    arrays, args = {}, []
    for name, v in feeds:
        v = _np.ascontiguousarray(v)
        arrays[f"in_{name}_dram"] = v
        args.append(nc.dram_tensor(f"in_{name}_dram", v.shape, _mybir.dt.from_np(v.dtype), kind="ExternalInput").ap())
    args.append(nc.dram_tensor("out_0_dram", (B, S, D), _mybir.dt.float32, kind="ExternalOutput").ap())
    program(nc, *args)
    r = _run(nc, [arrays], core_ids=[0])
    return r.results[0]["out_0_dram"]
```
